# Optimizing a Trainium2 kernel written in Bass

```python
import numpy as np
import jax
import jax.numpy as jnp

def _softmax(x, axis=-1):
    return jax.nn.softmax(x, axis=axis)

def _gelu(x):
    return jax.nn.gelu(x, approximate=True)

def _silu(x):
    return jax.nn.silu(x)

def _sigmoid(x):
    return jax.nn.sigmoid(x)

def _layernorm(x, axis=-1, eps=1e-05):
    m = jnp.mean(x, axis=axis, keepdims=True)
    v = jnp.var(x, axis=axis, keepdims=True)
    return (x - m) / jnp.sqrt(v + eps)

def _scatter_add(tgt, idx, src, axis=0):
    return tgt.at[idx].add(src)

def _segment_sum(src, seg, n):
    return jax.ops.segment_sum(src, seg, n)
kernel_name = 'mk_xattn_ffn_d2_seqx_r4_0da4d4'

def setup_inputs(seed: int=0):
    np.random.seed(seed)
    _w = jnp.asarray

    def _rec_inputs():
        import jax
        import jax.numpy as jnp
        _rk = jax.random.key(seed)
        x = -0.0002928 + 1 * jax.random.normal(jax.random.fold_in(_rk, 1), (16, 112, 256), jnp.float32)
        _lenS = 112 - jax.random.randint(jax.random.fold_in(_rk, 7), (16,), 0, max(1, 112 // 4) + 1, jnp.int32)
        _lenS2 = 375 - jax.random.randint(jax.random.fold_in(_rk, 8), (16,), 0, max(1, 375 // 4) + 1, jnp.int32)
        _ctx_1024P = jax.random.normal(jax.random.fold_in(_rk, 11), (16, 16, 256), jnp.float32)
        _ctx_1024c = jax.random.dirichlet(jax.random.fold_in(_rk, 511), 0.3 * jnp.ones((16,), jnp.float32), (16, 375))
        _ctx_1024t = jnp.einsum('bsk,bkd->bsd', _ctx_1024c, _ctx_1024P)
        _ctx_1024t = _ctx_1024t * jax.lax.rsqrt(jnp.mean(jnp.square(_ctx_1024t)) + 1e-12) * 0.953939
        ctx_1024 = 1.43633e-05 + 1.0001 * (_ctx_1024t + 0.3 * jax.random.normal(jax.random.fold_in(_rk, 611), (16, 375, 256), jnp.float32))
        return (x, ctx_1024)
    x, ctx_1024 = _rec_inputs()

    def _L0_xattn_setup():
        import jax, jax.numpy as jnp
        import numpy as np
        D, H = (256, 16)
        DH = D // H

        def _split_heads(z):
            b, t, _ = z.shape
            return z.reshape(b, t, H, DH).transpose(0, 2, 1, 3)
        key = jax.random.key(seed)
        ks = jax.random.split(key, 11)
        b, t, ta = (2, 512, 375)
        s = 1.0 / np.sqrt(D)
        return {'x': jax.random.normal(ks[0], (b, t, D), dtype=jnp.float32), 'xa': jax.random.normal(ks[1], (b, ta, D), dtype=jnp.float32), 'Wqkv': jax.random.normal(ks[2], (D, 3 * D), dtype=jnp.float32) * s, 'bqkv': jax.random.normal(ks[3], (3 * D,), dtype=jnp.float32) * 0.01, 'Wqkv_aux': jax.random.normal(ks[4], (D, 3 * D), dtype=jnp.float32) * s, 'bqkv_aux': jax.random.normal(ks[5], (3 * D,), dtype=jnp.float32) * 0.01, 'Wo': jax.random.normal(ks[6], (D, D), dtype=jnp.float32) * s, 'bo': jax.random.normal(ks[7], (D,), dtype=jnp.float32) * 0.01, 'g': jnp.zeros((H,), dtype=jnp.float32)}
    _L0_xattn_all = _L0_xattn_setup()
    _L0_xattn_in = {k: v for k, v in _L0_xattn_all.items() if k in ('Wqkv', 'bqkv', 'Wqkv_aux', 'bqkv_aux', 'Wo', 'bo', 'g')}
    del _L0_xattn_all

    def _L0_ffn_setup():
        import jax, jax.numpy as jnp
        import numpy as np
        B, S, D, F, E = (2, 256, 256, 512, 8)
        key = jax.random.key(seed)
        ks = jax.random.split(key, 6)
        scale = 0.02
        return {'x': jax.random.normal(ks[0], (B, S, D), dtype=jnp.float32), 'W1': jax.random.normal(ks[1], (E, D, F), dtype=jnp.float32) * scale, 'b1': jnp.zeros((E, F), dtype=jnp.float32), 'W2': jax.random.normal(ks[2], (E, F, D), dtype=jnp.float32) * scale, 'b2': jnp.zeros((E, D), dtype=jnp.float32), 'Wr': jax.random.normal(ks[3], (D, E), dtype=jnp.float32) * scale, 'br': jnp.zeros((E,), dtype=jnp.float32)}
    _L0_ffn_all = _L0_ffn_setup()
    _L0_ffn_in = {k: v for k, v in _L0_ffn_all.items() if k in ('W1', 'b1', 'W2', 'b2', 'Wr', 'br')}
    del _L0_ffn_all

    def _L1_xattn_setup():
        import jax, jax.numpy as jnp
        import numpy as np
        D_MODEL = 256
        B, S = (4, 512)
        key = jax.random.key(seed)
        ks = jax.random.split(key, 10)
        s = 1.0 / np.sqrt(D_MODEL)
        return {'k': jax.random.normal(ks[0], (B, S, D_MODEL), jnp.float32), 'v': jax.random.normal(ks[1], (B, S, D_MODEL), jnp.float32), 'q': jax.random.normal(ks[2], (B, S, D_MODEL), jnp.float32), 'Wk': jax.random.normal(ks[3], (D_MODEL, D_MODEL), jnp.float32) * s, 'Wv': jax.random.normal(ks[4], (D_MODEL, D_MODEL), jnp.float32) * s, 'bv': jnp.zeros((D_MODEL,), jnp.float32), 'Wq': jax.random.normal(ks[5], (D_MODEL, D_MODEL), jnp.float32) * s, 'bq': jnp.zeros((D_MODEL,), jnp.float32), 'Wo': jax.random.normal(ks[6], (D_MODEL, D_MODEL), jnp.float32) * s, 'bo': jnp.zeros((D_MODEL,), jnp.float32)}
    _L1_xattn_all = _L1_xattn_setup()
    _L1_xattn_in = {k: v for k, v in _L1_xattn_all.items() if k in ('Wk', 'Wv', 'bv', 'Wq', 'bq', 'Wo', 'bo')}
    del _L1_xattn_all

    def _L1_ffn_setup():
        import jax, jax.numpy as jnp
        import numpy as np
        key = jax.random.key(seed)
        k1, k2, k3, k4 = jax.random.split(key, 4)
        B, T, M = (4, 512, 256)
        E, F = (16, 1024)
        x = jax.random.normal(k1, (B, T, M), dtype=jnp.float32) * 0.02
        Wg = jax.random.normal(k2, (M, E), dtype=jnp.float32) * 0.02
        w1 = jax.random.normal(k3, (E, M, F), dtype=jnp.float32) * 0.02
        w2 = jax.random.normal(k4, (E, F, M), dtype=jnp.float32) * 0.02
        return {'x': x, 'Wg': Wg, 'w1': w1, 'w2': w2}
    _L1_ffn_all = _L1_ffn_setup()
    _L1_ffn_in = {k: v for k, v in _L1_ffn_all.items() if k in ('Wg', 'w1', 'w2')}
    del _L1_ffn_all
    return {'x': x, 'ctx_1024': ctx_1024, 'L0_xattn_Wqkv': _L0_xattn_in['Wqkv'], 'L0_xattn_bqkv': _L0_xattn_in['bqkv'], 'L0_xattn_Wqkv_aux': _L0_xattn_in['Wqkv_aux'], 'L0_xattn_bqkv_aux': _L0_xattn_in['bqkv_aux'], 'L0_xattn_Wo': _L0_xattn_in['Wo'], 'L0_xattn_bo': _L0_xattn_in['bo'], 'L0_xattn_g': _L0_xattn_in['g'], 'L0_ffn_W1': _L0_ffn_in['W1'], 'L0_ffn_b1': _L0_ffn_in['b1'], 'L0_ffn_W2': _L0_ffn_in['W2'], 'L0_ffn_b2': _L0_ffn_in['b2'], 'L0_ffn_Wr': _L0_ffn_in['Wr'], 'L0_ffn_br': _L0_ffn_in['br'], 'L1_xattn_Wk': _L1_xattn_in['Wk'], 'L1_xattn_Wv': _L1_xattn_in['Wv'], 'L1_xattn_bv': _L1_xattn_in['bv'], 'L1_xattn_Wq': _L1_xattn_in['Wq'], 'L1_xattn_bq': _L1_xattn_in['bq'], 'L1_xattn_Wo': _L1_xattn_in['Wo'], 'L1_xattn_bo': _L1_xattn_in['bo'], 'L1_ffn_Wg': _L1_ffn_in['Wg'], 'L1_ffn_w1': _L1_ffn_in['w1'], 'L1_ffn_w2': _L1_ffn_in['w2']}

def reference(x, ctx_1024, L0_xattn_Wqkv, L0_xattn_bqkv, L0_xattn_Wqkv_aux, L0_xattn_bqkv_aux, L0_xattn_Wo, L0_xattn_bo, L0_xattn_g, L0_ffn_W1, L0_ffn_b1, L0_ffn_W2, L0_ffn_b2, L0_ffn_Wr, L0_ffn_br, L1_xattn_Wk, L1_xattn_Wv, L1_xattn_bv, L1_xattn_Wq, L1_xattn_bq, L1_xattn_Wo, L1_xattn_bo, L1_ffn_Wg, L1_ffn_w1, L1_ffn_w2):
    import jax
    import jax.numpy as jnp

    def _L0_xattn_ref(x, xa, Wqkv, bqkv, Wqkv_aux, bqkv_aux, Wo, bo, g):
        import jax, jax.numpy as jnp
        import numpy as np
        D, H = (256, 16)
        DH = D // H

        def _split_heads(z):
            b, t, _ = z.shape
            return z.reshape(b, t, H, DH).transpose(0, 2, 1, 3)
        qkv = x @ Wqkv + bqkv
        qkv_a = xa @ Wqkv_aux + bqkv_aux
        q, k, v = (_split_heads(c) for c in jnp.split(qkv, 3, axis=-1))
        qa, ka, va = (_split_heads(c) for c in jnp.split(qkv_a, 3, axis=-1))
        scale = 1.0 / jnp.sqrt(jnp.float32(DH))
        dots = jnp.einsum('bhqd,bhkd->bhqk', q, k) * scale
        dots_aux = jnp.einsum('bhqd,bhkd->bhqk', q, ka) * scale
        p = jax.nn.softmax(dots, axis=-1)
        pa = jax.nn.softmax(dots_aux, axis=-1)
        h_main = jnp.einsum('bhqk,bhkd->bhqd', p, v)
        h_aux = jnp.einsum('bhqk,bhkd->bhqd', pa, va)
        gate = jax.nn.sigmoid(g).reshape(1, H, 1, 1)
        out = h_main * (1.0 - gate) + h_aux * gate
        b, _, t, _ = out.shape
        out = out.transpose(0, 2, 1, 3).reshape(b, t, H * DH)
        return out @ Wo + bo

    def _L0_ffn_ref(x, W1, b1, W2, b2, Wr, br):
        import jax, jax.numpy as jnp
        import numpy as np
        B, S, D, F, E = (2, 256, 256, 512, 8)
        router_logits = jnp.einsum('bsd,de->bse', x, Wr) + br
        expert_idx = jnp.argmax(router_logits, axis=-1)
        h = jax.nn.relu(jnp.einsum('bsd,edf->ebsf', x, W1) + b1[:, None, None, :])
        y = jnp.einsum('ebsf,efd->ebsd', h, W2) + b2[:, None, None, :]
        onehot = jax.nn.one_hot(expert_idx, E, dtype=x.dtype)
        out = jnp.einsum('ebsd,bse->bsd', y, onehot)
        return out

    def _L1_xattn_ref(k, v, q, Wk, Wv, bv, Wq, bq, Wo, bo):
        import jax, jax.numpy as jnp
        import numpy as np
        D_MODEL = 256
        B, S = (4, 512)
        kp = jnp.einsum('bsd,ed->bse', k, Wk)
        vp = jnp.einsum('bsd,ed->bse', v, Wv) + bv
        qp = jnp.einsum('bsd,ed->bse', q, Wq) + bq
        scale = 1.0 / jnp.sqrt(jnp.float32(kp.shape[-1]))
        scores = jnp.einsum('bqd,bkd->bqk', qp, kp) * scale
        probs = jax.nn.softmax(scores, axis=-1)
        ctx = jnp.einsum('bqk,bkd->bqd', probs, vp)
        return jnp.einsum('bqd,ed->bqe', ctx, Wo) + bo

    def _L1_ffn_ref(x, Wg, w1, w2):
        import jax, jax.numpy as jnp
        import numpy as np
        d = x.shape[-1]
        xr = x.reshape(-1, d)
        S = xr.shape[0]
        E = Wg.shape[1]
        C = (S + E - 1) // E
        gate = jax.nn.softmax(xr @ Wg, axis=-1)
        idx = jnp.argmax(gate, axis=1)
        gates_s = jnp.take_along_axis(gate, idx[:, None], axis=1)[:, 0]
        onehot = jax.nn.one_hot(idx, E, dtype=jnp.int32)
        loc = jnp.sum((jnp.cumsum(onehot, axis=0) - 1) * onehot, axis=1)
        valid = loc < C
        loc_pad = jnp.minimum(loc, C)
        dispatched = jnp.zeros((E, C + 1, d), dtype=x.dtype).at[idx, loc_pad].set(xr)
        dispatched = dispatched[:, :C]
        h = jax.nn.relu(jnp.einsum('ecm,emf->ecf', dispatched, w1))
        expert_out = jnp.einsum('ecf,efm->ecm', h, w2)
        gathered = expert_out[idx, jnp.minimum(loc, C - 1)]
        combined = gathered * (gates_s * valid.astype(x.dtype))[:, None]
        return combined.reshape(x.shape)
    x = x + _L0_xattn_ref(_layernorm(x, axis=-1), ctx_1024, L0_xattn_Wqkv, L0_xattn_bqkv, L0_xattn_Wqkv_aux, L0_xattn_bqkv_aux, L0_xattn_Wo, L0_xattn_bo, L0_xattn_g)
    x = x + _L0_ffn_ref(_layernorm(x, axis=-1), L0_ffn_W1, L0_ffn_b1, L0_ffn_W2, L0_ffn_b2, L0_ffn_Wr, L0_ffn_br)
    x = x + _L1_xattn_ref(ctx_1024, ctx_1024, _layernorm(x, axis=-1), L1_xattn_Wk, L1_xattn_Wv, L1_xattn_bv, L1_xattn_Wq, L1_xattn_bq, L1_xattn_Wo, L1_xattn_bo)
    x = x + _L1_ffn_ref(_layernorm(x, axis=-1), L1_ffn_Wg, L1_ffn_w1, L1_ffn_w2)
    return x

_drawn_inputs = setup_inputs


def setup_inputs(seed=0):
    import zlib

    import numpy as np

    out = dict(_drawn_inputs(seed))
    spreads = {'L0_xattn_g': (0.0, 0.355),
     'L0_ffn_b1': (0.0, 0.298),
     'L0_ffn_b2': (0.0, 0.1),
     'L0_ffn_br': (0.0, 0.1),
     'L1_xattn_bv': (0.0, 0.1),
     'L1_xattn_bq': (0.0, 0.441),
     'L1_xattn_bo': (0.0, 0.1)}
    factors = {'L0_xattn_bqkv': 7.708,
     'L0_xattn_bqkv_aux': 6.291,
     'L0_xattn_bo': 3.888,
     'L1_ffn_Wg': 4.809,
     'L1_ffn_w1': 5.647,
     'L1_ffn_w2': 4.684}
    for name, (base, spread) in spreads.items():
        noise = np.random.default_rng([zlib.crc32(name.encode()), seed]).standard_normal(out[name].shape)
        drawn = base * np.exp(spread * noise) if base else spread * noise
        out[name] = jnp.asarray(drawn.astype(out[name].dtype))
    for name, factor in factors.items():
        out[name] = (out[name] * factor).astype(out[name].dtype)
    return out
```

```python
from contextlib import ExitStack

import concourse.bass as bass
from concourse import mybir

F32 = mybir.dt.float32
BF16 = mybir.dt.bfloat16
I32 = mybir.dt.int32
ALU = mybir.AluOpType
ACT = mybir.ActivationFunctionType
AX = mybir.AxisListType.X

B, T, D = 16, 112, 256
S = 375
H, DH = 16, 16
KC, NC = 125, 3
KV = S + T
EPS = 1e-5
TERMS_Q = (0, 0, 1, 0, 2, 1)
TERMS_K = (0, 1, 0, 2, 0, 1)
NT = len(TERMS_Q)
QK = NT * DH
ROWS = QK + 6
HG = 4
P = 128
E0, F0 = 8, 512
ROW_TILES = B * T // P
TILES = ROW_TILES + E0 - 1
E1, F1 = 16, 1024
C1 = (B * T) // E1
FAR = 1024.0


class Item:

    def __init__(self, i, c, n, unroll=2):
        self.i, self.c, self.n, self.unroll = i, c, n, unroll
        self.parity = c % 2
        self.quarter = c % 4

    def __sub__(self, k):
        return Item(self.i, self.c - k, self.n, self.unroll)

    def __add__(self, k):
        return Item(self.i, self.c + k, self.n, self.unroll)

    def number(self, per=1):
        return per * self.c if isinstance(self.i, int) else self.i * (self.unroll * per) + per * self.c

    def count(self, per=1, plus=0):
        const = per * self.c + plus
        assert const > (0 if self.looped() else -1)
        return const if isinstance(self.i, int) else self.i * (self.unroll * per) + const

    def looped(self):
        return not isinstance(self.i, int)

    def turn(self, per=16, plus=0, of=2):
        const = per * (self.c // of) + plus
        assert const > (0 if self.looped() else -1)
        return const if isinstance(self.i, int) else self.i * (self.unroll // of * per) + const

    def at(self):
        return bass.ds(self.number(), 1)

    def rows(self, size):
        return bass.ds(self.number(size), size)

    def real(self):
        return self.looped() or 0 <= self.c < self.n


def steps(engine, step, n, first, last, end, unroll=2):
    loops = (last - first + 1) // unroll
    for c in range(first):
        step(Item(0, c, n))
    with engine.Fori(0, loops) as i:
        for c in range(unroll):
            step(Item(i, first + c, n, unroll))
    for c in range(first + loops * unroll, end):
        step(Item(0, c, n))


def attention_steps(engine, step):
    steps(engine, step, B, 5, B - 2, B + 3)


class Shared:
    pass


def program(nc, a, out):
    with ExitStack() as ctx:
        g = Shared()
        g.nc = nc

        def sb(name, shape, dt=F32, where=ctx):
            return where.enter_context(nc.sbuf_tensor(name, shape, dt))

        def sem(name):
            handle = nc.alloc_semaphore(name=name)
            if g.phase_sems is not None:
                g.phase_sems.append(handle)
            return handle

        g.phase_sems = None

        def phase(run, *args):
            g.phase_sems = []
            run(*args)
            nc.all_engine_barrier()
            nc.clear_and_free_semaphores(g.phase_sems)
            nc.all_engine_barrier()
            g.phase_sems = None

        def dram(name, shape, dt=F32):
            return nc.dram_tensor(name, shape, dt, kind="Internal").ap()

        g.sb, g.sem, g.dram = sb, sem, dram
        g.bank = [ctx.enter_context(nc.psum_tensor(f"bank{k}", [P, 512], F32)) for k in range(8)]
        g.xs = sb("xs", [T, B, D])
        g.ident = sb("ident", [P, P])
        g.ident16 = sb("ident16", [P, P], BF16)
        g.neg_half = sb("neg_half", [P, 1])
        g.eps = sb("eps", [P, 1])
        g.ct_dram = dram("ct_dram", (B, P, 2, S))
        g.sorted0 = dram("sorted0", (TILES * P, D))
        g.made0 = dram("made0", (TILES * P, D))
        g.sorted1 = dram("sorted1", (2 * E1 * C1, D))
        g.made1 = dram("made1", (E1 * C1, D))
        g.s_w0 = sem("experts0_loaded")
        g.s_zero = sem("sorted_cleared")
        with ExitStack() as layer0:
            g.w1 = sb("w1", [P, E0, 2, F0], F32, layer0)
            g.w2 = sb("w2", [P, E0, F0 // P, D], F32, layer0)
            g.b1 = sb("b1", [P, E0, F0 // P], F32, layer0)
            phase(attention0, nc, a, g)
            phase(ffn0, nc, a, g)
        with ExitStack() as layer1:
            g.ring1 = [sb(f"ring1_{k}", [P, 2, F1], F32, layer1) for k in range(4)]
            g.ring2 = [sb(f"ring2_{k}", [P, F1 // P, D], F32, layer1) for k in range(4)]
            g.s_ring1 = [sem(f"w1_loaded{k}") for k in range(4)]
            g.s_ring2 = [sem(f"w2_loaded{k}") for k in range(4)]
            g.rows1_buffer = sb("rows1", [T, B, D], F32, layer1)
            phase(attention1, nc, a, g)
            phase(ffn1, nc, a, out, g)


def attention0(nc, a, g_):
    sem, dram, bank, xs, ident, ident16 = g_.sem, g_.dram, g_.bank, g_.xs, g_.ident, g_.ident16
    neg_half, eps = g_.neg_half, g_.eps
    with ExitStack() as phase:
        def sb(name, shape, dt=F32):
            return g_.sb(name, shape, dt, phase)

        w_x = sb("w_x", [P, 2, 3 * D])
        w_aux = sb("w_aux", [P, 2, 2 * D])
        wo = sb("wo", [P, HG, D])
        bias_t = sb("bias_t", [P, 6])
        gate = sb("gate", [P, HG, 2])
        bv = sb("bv", [P, HG, 2])
        bv_mix = sb("bv_mix", [P, HG])
        bv_wide = sb("bv_wide", [P, HG, T])
        bo_wide = sb("bo_wide", [T, D])
        clear = sb("clear", [P, D])
        c_wide = sb("c_wide", [T, D])
        ctx_in = [sb(f"ctx_in{p}", [KC, NC, D]) for p in range(2)]
        ln_stats = sb("ln_stats", [T, 6])
        ln_mv = sb("ln_mv", [T, 2])
        ln_rstd = sb("ln_rstd", [T, 2])
        xn = [sb(f"xn{p}", [T, D]) for p in range(2)]
        xt = [sb(f"xt{p}", [P, 2, T]) for p in range(2)]
        ct = [sb(f"ct{p}", [P, 2, S]) for p in range(2)]
        parts = [sb(f"parts{p}", [P, 3, 2, KV + T], BF16) for p in range(2)]
        rest = sb("rest", [P, 2, KV + T])
        k_stack = [sb(f"k_stack{p}", [ROWS, H, KV], BF16) for p in range(2)]
        q_stack = [sb(f"q_stack{p}", [ROWS, H, T], BF16) for p in range(2)]
        v = [sb(f"v{p}", [KC, NC + 1, H, 2 * DH]) for p in range(2)]
        neg_max = sb("neg_max", [T, 2, H])
        max_rest = sb("max_rest", [T, 2, H])
        max_parts = sb("max_parts", [T, 2, 3, H], BF16)
        mt = sb("mt", [QK, T], BF16)
        probs = [sb(f"probs{k}", [KC, 4, T]) for k in range(4)]
        recip = [sb(f"recip{u}", [P, 2, 2, T]) for u in range(2)]
        heads = [sb(f"heads{u}", [P, 2, 2, T]) for u in range(2)]
        mixed = sb("mixed", [P, HG, T])

        parts_dram = [dram(f"parts_dram{p}", (6, P, KV + T), BF16) for p in range(2)]
        max_dram = [dram(f"max_dram{p}", (QK, T), BF16) for p in range(2)]

        s = {n: sem(n) for n in """consts zeroed loaded ones_ready gate_load gate_exp gate_one gate_recip gate_ready
            bv_step c_mm c_ready
            ln_stats_ready ln_mv_ready ln_eps_ready ln_rstd_ready xn_ready xc_ready
            xt_mm ct_mm xt_ready ct_ready v01_mm v23_mm v_ready qk_mm ka0_mm ka1_mm
            high_done rest_done mid_done low_done scored max_done msplit mt_mm mt_ready
            logits_mm exp_done pv_done shuffled recip_ready gated heads_ready0 heads_ready1 mixed_ready wo_mm x1_ready
            dve_turns pool_turns sp_turns done""".split()}
        s_spill = [sem(f"ct_spilled{p}") for p in range(2)]
        s_ctx = [sem(f"ctx_loaded{p}") for p in range(2)]
        s_parts = [sem(f"parts_written{p}") for p in range(2)]
        s_stack = [sem(f"stack_ready{p}") for p in range(2)]
        s_mw = [sem(f"max_written{p}") for p in range(2)]
        s_mr = [sem(f"max_ready{p}") for p in range(2)]
        heads_ready = [s["heads_ready0"], s["heads_ready1"]]
        LOADS = 8 + 6 + 1 + 8 + 4 + 1 + 1
        block = phase.enter_context(nc.Block())

        @block.sync
        def _(sp):
            sp.dma_start(xs[:, :, :], a["x"].rearrange("b t d -> t b d")).then_inc(s["loaded"], 16)
            sp.dma_start(ctx_in[0][:, :, :], a["ctx_1024"][0].rearrange("(c k) d -> k c d", k=KC)).then_inc(s_ctx[0], 16)
            sp.dma_start(w_x[:, :, :], a["L0_xattn_Wqkv"].rearrange("(a p) n -> p a n", p=P)).then_inc(s["loaded"], 16)
            sp.dma_start(w_aux[:, :, :], a["L0_xattn_Wqkv_aux"][:, D:3 * D].rearrange("(a p) n -> p a n", p=P)).then_inc(s["loaded"], 16)
            for k in range(4):
                src = a["L0_xattn_bqkv"][k * P:(k + 1) * P].rearrange("(p o) -> p o", o=1)
                sp.dma_start(bias_t[:, k:k + 1], src).then_inc(s["loaded"], 16)
            for k in range(2):
                src = a["L0_xattn_bqkv_aux"][D + k * P:D + (k + 1) * P].rearrange("(p o) -> p o", o=1)
                sp.dma_start(bias_t[:, 4 + k:5 + k], src).then_inc(s["loaded"], 16)
            bo = a["L0_xattn_bo"].rearrange("(o n) -> o n", o=1)
            sp.dma_start(bo_wide[:, :], bo.broadcast_to((T, D))).then_inc(s["loaded"], 16)
            sp.wait_ge(s["zeroed"], 4)
            for j in range(4):
                rows = slice(32 * j, 32 * j + DH)
                wsrc = a["L0_xattn_Wo"].rearrange("(g j d) n -> j d g n", g=HG, j=4)
                sp.dma_start(wo[rows, :, :], wsrc[j]).then_inc(s["loaded"], 16)
                for o, name in enumerate(("L0_xattn_bqkv", "L0_xattn_bqkv_aux")):
                    bsrc = a[name][2 * D:3 * D].rearrange("(g j d) -> j d g", g=HG, j=4)
                    sp.dma_start(bv[rows, :, o], bsrc[j], allow_slow_non_contiguous=True).then_inc(s["loaded"], 16)
                gsrc = a["L0_xattn_g"].rearrange("(o g j) -> j o g", o=1, g=HG)
                sp.dma_start(gate[32 * j:32 * j + 32, :, 0], gsrc[j].broadcast_to((32, HG)), allow_slow_non_contiguous=True).then_inc(s["gate_load"], 16)

            def load_experts():
                for e in range(E0):
                    sp.dma_start(g_.w1[:, e, :, :], a["L0_ffn_W1"][e].rearrange("(k p) f -> p k f", p=P)).then_inc(g_.s_w0, 16)
                    sp.dma_start(g_.w2[:, e, :, :], a["L0_ffn_W2"][e].rearrange("(k p) d -> p k d", p=P)).then_inc(g_.s_w0, 16)
                    for f in range(F0 // P):
                        sp.dma_start(g_.b1[:, e, f:f + 1], a["L0_ffn_b1"][e, f * P:(f + 1) * P].rearrange("(p o) -> p o", o=1)).then_inc(g_.s_w0, 16)
                for rows, n in ((g_.sorted0, TILES), (g_.sorted1, E1 * C1 // P)):
                    for k in range(n):
                        sp.dma_start(rows[k * P:(k + 1) * P, :], clear[:, :]).then_inc(g_.s_zero, 16)

            def step(b):
                if isinstance(b.i, int) and b.c == 2:
                    load_experts()
                if (b + 1).real():
                    if not isinstance(b.i, int) or b.c >= 1:
                        sp.wait_ge(s["ct_mm"], b.count())
                        sp.sem_inc(s["sp_turns"], 1)
                    src = a["ctx_1024"][(b + 1).at()].rearrange("o (c k) d -> k (o c) d", k=KC)
                    sp.dma_start(ctx_in[(b + 1).parity][:, :, :], src).then_inc(s_ctx[(b + 1).parity], 16)
                if (b - 1).real():
                    n = b - 1
                    sp.wait_ge(s_parts[n.parity], n.turn(16, 16))
                    sp.sem_inc(s["sp_turns"], 1)
                    if (b - 3).real():
                        sp.wait_ge(s["pv_done"], (b - 3).count(16, 16))
                    src = parts_dram[n.parity].rearrange("(t a) p n -> t (a p) n", a=2)
                    for t in range(NT):
                        rows = slice(DH * t, DH * t + DH)
                        k_src = src[TERMS_K[t]][:, 0:KV].rearrange("(h d) n -> d h n", d=DH)
                        q_src = src[TERMS_Q[t]][:, KV:KV + T].rearrange("(h d) n -> d h n", d=DH)
                        sp.dma_start(k_stack[n.parity][rows, :, :], k_src).then_inc(s_stack[n.parity], 16)
                        sp.dma_start(q_stack[n.parity][rows, :, :], q_src).then_inc(s_stack[n.parity], 16)
                if (b - 2).real():
                    n = b - 2
                    sp.wait_ge(s["mt_ready"], n.count(1, 1))
                    sp.dma_start(max_dram[n.parity], mt[:, :]).then_inc(s_mw[n.parity], 16)
                    sp.wait_ge(s_mw[n.parity], n.turn(16, 16))
                    sp.dma_start(q_stack[n.parity][QK:ROWS, :, :],
                                 max_dram[n.parity].rearrange("(k h) n -> k h n", h=H)).then_inc(s_mr[n.parity], 16)
                if b.real():
                    sp.wait_ge(s["ct_ready"], b.count(2, 2))
                    spill = g_.ct_dram[b.at()].rearrange("o p a n -> p (o a) n")
                    sp.sem_inc(s["sp_turns"], 1)
                    sp.dma_start(spill, ct[b.parity][:, :, :]).then_inc(s_spill[b.parity], 16)
                    sp.wait_ge(s["low_done"], b.count(2, 2))
                    sp.dma_start(parts_dram[b.parity].rearrange("g p n -> p g n"),
                                 parts[b.parity][:, :, :, :].rearrange("p t a n -> p (t a) n")).then_inc(s_parts[b.parity], 16)

            attention_steps(sp, step)
            for p in range(2):
                sp.wait_ge(s_spill[p], 16 * B // 2)
            sp.wait_ge(g_.s_w0, 16 * E0 * 6)
            sp.wait_ge(g_.s_zero, 16 * (TILES + E1 * C1 // P))

        @block.gpsimd
        def _(pool):
            pool.memset(wo[:, :, :], 0.0).then_inc(s["zeroed"], 1)
            pool.memset(bv[:, :, :], 0.0).then_inc(s["zeroed"], 1)
            pool.memset(gate[:, :, :], 0.0).then_inc(s["zeroed"], 1)
            pool.memset(ident[:, :], 0.0).then_inc(s["consts"], 1)
            pool.memset(ident16[:, :], 0.0).then_inc(s["consts"], 1)
            pool.memset(neg_half[:, :], -0.5).then_inc(s["consts"], 1)
            pool.memset(eps[:, :], EPS).then_inc(s["consts"], 1)
            pool.memset(clear[:, :], 0.0).then_inc(s["zeroed"], 1)
            for p in range(2):
                pool.memset(v[p][:, :, :, DH:2 * DH], 1.0).then_inc(s["ones_ready"], 1)
                pool.wait_ge(s["ones_ready"], p + 1)
                pool.memset(k_stack[p][QK:ROWS, :, :], 0.0).then_inc(s["consts"], 1)
                pool.wait_ge(s["consts"], 5 + p)
            for m in (ident, ident16):
                pool.affine_select(out=m[:, :], in_=m[:, :], compare_op=ALU.not_equal, fill=1.0, base=0,
                                   pattern=[[-1, P]], channel_multiplier=1).then_inc(s["consts"], 1)
            pool.wait_ge(s["consts"], 8)
            for p in range(2):
                mx = k_stack[p][QK:ROWS, :, :]
                pool.affine_select(out=mx[:, :, 0:S], in_=mx[:, :, 0:S], compare_op=ALU.is_ge, fill=1.0, base=-3,
                                   pattern=[[0, H], [0, S]], channel_multiplier=1).then_inc(s["ones_ready"], 1)
                pool.affine_select(out=mx[:, :, S:KV], in_=mx[:, :, S:KV], compare_op=ALU.is_ge, fill=1.0, base=2,
                                   pattern=[[0, H], [0, T]], channel_multiplier=-1).then_inc(s["ones_ready"], 1)

            def ln(b):
                pool.wait_ge(s["ln_mv_ready"], b.count(1, 1))
                nc.gpsimd.tensor_tensor(ln_rstd[:, 0:1], ln_mv[:, 1:2], eps[0:T, :], ALU.add).then_inc(s["ln_eps_ready"], 1)
                pool.wait_ge(s["ln_eps_ready"], b.count(1, 1))
                nc.gpsimd.tensor_tensor(ln_rstd[:, 1:2], ln_rstd[:, 0:1], neg_half[0:T, :], ALU.pow).then_inc(s["ln_rstd_ready"], 1)

            def add_c(b):
                pool.wait_ge(s["xn_ready"], b.count(1, 1))
                row = xs[:, b.at(), :].rearrange("t o d -> t (o d)")
                nc.gpsimd.tensor_tensor(row, row, c_wide[:, :], ALU.add).then_inc(s["xc_ready"], 1)

            pool.wait_ge(s["ones_ready"], 6)
            ln(Item(0, 0, B))
            pool.wait_ge(s["c_ready"], 1)
            add_c(Item(0, 0, B))

            def step(b):
                if (b - 3).real():
                    n = b - 3
                    for u in range(2):
                        pool.wait_ge(s["recip_ready"], n.count(2, u + 1))
                        g = gate[:, 2 * u:2 * u + 2, :].rearrange("p g (s o) -> p g s o", o=1).broadcast_to((P, 2, 2, T))
                        nc.gpsimd.tensor_tensor(recip[u][:, :, :, :], recip[u][:, :, :, :], g, ALU.mult).then_inc(s["gated"], 1)
                    for u in range(2):
                        pool.wait_ge(heads_ready[u], n.count(1, 1))
                        if u == 0:
                            pool.wait_ge(s["wo_mm"], n.count())
                        nc.gpsimd.tensor_tensor(mixed[:, 2 * u:2 * u + 2, :], heads[u][:, :, 0, :], heads[u][:, :, 1, :],
                                                ALU.add).then_inc(s["mixed_ready"], 1)
                if (b + 1).real():
                    ln(b + 1)
                    add_c(b + 1)
                if b.real():
                    for k, (lo, hi, need) in enumerate(((S, KV + T, 4), (0, S, 6))):
                        pool.wait_ge(s["rest_done"], b.count(6, need))
                        pool.sem_inc(s["pool_turns"], 1)
                        nc.gpsimd.tensor_copy(parts[b.parity][:, 1, :, lo:hi], rest[:, :, lo:hi]).then_inc(s["mid_done"], 1)
                        pool.wait_ge(s["mid_done"], b.count(2, k + 1))
                        nc.gpsimd.tensor_tensor(parts[b.parity][:, 2, :, lo:hi], rest[:, :, lo:hi],
                                                parts[b.parity][:, 1, :, lo:hi], ALU.subtract).then_inc(s["low_done"], 1)

            attention_steps(pool, step)

        @block.scalar
        def _(act):
            act.wait_ge(s["gate_load"], 64)
            nc.scalar.activation(gate[:, :, 1], gate[:, :, 0], ACT.Exp, scale=-1.0).then_inc(s["gate_exp"], 1)
            act.wait_ge(s["loaded"], 16 * (3 + 6 + 1))

            def step(b):
                if (b - 3).real():
                    n = b - 3
                    for k in range(16):
                        keys = T if k % 4 == 0 else KC
                        act.wait_ge(s["logits_mm"], n.count(16, k + 1))
                        act.wait_ge(s["pv_done"], n.count(16, max(k - 3, 0)))
                        src = bank[4 + k % 2][0:keys, 0:4 * T].rearrange("p (j q) -> p j q", j=4)
                        nc.scalar.activation(probs[k % 4][0:keys, :, :], src, ACT.Exp, scale=DH ** -0.5).then_inc(s["exp_done"], 1)
                if b.real():
                    act.wait_ge(s["xt_mm"], b.count(1, 1))
                    if (b - 2).real():
                        act.wait_ge(s["v23_mm"], (b - 2).count(1, 1))
                    nc.scalar.copy(xt[b.parity][:, :, :], bank[0][:, 0:2 * T].rearrange("p (a t) -> p a t", a=2)).then_inc(s["xt_ready"], 1)
                    act.wait_ge(s["ct_mm"], b.count(1, 1))
                    if (b - 2).real():
                        act.wait_ge(s_spill[b.parity], (b - 2).turn(16, 16))
                    for h in range(2):
                        nc.scalar.copy(ct[b.parity][:, h, :], bank[1 + h][:, 0:S]).then_inc(s["ct_ready"], 1)
                if (b - 2).real():
                    n = b - 2
                    act.wait_ge(s["mt_mm"], n.count(1, 1))
                    if (b - 3).real():
                        act.wait_ge(s_mw[(b - 3).parity], (b - 3).turn(16, 16))
                    nc.scalar.copy(mt[:, :], bank[3][0:QK, 256:256 + T // 2].bitcast(BF16)).then_inc(s["mt_ready"], 1)
                if (b - 1).real():
                    n = b - 1
                    if n.parity == n.c and isinstance(n.i, int):
                        act.wait_ge(s["ones_ready"], 6)
                    act.wait_ge(s["v01_mm"], n.count(1, 1))
                    nc.scalar.copy(v[n.parity][:, 0:2, :, 0:DH],
                                   bank[0][0:KC, :].rearrange("p (c h d) -> p c h d", c=2, h=H)).then_inc(s["v_ready"], 1)
                    act.wait_ge(s["v23_mm"], n.count(1, 1))
                    nc.scalar.copy(v[n.parity][:, 2, :, 0:DH],
                                   bank[1][0:KC, 0:D].rearrange("p (h d) -> p h d", h=H)).then_inc(s["v_ready"], 1)
                    nc.scalar.copy(v[n.parity][0:T, 3, :, 0:DH],
                                   bank[1][0:T, D:2 * D].rearrange("p (h d) -> p h d", h=H)).then_inc(s["v_ready"], 1)
                if b.real():
                    if (b - 2).real():
                        act.wait_ge(s_parts[b.parity], (b - 2).turn(16, 16))
                    act.wait_ge(s["qk_mm"], b.count(1, 1))
                    for h in range(2):
                        for o, col in enumerate((S, KV)):
                            nc.scalar.activation(parts[b.parity][:, 0, h, col:col + T], bank[2][:, (2 * h + o) * T:(2 * h + o + 1) * T],
                                                 ACT.Identity, bias=bias_t[:, (2, 0)[o] + h:(2, 0)[o] + h + 1]).then_inc(s["high_done"], 1)
                    for h in range(2):
                        act.wait_ge(s[f"ka{h}_mm"], b.count(1, 1))
                        nc.scalar.activation(parts[b.parity][:, 0, h, 0:S], bank[(0, 3)[h]][:, 0:S], ACT.Identity,
                                             bias=bias_t[:, 4 + h:5 + h]).then_inc(s["high_done"], 1)

            attention_steps(act, step)

        @block.vector
        def _(dve):
            dve.wait_ge(s["loaded"], 16 * (3 + 6 + 1 + 12))

            def ln(b):
                row = xs[:, b.at(), :].rearrange("t o d -> t (o d)")
                nc.vector.bn_stats(ln_stats[:, :], row).then_inc(s["ln_stats_ready"], 1)
                dve.wait_ge(s["ln_stats_ready"], b.count(1, 1))
                dve.sem_inc(s["dve_turns"], 1)
                nc.vector.bn_aggr(ln_mv[:, :], ln_stats[:, :]).then_inc(s["ln_mv_ready"], 1)
                dve.wait_ge(s["ln_rstd_ready"], b.count(1, 1))
                if (b - 2).real():
                    dve.wait_ge(s["xt_mm"], (b - 2).count(1, 1))
                nc.vector.tensor_scalar(xn[b.parity][:, :], row, ln_mv[:, 0:1], ln_rstd[:, 1:2],
                                        ALU.subtract, ALU.mult).then_inc(s["xn_ready"], 1)

            ln(Item(0, 0, B))
            dve.wait_ge(s["gate_exp"], 1)
            nc.vector.tensor_scalar(gate[:, :, 0], gate[:, :, 1], 1.0, None, ALU.add).then_inc(s["gate_one"], 1)
            dve.wait_ge(s["gate_one"], 1)
            nc.vector.reciprocal(gate[:, :, 1], gate[:, :, 0]).then_inc(s["gate_recip"], 1)
            dve.wait_ge(s["gate_recip"], 1)
            nc.vector.tensor_scalar(gate[:, :, 0], gate[:, :, 1], -1.0, 1.0, ALU.mult, ALU.add).then_inc(s["gate_ready"], 1)
            dve.wait_ge(s["gate_ready"], 1)
            nc.vector.tensor_tensor(bv[:, :, :], bv[:, :, :], gate[:, :, :], ALU.mult).then_inc(s["bv_step"], 1)
            dve.wait_ge(s["bv_step"], 1)
            nc.vector.tensor_tensor(bv_mix[:, :], bv[:, :, 0], bv[:, :, 1], ALU.add).then_inc(s["bv_step"], 1)
            dve.wait_ge(s["bv_step"], 2)
            nc.vector.tensor_copy(bv_wide[:, :, :], bv_mix[:, :].rearrange("p (g o) -> p g o", o=1).broadcast_to((P, HG, T))).then_inc(s["bv_step"], 1)
            dve.wait_ge(s["c_mm"], 1)
            nc.vector.tensor_tensor(c_wide[:, :], bank[4][0:T, 0:D], bo_wide[:, :], ALU.add).then_inc(s["c_ready"], 1)

            def half_norm(n, u):
                dve.wait_ge(s["pv_done"], n.count(16, 8 * (u + 1)))
                if (n - 1).real():
                    dve.wait_ge(heads_ready[u], n.count())
                dve.sem_inc(s["dve_turns"], 1)
                src = bank[6 + u][:, 0:4 * T]
                flat = recip[u][:, :, :, :].rearrange("p g s t -> p (g s t)")
                nc.vector.stream_shuffle(flat, src, [DH + k % DH for k in range(32)]).then_inc(s["shuffled"], 1)
                dve.wait_ge(s["shuffled"], n.count(2, u + 1))
                nc.vector.reciprocal(flat, flat).then_inc(s["recip_ready"], 1)

            def half_scale(n, u):
                dve.wait_ge(s["gated"], n.count(2, u + 1))
                if (n - 1).real():
                    dve.wait_ge(s["mixed_ready"], n.count(2))
                nc.vector.tensor_tensor(heads[u][:, :, :, :].rearrange("p g s t -> p (g s t)"), bank[6 + u][:, 0:4 * T],
                                        recip[u][:, :, :, :].rearrange("p g s t -> p (g s t)"), ALU.mult).then_inc(heads_ready[u], 1)

            def step(b):
                for k in range(8):
                    if (b - 2).real():
                        n = b - 2
                        dve.wait_ge(s["scored"], n.count(8, k + 1))
                        if k == 0 and (n - 1).real():
                            dve.wait_ge(s["msplit"], n.count(4))
                        for j in range(2):
                            src = bank[2 * (k % 2) + j]
                            h = 2 * k + j
                            nc.vector.tensor_reduce(neg_max[:, 0, h:h + 1], src[0:T, 0:S], AX, ALU.max, negate=True)
                            last = nc.vector.tensor_reduce(neg_max[:, 1, h:h + 1], src[0:T, S:KV], AX, ALU.max, negate=True)
                        last.then_inc(s["max_done"], 1)
                    if (b - 3).real():
                        if k == 4:
                            half_norm(b - 3, 0)
                        if k == 6:
                            half_scale(b - 3, 0)
                if (b - 2).real():
                    n = b - 2
                    dve.wait_ge(s["max_done"], n.count(8, 8))
                    if (n - 1).real():
                        dve.wait_ge(s["mt_mm"], n.count())
                    nc.vector.tensor_copy(max_parts[:, :, 0, :], neg_max[:, :, :]).then_inc(s["msplit"], 1)
                    dve.wait_ge(s["msplit"], n.count(4, 1))
                    nc.vector.tensor_tensor(max_rest[:, :, :], neg_max[:, :, :], max_parts[:, :, 0, :], ALU.subtract).then_inc(s["msplit"], 1)
                    dve.wait_ge(s["msplit"], n.count(4, 2))
                    nc.vector.tensor_copy(max_parts[:, :, 1, :], max_rest[:, :, :]).then_inc(s["msplit"], 1)
                    dve.wait_ge(s["msplit"], n.count(4, 3))
                    nc.vector.tensor_tensor(max_parts[:, :, 2, :], max_rest[:, :, :], max_parts[:, :, 1, :], ALU.subtract).then_inc(s["msplit"], 1)
                if (b - 3).real():
                    half_norm(b - 3, 1)
                    half_scale(b - 3, 1)
                if (b + 1).real():
                    ln(b + 1)
                if (b - 3).real():
                    n = b - 3
                    dve.wait_ge(s["wo_mm"], n.count(1, 1))
                    dve.wait_ge(s["xc_ready"], n.count(1, 1))
                    row = xs[:, n.at(), :].rearrange("t o d -> t (o d)")
                    nc.vector.tensor_tensor(row, bank[3][0:T, 0:D], row, ALU.add).then_inc(s["x1_ready"], 1)
                if b.real():
                    if (b - 1).real():
                        dve.wait_ge(s["low_done"], b.count(2))
                    dve.wait_ge(s["high_done"], b.count(6, 4))
                    for h in range(2):
                        for o, col in enumerate((S, KV)):
                            nc.vector.scalar_tensor_tensor(out=rest[:, h, col:col + T], in0=bank[2][:, (2 * h + o) * T:(2 * h + o + 1) * T],
                                                           scalar=bias_t[:, (2, 0)[o] + h:(2, 0)[o] + h + 1], in1=parts[b.parity][:, 0, h, col:col + T],
                                                           op0=ALU.add, op1=ALU.subtract).then_inc(s["rest_done"], 1)
                    for h in range(2):
                        dve.wait_ge(s["high_done"], b.count(6, 5 + h))
                        nc.vector.scalar_tensor_tensor(out=rest[:, h, 0:S], in0=bank[(0, 3)[h]][:, 0:S], scalar=bias_t[:, 4 + h:5 + h],
                                                       in1=parts[b.parity][:, 0, h, 0:S], op0=ALU.add, op1=ALU.subtract).then_inc(s["rest_done"], 1)

            attention_steps(dve, step)

        @block.tensor
        def _(pe):
            pe.wait_ge(s["loaded"], 16 * (3 + 6 + 1 + 12))
            pe.wait_ge(s["bv_step"], 3)
            for g in range(HG):
                last = nc.tensor.matmul(bank[4][0:T, 0:D], bv_wide[:, g, :], wo[:, g, :], start=(g == 0), stop=(g == HG - 1))
            last.then_inc(s["c_mm"], 1)
            pe.wait_ge(s["c_ready"], 1)
            pe.wait_ge(s["consts"], 8)
            pe.wait_ge(s["ones_ready"], 6)

            def max_scores(n, k):
                if k == 0:
                    pe.wait_ge(s_stack[n.parity], n.turn(192, 192))
                    if (n + 1).real():
                        pe.wait_ge(s["rest_done"], n.count(6, 12))
                    pe.wait_ge(s["v_ready"], n.count(3, 3))
                if k == 1 and (n - 2).real():
                    pe.wait_ge(s["x1_ready"], (n - 2).count(1, 1))
                if k >= 2:
                    pe.wait_ge(s["max_done"], n.count(8, k - 1))
                for j in range(2):
                    h = 2 * k + j
                    last = nc.tensor.matmul(bank[2 * (k % 2) + j][0:T, 0:KV], q_stack[n.parity][0:QK, h, :],
                                            k_stack[n.parity][0:QK, h, :], start=True, stop=True)
                last.then_inc(s["scored"], 1)

            def logits(n, k):
                g, c = k // 4, k % 4
                if k >= 2:
                    pe.wait_ge(s["exp_done"], n.count(16, k - 1))
                lo, keys = (S, T) if c == 0 else ((c - 1) * KC, KC)
                for j in range(4):
                    h = 4 * g + j
                    last = nc.tensor.matmul(bank[4 + k % 2][0:keys, j * T:(j + 1) * T], k_stack[n.parity][:, h, lo:lo + keys],
                                            q_stack[n.parity][:, h, :], start=True, stop=True)
                last.then_inc(s["logits_mm"], 1)

            def values(n, k):
                g, c = k // 4, k % 4
                pe.wait_ge(s["exp_done"], n.count(16, k + 1))
                if k in (0, 8) and (n - 1).real():
                    pe.wait_ge(heads_ready[k // 8], n.count())
                keys, chunk, o = (T, 3, 0) if c == 0 else (KC, c - 1, 1)
                for j in range(4):
                    h = 4 * g + j
                    col = (2 * (g % 2) + o) * T
                    last = nc.tensor.matmul(bank[6 + g // 2][32 * j:32 * j + 32, col:col + T], v[n.parity][0:keys, chunk, h, :],
                                            probs[k % 4][0:keys, j, :], start=(c <= 1), stop=(c == 0 or c == 3))
                last.then_inc(s["pv_done"], 1)

            def step(b):
                if (b - 3).real():
                    n = b - 3
                    pe.wait_ge(s_mr[n.parity], n.turn(16, 16))
                for k in range(16):
                    if (b - 3).real():
                        logits(b - 3, k)
                    if (b - 2).real() and k % 2 == 0:
                        max_scores(b - 2, k // 2)
                    if (b - 3).real() and k >= 1:
                        values(b - 3, k - 1)
                if (b - 3).real():
                    values(b - 3, 15)
                if b.real():
                    pe.wait_ge(s["xn_ready"], b.count(1, 1))
                    if (b - 2).real():
                        pe.wait_ge(s["max_done"], (b - 2).count(8, 8))
                    elif (b - 1).real():
                        pe.wait_ge(s["rest_done"], 6)
                    for h in range(2):
                        last = nc.tensor.transpose(bank[0][:, h * T:(h + 1) * T], xn[b.parity][:, h * P:(h + 1) * P], ident[0:T, 0:T])
                    last.then_inc(s["xt_mm"], 1)
                    pe.wait_ge(s_ctx[b.parity], b.turn(16, 16))
                    for h in range(2):
                        for c in range(NC):
                            last = nc.tensor.transpose(bank[1 + h][:, c * KC:(c + 1) * KC], ctx_in[b.parity][:, c, h * P:(h + 1) * P],
                                                       ident[0:KC, 0:KC])
                    last.then_inc(s["ct_mm"], 1)
                if (b - 2).real():
                    n = b - 2
                    pe.wait_ge(s["msplit"], n.count(4, 4))
                    pe.wait_ge(s["max_done"], n.count(8, 8))
                    nc.tensor.transpose(bank[3][0:QK, 256:256 + T // 2].bitcast(BF16), max_parts[:, :, :, :].rearrange("t s k h -> t (s k h)"),
                                        ident16[0:T, 0:T]).then_inc(s["mt_mm"], 1)
                if (b - 1).real():
                    n = b - 1
                    if b.real():
                        pe.wait_ge(s["xt_ready"], b.count(1, 1))
                        pe.wait_ge(s["ct_ready"], b.count(2, 1))
                    else:
                        pe.wait_ge(s["max_done"], (b - 2).count(8, 8))
                    for c in range(2):
                        for h in range(2):
                            last = nc.tensor.matmul(bank[0][0:KC, c * D:(c + 1) * D], ct[n.parity][:, h, c * KC:(c + 1) * KC],
                                                    w_aux[:, h, D:2 * D], start=(h == 0), stop=(h == 1))
                    last.then_inc(s["v01_mm"], 1)
                    for h in range(2):
                        nc.tensor.matmul(bank[1][0:KC, 0:D], ct[n.parity][:, h, 2 * KC:3 * KC], w_aux[:, h, D:2 * D],
                                         start=(h == 0), stop=(h == 1))
                    for h in range(2):
                        last = nc.tensor.matmul(bank[1][0:T, D:2 * D], xt[n.parity][:, h, :], w_x[:, h, 2 * D:3 * D],
                                                start=(h == 0), stop=(h == 1))
                    last.then_inc(s["v23_mm"], 1)
                if (b - 3).real():
                    n = b - 3
                    if (b - 2).real():
                        pe.wait_ge(s["mt_ready"], (b - 2).count(1, 1))
                    pe.wait_ge(s["mixed_ready"], n.count(2, 2))
                    for g in range(HG):
                        last = nc.tensor.matmul(bank[3][0:T, 0:D], mixed[:, g, :], wo[:, g, :], start=(g == 0), stop=(g == HG - 1))
                    last.then_inc(s["wo_mm"], 1)
                if b.real():
                    pe.wait_ge(s["xt_ready"], b.count(1, 1))
                    pe.wait_ge(s["ct_ready"], b.count(2, 2))
                    for h in range(2):
                        for o in range(2):
                            col = (1 - o) * D + h * P
                            for a_ in range(2):
                                last = nc.tensor.matmul(bank[2][:, (2 * h + o) * T:(2 * h + o + 1) * T], w_x[:, a_, col:col + P],
                                                        xt[b.parity][:, a_, :], start=(a_ == 0), stop=(a_ == 1))
                    last.then_inc(s["qk_mm"], 1)
                    for h in range(2):
                        if h == 0 and (b - 1).real():
                            pe.wait_ge(s["v_ready"], (b - 1).count(3, 1))
                        elif h == 1 and (b - 3).real():
                            pe.wait_ge(s["x1_ready"], (b - 3).count(1, 1))
                        elif h == 1 and (b - 2).real():
                            pe.wait_ge(s["mt_ready"], (b - 2).count(1, 1))
                        for a_ in range(2):
                            last = nc.tensor.matmul(bank[(0, 3)[h]][:, 0:S], w_aux[:, a_, h * P:(h + 1) * P], ct[b.parity][:, a_, :],
                                                    start=(a_ == 0), stop=(a_ == 1))
                        last.then_inc(s[f"ka{h}_mm"], 1)

            attention_steps(pe, step)


def routing(nc, g, phase, experts, tag):
    def sb(name, shape, dt=F32):
        return g.sb(f"{name}{tag}", shape, dt, phase)

    r = Shared()
    r.logits = sb("logits", [T, B, experts])
    r.best = sb("best", [T, B])
    r.cand = sb("cand", [T, B, experts])
    r.which = sb("which", [T, B])
    r.iota_e = sb("iota_e", [T, experts])
    r.onehot = sb("onehot", [T, experts, B])
    r.before = sb("before", [T, T])
    r.ones = sb("ones", [T, T])
    r.total = sb("total", [T, experts, B])
    r.carry = sb("carry", [T, experts, B])
    r.upto = sb("upto", [T, experts, B])
    r.rank = sb("rank", [T, experts, B])
    r.place = sb("place", [T, B])
    r.place_i = sb("place_i", [T, B], I32)
    r.row_bank, r.total_bank = g.bank[0][0:T, 0:experts * B], g.bank[1][0:T, 0:experts * B]

    def constants(pool, made):
        nc.gpsimd.iota(r.iota_e[:, :], [[1, experts]], base=0, channel_multiplier=0,
                       allow_small_or_imprecise_dtypes=True).then_inc(made, 1)
        nc.gpsimd.memset(r.ones[:, :], 1.0).then_inc(made, 1)
        nc.gpsimd.memset(r.before[:, :], 1.0).then_inc(made, 1)
        nc.gpsimd.memset(r.carry[:, :, :], 1.0).then_inc(made, 1)
        pool.wait_ge(made, 4)
        nc.gpsimd.affine_select(out=r.before[:, :], in_=r.before[:, :], compare_op=ALU.is_gt, fill=0.0, base=0,
                                pattern=[[1, T]], channel_multiplier=-1).then_inc(made, 1)
        pool.wait_ge(made, 5)
        nc.gpsimd.memset(r.carry[:, :, 0:1], 0.0).then_inc(made, 1)
        pool.wait_ge(made, 6)

    def choose(dve, step):
        wide = (T, B, experts)
        best = r.best[:, :].rearrange("t (b o) -> t b o", o=1).broadcast_to(wide)
        nc.vector.tensor_reduce(r.best[:, :], r.logits[:, :, :], AX, ALU.max).then_inc(step, 1)
        dve.wait_ge(step, 1)
        nc.vector.tensor_tensor(r.cand[:, :, :], r.logits[:, :, :], best, ALU.is_lt).then_inc(step, 1)
        dve.wait_ge(step, 2)
        numbers = r.iota_e[:, :].rearrange("t (o e) -> t o e", o=1).broadcast_to(wide)
        nc.vector.scalar_tensor_tensor(out=r.cand[:, :, :], in0=r.cand[:, :, :], scalar=FAR, in1=numbers,
                                       op0=ALU.mult, op1=ALU.add).then_inc(step, 1)
        dve.wait_ge(step, 3)
        nc.vector.tensor_reduce(r.which[:, :], r.cand[:, :, :], AX, ALU.min).then_inc(step, 1)
        dve.wait_ge(step, 4)
        nc.vector.tensor_tensor(r.onehot[:, :, :], r.iota_e[:, :].rearrange("t (e o) -> t e o", o=1).broadcast_to((T, experts, B)),
                                r.which[:, :].rearrange("t (o b) -> t o b", o=1).broadcast_to((T, experts, B)),
                                ALU.is_equal).then_inc(step, 1)

    def count_rows(pe, step, counted):
        pe.wait_ge(step, 5)
        flat = r.onehot[:, :, :].rearrange("t e b -> t (e b)")
        nc.tensor.matmul(r.row_bank, r.before[:, :], flat, start=True, stop=True).then_inc(counted, 1)
        nc.tensor.matmul(r.total_bank, r.ones[:, :], flat, start=True, stop=True).then_inc(counted, 1)

    def rank(dve, step, counted):
        dve.wait_ge(counted, 2)
        flat = "t e b -> t (e b)"
        nc.vector.tensor_copy(r.total[:, :, :].rearrange(flat), r.total_bank).then_inc(step, 1)
        dve.wait_ge(step, 6)
        nc.vector.tensor_tensor_scan(r.upto[:, :, :].rearrange(flat), r.carry[:, :, :].rearrange(flat),
                                     r.total[:, :, :].rearrange(flat), 0.0, ALU.mult, ALU.add).then_inc(step, 1)
        dve.wait_ge(step, 7)
        nc.vector.tensor_tensor(r.rank[:, :, :], r.upto[:, :, :], r.total[:, :, :], ALU.subtract).then_inc(step, 1)
        dve.wait_ge(step, 8)
        nc.vector.tensor_tensor(r.rank[:, :, :].rearrange(flat), r.row_bank, r.rank[:, :, :].rearrange(flat), ALU.add).then_inc(step, 1)
        dve.wait_ge(step, 9)

    def pick(dve, out, step, n):
        nc.vector.tensor_tensor(r.rank[:, :, :], r.rank[:, :, :], r.onehot[:, :, :], ALU.mult).then_inc(step, 1)
        dve.wait_ge(step, n + 1)
        nc.vector.tensor_reduce(out, r.rank[:, :, :].rearrange("t e b -> t b e"), AX, ALU.add).then_inc(step, 1)
        dve.wait_ge(step, n + 2)

    r.constants, r.choose, r.count_rows, r.rank_rows, r.pick = constants, choose, count_rows, rank, pick
    return r


def ffn0(nc, a, g):
    bank, xs = g.bank, g.xs
    K2 = F0 // P
    with ExitStack() as phase:
        def sb(name, shape, dt=F32):
            return g.sb(name, shape, dt, phase)

        def sems(names):
            return {n: g.sem("f0_" + n) for n in names.split()}

        wr = sb("wr", [P, 2, E0])
        br = sb("br", [T, E0])
        b2 = sb("b2", [P, E0, D])
        ln_stats = [sb(f"f0_stats{p}", [T, 6]) for p in range(2)]
        ln_mv = [sb(f"f0_mv{p}", [T, 2]) for p in range(2)]
        ln_rstd = [sb(f"f0_rstd{p}", [T, 2]) for p in range(2)]
        xn = [sb(f"f0_xn{p}", [T, D]) for p in range(2)]
        rows = sb("f0_rows", [T, B, D])
        xt = [sb(f"f0_xt{p}", [P, 2, T]) for p in range(2)]
        tile_no = sb("tile_no", [T, TILES])
        edges = sb("edges", [T, ROW_TILES])
        over = sb("over", [T, E0, ROW_TILES])
        tiles_of = sb("tiles_of", [T, E0])
        tiles_to = sb("tiles_to", [T, E0])
        starts = sb("starts", [T, E0])
        passed = sb("passed", [1, TILES, E0])
        owner = sb("owner", [1, TILES])
        owner_i = sb("owner_i", [1, TILES], I32)
        g.place0 = g.sb("place0", [T, B], I32, phase)
        s = sems("""loaded made stats mv eps rstd xn xt_mm xt row logits_mm logits step counted placed scattered
            in_free x_mm x_copy up up_copy back back_copy down down_copy gathered dve_turns sp_turns pool_turns act_turns x2""")
        s_in = [g.sem(f"f0_tile_loaded{p}") for p in range(2)]
        s_out = [g.sem(f"f0_tile_stored{p}") for p in range(2)]
        r = routing(nc, g, phase, E0, "_0")

        block = nc.Block()
        with block:
            @block.sync
            def _(sp):
                sp.dma_start(wr[:, :, :], a["L0_ffn_Wr"].rearrange("(k p) e -> p k e", p=P)).then_inc(s["loaded"], 16)
                sp.dma_start(br[:, :], a["L0_ffn_br"].rearrange("(o e) -> o e", o=1).broadcast_to((T, E0))).then_inc(s["loaded"], 16)
                sp.dma_start(b2[:, :, :], a["L0_ffn_b2"].rearrange("(o e) d -> o e d", o=1).broadcast_to((P, E0, D))).then_inc(s["loaded"], 16)
                sp.wait_ge(s["loaded"], 48)

            @block.gpsimd
            def _(pool):
                r.constants(pool, s["made"])
                nc.gpsimd.iota(tile_no[:, :], [[1, TILES]], base=0, channel_multiplier=0,
                               allow_small_or_imprecise_dtypes=True).then_inc(s["made"], 1)
                nc.gpsimd.iota(edges[:, :], [[P, ROW_TILES]], base=0, channel_multiplier=0,
                               allow_small_or_imprecise_dtypes=True).then_inc(s["made"], 1)
                pool.wait_ge(s["made"], 8)

                def step(b):
                    if b.real():
                        pool.wait_ge(s["mv"], b.count(1, 1))
                        nc.gpsimd.tensor_tensor(ln_rstd[b.parity][:, 0:1], ln_mv[b.parity][:, 1:2], g.eps[0:T, :], ALU.add).then_inc(s["eps"], 1)
                        pool.wait_ge(s["eps"], b.count(1, 1))
                        nc.gpsimd.tensor_tensor(ln_rstd[b.parity][:, 1:2], ln_rstd[b.parity][:, 0:1], g.neg_half[0:T, :], ALU.pow).then_inc(s["rstd"], 1)

                steps(pool, step, B, 0, B - 1, B)
                pool.wait_ge(s["placed"], 1)
                pool.wait_ge(s["row"], B)
                for b in range(B):
                    pool.indirect_dma_start(out=g.sorted0, out_offset=bass.IndirectOffsetOnAxis(g.place0[:, b:b + 1], 0),
                                            in_=rows[:, b, :], in_offset=None).then_inc(s["scattered"], 16)
                pool.wait_ge(s["scattered"], 16 * B)

            @block.scalar
            def _(act):
                def step(b):
                    if b.real():
                        act.wait_ge(s["xn"], b.count(1, 1))
                        nc.scalar.copy(rows[:, b.at(), :].rearrange("t o d -> t (o d)"), xn[b.parity][:, :]).then_inc(s["row"], 1)
                        act.wait_ge(s["xt_mm"], b.count(1, 1))
                        if (b - 2).real():
                            act.wait_ge(s["logits_mm"], (b - 2).count(1, 1))
                        nc.scalar.copy(xt[b.parity][:, :, :], bank[2 + b.parity][:, 0:2 * T].rearrange("p (k t) -> p k t", k=2)).then_inc(s["xt"], 1)

                steps(act, step, B, 2, B - 1, B)

            @block.vector
            def _(dve):
                def step(b):
                    n = b
                    row = xs[:, n.at(), :].rearrange("t o d -> t (o d)")
                    if (n - 2).real():
                        dve.wait_ge(s["xt_mm"], (n - 2).count(1, 1))
                        dve.wait_ge(s["row"], (n - 2).count(1, 1))
                    nc.vector.bn_stats(ln_stats[n.parity][:, :], row).then_inc(s["stats"], 1)
                    dve.wait_ge(s["stats"], n.count(1, 1))
                    dve.sem_inc(s["dve_turns"], 1)
                    nc.vector.bn_aggr(ln_mv[n.parity][:, :], ln_stats[n.parity][:, :]).then_inc(s["mv"], 1)
                    dve.wait_ge(s["rstd"], n.count(1, 1))
                    nc.vector.tensor_scalar(xn[n.parity][:, :], row, ln_mv[n.parity][:, 0:1], ln_rstd[n.parity][:, 1:2],
                                            ALU.subtract, ALU.mult).then_inc(s["xn"], 1)

                steps(dve, step, B, 2, B - 1, B)
                dve.wait_ge(s["logits_mm"], B)
                dve.wait_ge(s["loaded"], 48)
                dve.wait_ge(s["made"], 8)
                nc.vector.tensor_tensor(r.logits[:, :, :], bank[4][0:T, 0:B * E0].rearrange("t (b e) -> t b e", b=B),
                                        br[:, :].rearrange("t (o e) -> t o e", o=1).broadcast_to((T, B, E0)), ALU.add).then_inc(s["logits"], 1)
                dve.wait_ge(s["logits"], 1)
                step_ = s["step"]
                r.choose(dve, step_)
                r.rank_rows(dve, step_, s["counted"])
                count = r.upto[:, :, B - 1:B].broadcast_to((T, E0, ROW_TILES))
                nc.vector.tensor_tensor(over[:, :, :], count, edges[:, :].rearrange("t (o k) -> t o k", o=1).broadcast_to((T, E0, ROW_TILES)),
                                        ALU.is_gt).then_inc(step_, 1)
                dve.wait_ge(step_, 10)
                nc.vector.tensor_reduce(tiles_of[:, :], over[:, :, :], AX, ALU.add).then_inc(step_, 1)
                dve.wait_ge(step_, 11)
                nc.vector.tensor_tensor_scan(tiles_to[:, :], r.ones[:, 0:E0], tiles_of[:, :], 0.0, ALU.mult, ALU.add).then_inc(step_, 1)
                dve.wait_ge(step_, 12)
                nc.vector.tensor_tensor(starts[:, :], tiles_to[:, :], tiles_of[:, :], ALU.subtract).then_inc(step_, 1)
                dve.wait_ge(step_, 13)
                nc.vector.scalar_tensor_tensor(out=r.rank[:, :, :], in0=starts[:, :].rearrange("t (e o) -> t e o", o=1).broadcast_to((T, E0, B)),
                                               scalar=float(P), in1=r.rank[:, :, :], op0=ALU.mult, op1=ALU.add).then_inc(step_, 1)
                dve.wait_ge(step_, 14)
                r.pick(dve, r.place[:, :], step_, 14)
                nc.vector.tensor_copy(g.place0[:, :], r.place[:, :]).then_inc(s["placed"], 1)
                nc.vector.tensor_tensor(passed[:, :, :], tiles_to[0:1, :].rearrange("t (o e) -> t o e", o=1).broadcast_to((1, TILES, E0)),
                                        tile_no[0:1, :].rearrange("t (j o) -> t j o", o=1).broadcast_to((1, TILES, E0)), ALU.is_le).then_inc(step_, 1)
                dve.wait_ge(step_, 17)
                nc.vector.tensor_reduce(owner[:, :], passed[:, :, :], AX, ALU.add).then_inc(step_, 1)
                dve.wait_ge(step_, 18)
                nc.vector.tensor_scalar(owner_i[:, :], owner[:, :], float(E0 - 1), None, ALU.min).then_inc(s["placed"], 1)

            @block.tensor
            def _(pe):
                pe.wait_ge(s["loaded"], 48)

                def step(b):
                    if b.real():
                        pe.wait_ge(s["xn"], b.count(1, 1))
                        if (b - 2).real():
                            pe.wait_ge(s["xt"], (b - 2).count(1, 1))
                        for h in range(2):
                            last = nc.tensor.transpose(bank[2 + b.parity][:, h * T:(h + 1) * T],
                                                       xn[b.parity][:, h * P:(h + 1) * P], g.ident[0:T, 0:T])
                        last.then_inc(s["xt_mm"], 1)
                    if (b - 1).real():
                        n = b - 1
                        pe.wait_ge(s["xt"], n.count(1, 1))
                        for h in range(2):
                            last = nc.tensor.matmul(bank[4][0:T, n.rows(E0)], xt[n.parity][:, h, :], wr[:, h, :],
                                                    start=(h == 0), stop=(h == 1))
                        last.then_inc(s["logits_mm"], 1)

                steps(pe, step, B, 2, B - 1, B + 1)
                pe.wait_ge(s["made"], 8)
                r.count_rows(pe, s["step"], s["counted"])

        with ExitStack() as tiles:
            def tb(name, shape, dt=F32):
                return g.sb(name, shape, dt, tiles)

            x_in = [tb(f"t0_in{p}", [P, D]) for p in range(2)]
            xt2 = [tb(f"t0_xt{p}", [P, 2, P]) for p in range(2)]
            up = [tb(f"t0_up{p}", [P, F0]) for p in range(2)]
            hid = [tb(f"t0_hid{p}", [P, K2, P]) for p in range(2)]
            y = [tb(f"t0_y{p}", [P, D]) for p in range(2)]
            end = TILES + 2

            def tile_steps(engine, step):
                steps(engine, step, TILES, 4, TILES - 3, end)

            block = nc.Block()
            with block:
                @block.sync
                def _(sp):
                    def load(j):
                        sp.dma_start(x_in[j.parity][:, :], g.sorted0[j.rows(P), :]).then_inc(s_in[j.parity], 16)

                    load(Item(0, 0, TILES))
                    load(Item(0, 1, TILES))

                    def step(j):
                        if (j + 2).real():
                            sp.wait_ge(s["x_mm"], j.count(1, 1))
                            sp.sem_inc(s["sp_turns"], 1)
                            load(j + 2)
                        if (j - 2).real():
                            n = j - 2
                            sp.wait_ge(s["down_copy"], n.count(1, 1))
                            sp.sem_inc(s["sp_turns"], 1)
                            sp.dma_start(g.made0[n.rows(P), :], y[n.parity][:, :]).then_inc(s_out[n.parity], 16)

                    tile_steps(sp, step)
                    sp.wait_ge(s_out[0], 16 * ((TILES + 1) // 2))
                    sp.wait_ge(s_out[1], 16 * (TILES // 2))

                @block.scalar
                def _(act):
                    def step(j):
                        if j.real():
                            act.wait_ge(s["x_mm"], j.count(1, 1))
                            if (j - 2).real():
                                act.wait_ge(s["up"], (j - 2).count(1, 1))
                            nc.scalar.copy(xt2[j.parity][:, :, :], bank[2 + j.parity][:, 0:2 * P].rearrange("p (k t) -> p k t", k=2)).then_inc(s["x_copy"], 1)
                        if (j - 1).real():
                            n = j - 1
                            e = act.value_load(owner_i[0:1, n.at()], min_val=0, max_val=E0 - 1)
                            act.wait_ge(s["back"], n.count(1, 1))
                            if (n - 2).real():
                                act.wait_ge(s["down"], (n - 2).count(1, 1))
                            for f in range(K2):
                                bias = g.b1[:, bass.ds(e, 1), f:f + 1].rearrange("p o f -> p (o f)")
                                nc.scalar.activation(hid[n.parity][:, f, :], bank[4 + n.parity][:, f * P:(f + 1) * P], ACT.Relu,
                                                     bias=bias).then_inc(s["back_copy"], 1)

                    tile_steps(act, step)

                @block.vector
                def _(dve):
                    def step(j):
                        if j.real():
                            dve.wait_ge(s["up"], j.count(1, 1))
                            if (j - 2).real():
                                dve.wait_ge(s["back"], (j - 2).count(1, 1))
                            nc.vector.tensor_copy(up[j.parity][:, :], bank[j.parity][:, :]).then_inc(s["up_copy"], 1)
                        if (j - 2).real():
                            n = j - 2
                            e = dve.value_load(owner_i[0:1, n.at()], min_val=0, max_val=E0 - 1)
                            dve.wait_ge(s["down"], n.count(1, 1))
                            if (n - 2).real():
                                dve.wait_ge(s_out[n.parity], (n - 2).turn(16, 16))
                            nc.vector.tensor_tensor(y[n.parity][:, :], bank[6 + n.parity][:, 0:D],
                                                    b2[:, bass.ds(e, 1), :].rearrange("p o d -> p (o d)"), ALU.add).then_inc(s["down_copy"], 1)

                    tile_steps(dve, step)

                @block.tensor
                def _(pe):
                    def transpose_in(j):
                        pe.wait_ge(s_in[j.parity], j.turn(16, 16))
                        if (j - 2).real():
                            pe.wait_ge(s["x_copy"], (j - 2).count(1, 1))
                        for h in range(2):
                            last = nc.tensor.transpose(bank[2 + j.parity][:, h * P:(h + 1) * P], x_in[j.parity][:, h * P:(h + 1) * P], g.ident[:, :])
                        last.then_inc(s["x_mm"], 1)

                    transpose_in(Item(0, 0, TILES))

                    def step(j):
                        if j.real():
                            e = pe.value_load(owner_i[0:1, j.at()], min_val=0, max_val=E0 - 1)
                            pe.wait_ge(s["x_copy"], j.count(1, 1))
                            if (j - 2).real():
                                pe.wait_ge(s["up_copy"], (j - 2).count(1, 1))
                            for h in range(2):
                                last = nc.tensor.matmul(bank[j.parity][:, :], xt2[j.parity][:, h, :],
                                                        g.w1[:, bass.ds(e, 1), h, :].rearrange("p o f -> p (o f)"), start=(h == 0), stop=(h == 1))
                            last.then_inc(s["up"], 1)
                        if (j + 1).real():
                            transpose_in(j + 1)
                        if (j - 2).real():
                            n = j - 2
                            e = pe.value_load(owner_i[0:1, n.at()], min_val=0, max_val=E0 - 1)
                            pe.wait_ge(s["back_copy"], n.count(K2, K2))
                            if (n - 2).real():
                                pe.wait_ge(s["down_copy"], (n - 2).count(1, 1))
                            for f in range(K2):
                                last = nc.tensor.matmul(bank[6 + n.parity][:, 0:D], hid[n.parity][:, f, :],
                                                        g.w2[:, bass.ds(e, 1), f, :].rearrange("p o d -> p (o d)"), start=(f == 0), stop=(f == K2 - 1))
                            last.then_inc(s["down"], 1)
                        if (j - 1).real():
                            n = j - 1
                            pe.wait_ge(s["up_copy"], n.count(1, 1))
                            if (n - 2).real():
                                pe.wait_ge(s["back_copy"], (n - 2).count(K2, K2))
                            for f in range(K2):
                                last = nc.tensor.transpose(bank[4 + n.parity][:, f * P:(f + 1) * P], up[n.parity][:, f * P:(f + 1) * P], g.ident[:, :])
                            last.then_inc(s["back"], 1)

                    tile_steps(pe, step)

        with ExitStack() as back:
            got = g.sb("got0", [T, B, D], F32, back)
            block = nc.Block()
            with block:
                @block.gpsimd
                def _(pool):
                    for b in range(B):
                        pool.indirect_dma_start(out=got[:, b, :], out_offset=None, in_=g.made0,
                                                in_offset=bass.IndirectOffsetOnAxis(g.place0[:, b:b + 1], 0)).then_inc(s["gathered"], 16)
                    pool.wait_ge(s["gathered"], 16 * B)

                @block.vector
                def _(dve):
                    dve.wait_ge(s["gathered"], 16 * B)
                    nc.vector.tensor_tensor(xs[:, :, :], xs[:, :, :], got[:, :, :], ALU.add).then_inc(s["x2"], 1)


def attention1(nc, a, g):
    bank, xs, ident = g.bank, g.xs, g.ident
    K2 = D // P
    with ExitStack() as phase:
        def sb(name, shape, dt=F32):
            return g.sb("a1_" + name, shape, dt, phase)

        def pair(name, shape, dt=F32):
            return [sb(f"{name}{p}", shape, dt) for p in range(2)]

        def psem(name):
            return [g.sem(f"a1_{name}{p}") for p in range(2)]

        weights = {n: sb(n, [P, K2, D]) for n in ("Wk", "Wv", "Wq", "Wo")}
        wo_t = sb("wo_t", [P, K2, D])
        w_qk = sb("w_qk", [P, K2, D])
        w_vo = sb("w_vo", [P, K2, D])
        bq = sb("bq", [P, K2])
        bv = sb("bv", [P, K2])
        bv_wide = sb("bv_wide", [P, K2, T])
        u = sb("u", [P, K2])
        row = sb("row", [T, D])
        xn2, xn3 = pair("xn2", [T, D]), pair("xn3", [T, D])
        xt2, xt3 = pair("xt2", [P, 2, T]), pair("xt3", [P, 2, T])
        stats2, stats3 = sb("stats2", [T, 6]), sb("stats3", [T, 6])
        mv2, mv3 = sb("mv2", [T, 2]), sb("mv3", [T, 2])
        rstd2, rstd3 = sb("rstd2", [T, 2]), sb("rstd3", [T, 2])
        q = pair("q", [P, 2, T])
        ct = pair("ct", [P, 2, S])
        cin = pair("ctx", [KC, NC, D])
        neg_max, total, inverse = pair("neg_max", [T, 1]), pair("total", [T, 1]), pair("inverse", [T, 1])
        prob = pair("prob", [T, S])
        prob_t = pair("prob_t", [KC, NC, T])
        mix = pair("mix", [P, 2, T])
        wg = sb("wg", [P, 2, E1])
        s = {n: g.sem("a1_" + n) for n in """loaded setup_mm setup_copy stats2 mv2 eps2 rstd2 xn2 xc t2 xt2 q_mm q scored maxed
            prob tp prob_t mix_mm mix out_mm inverse x3 stats3 mv3 eps3 rstd3 xn3 rows t3 xt3 logits_mm dve_turns sp_turns""".split()}
        s_ct, s_cin = psem("ct_loaded"), psem("ctx_loaded")
        g.rows1 = g.rows1_buffer
        SETUP = 6
        block = nc.Block()
        with block:
            @block.sync
            def _(sp):
                for n, w in weights.items():
                    sp.dma_start(w[:, :, :], a["L1_xattn_" + n].rearrange("(k p) d -> p k d", p=P)).then_inc(s["loaded"], 16)
                for b_, n in ((bq, "L1_xattn_bq"), (bv, "L1_xattn_bv")):
                    for k in range(K2):
                        sp.dma_start(b_[:, k:k + 1], a[n][k * P:(k + 1) * P].rearrange("(p o) -> p o", o=1)).then_inc(s["loaded"], 16)
                sp.dma_start(row[:, :], a["L1_xattn_bo"].rearrange("(o n) -> o n", o=1).broadcast_to((T, D))).then_inc(s["loaded"], 16)
                sp.dma_start(wg[:, :, :], a["L1_ffn_Wg"].rearrange("(k p) e -> p k e", p=P)).then_inc(s["loaded"], 16)

                def load_cin(b):
                    src = a["ctx_1024"][b.at()].rearrange("o (c k) d -> k (o c) d", k=KC)
                    sp.dma_start(cin[b.parity][:, :, :], src).then_inc(s_cin[b.parity], 16)

                def load_ct(b):
                    sp.dma_start(ct[b.parity][:, :, :], g.ct_dram[b.at()].rearrange("o p k n -> p (o k) n")).then_inc(s_ct[b.parity], 16)

                def step(b):
                    if b.real():
                        if (b - 2).real():
                            sp.wait_ge(s["scored"], (b - 2).count(1, 1))
                            sp.sem_inc(s["sp_turns"], 1)
                        load_ct(b)
                    if (b - 1).real():
                        n = b - 1
                        if (n - 2).real():
                            sp.wait_ge(s["mix_mm"], (n - 2).count(1, 1))
                            sp.sem_inc(s["sp_turns"], 1)
                        load_cin(n)
                    if isinstance(b.i, int) and b.c == 1:
                        for e in range(4):
                            load_w(nc, sp, a, g, Item(0, e, E1, 4), 1)
                            load_w(nc, sp, a, g, Item(0, e, E1, 4), 2)

                steps(sp, step, B, 3, B - 2, B + 1)

            def rstd_of(pool, b, k, mv, rstd):
                pool.wait_ge(s[f"mv{k}"], b.count(1, 1))
                nc.gpsimd.tensor_tensor(rstd[:, 0:1], mv[:, 1:2], g.eps[0:T, :], ALU.add).then_inc(s[f"eps{k}"], 1)
                pool.wait_ge(s[f"eps{k}"], b.count(1, 1))
                nc.gpsimd.tensor_tensor(rstd[:, 1:2], rstd[:, 0:1], g.neg_half[0:T, :], ALU.pow).then_inc(s[f"rstd{k}"], 1)

            @block.gpsimd
            def _(pool):
                def ahead(b):
                    rstd_of(pool, b, 2, mv2, rstd2)
                    pool.wait_ge(s["xn2"], b.count(1, 1))
                    stream = xs[:, b.at(), :].rearrange("t o d -> t (o d)")
                    nc.gpsimd.tensor_tensor(stream, stream, row[:, :], ALU.add).then_inc(s["xc"], 1)

                pool.wait_ge(s["setup_copy"], SETUP)
                ahead(Item(0, 0, B))

                def step(b):
                    if (b + 1).real():
                        ahead(b + 1)
                    if (b - 2).real():
                        rstd_of(pool, b - 2, 3, mv3, rstd3)

                attention_steps(pool, step)


            @block.scalar
            def _(act):
                def step(b):
                    if (b - 1).real():
                        n = b - 1
                        act.wait_ge(s["maxed"], n.count(1, 1))
                        if (n - 2).real():
                            act.wait_ge(s["tp"], (n - 2).count(1, 1))
                            act.wait_ge(s["inverse"], (n - 2).count(1, 1))
                        nc.scalar.activation(prob[n.parity][:, :], bank[0][0:T, 0:S], ACT.Exp, bias=neg_max[n.parity][:, :],
                                             accum_out=total[n.parity][:, :]).then_inc(s["prob"], 1)
                    if (b - 2).real():
                        n = b - 2
                        act.wait_ge(s["mix_mm"], n.count(1, 1))
                        if (n - 2).real():
                            act.wait_ge(s["out_mm"], (n - 2).count(1, 1))
                        nc.scalar.copy(mix[n.parity][:, :, :], bank[1][:, 0:2 * T].rearrange("p (k t) -> p k t", k=2)).then_inc(s["mix"], 1)
                    if b.real():
                        act.wait_ge(s["t2"], b.count(1, 1))
                        if (b - 2).real():
                            act.wait_ge(s["q_mm"], (b - 2).count(1, 1))
                        nc.scalar.copy(xt2[b.parity][:, :, :], bank[2][:, 0:2 * T].rearrange("p (k t) -> p k t", k=2)).then_inc(s["xt2"], 1)
                    if (b - 3).real():
                        n = b - 3
                        act.wait_ge(s["xn3"], n.count(1, 1))
                        nc.scalar.copy(g.rows1[:, n.at(), :].rearrange("t o d -> t (o d)"), xn3[n.parity][:, :]).then_inc(s["rows"], 1)
                        act.wait_ge(s["t3"], n.count(1, 1))
                        if (n - 2).real():
                            act.wait_ge(s["logits_mm"], (n - 2).count(1, 1))
                        nc.scalar.copy(xt3[n.parity][:, :, :], bank[3][:, 0:2 * T].rearrange("p (k t) -> p k t", k=2)).then_inc(s["xt3"], 1)
                    if b.real():
                        act.wait_ge(s["q_mm"], b.count(1, 1))
                        if (b - 2).real():
                            act.wait_ge(s["scored"], (b - 2).count(1, 1))
                        for h in range(2):
                            nc.scalar.activation(q[b.parity][:, h, :], bank[6][:, h * T:(h + 1) * T], ACT.Identity,
                                                 bias=u[:, h:h + 1], scale=D ** -0.5).then_inc(s["q"], 1)

                act.wait_ge(s["setup_copy"], SETUP)
                steps(act, step, B, 5, B - 2, B + 3)

            @block.vector
            def _(dve):
                dve.wait_ge(s["loaded"], 16 * 10)
                nc.vector.tensor_copy(bv_wide[:, :, :], bv[:, :].rearrange("p (k o) -> p k o", o=1).broadcast_to((P, K2, T))).then_inc(s["setup_copy"], 1)
                dve.wait_ge(s["setup_mm"], 1)
                nc.vector.tensor_copy(wo_t[:, :, :], bank[0][:, :].rearrange("p (k d) -> p k d", k=K2)).then_inc(s["setup_copy"], 1)
                dve.wait_ge(s["setup_mm"], 2)
                nc.vector.tensor_copy(w_qk[:, :, :], bank[1][:, :].rearrange("p (k d) -> p k d", k=K2)).then_inc(s["setup_copy"], 1)
                dve.wait_ge(s["setup_mm"], 4)
                nc.vector.tensor_scalar(u[:, :], bank[3][:, 0:K2], D ** -0.5, None, ALU.mult).then_inc(s["setup_copy"], 1)
                nc.vector.tensor_copy(w_vo[:, :, :], bank[2][:, :].rearrange("p (k d) -> p k d", k=K2)).then_inc(s["setup_copy"], 1)
                dve.wait_ge(s["setup_mm"], 5)
                nc.vector.tensor_tensor(row[:, :], bank[4][0:T, 0:D], row[:, :], ALU.add).then_inc(s["setup_copy"], 1)
                dve.wait_ge(s["setup_copy"], 6)

                def norm(b, k, stats, mv, rstd, xn, t_done, row_done=None):
                    stream = xs[:, b.at(), :].rearrange("t o d -> t (o d)")
                    nc.vector.bn_stats(stats[:, :], stream).then_inc(s[f"stats{k}"], 1)
                    dve.wait_ge(s[f"stats{k}"], b.count(1, 1))
                    dve.sem_inc(s["dve_turns"], 1)
                    nc.vector.bn_aggr(mv[:, :], stats[:, :]).then_inc(s[f"mv{k}"], 1)
                    dve.wait_ge(s[f"rstd{k}"], b.count(1, 1))
                    if (b - 2).real():
                        dve.wait_ge(t_done, (b - 2).count(1, 1))
                        if row_done is not None:
                            dve.wait_ge(row_done, (b - 2).count(1, 1))
                    nc.vector.tensor_scalar(xn[b.parity][:, :], stream, mv[:, 0:1], rstd[:, 1:2], ALU.subtract, ALU.mult).then_inc(s[f"xn{k}"], 1)

                norm(Item(0, 0, B), 2, stats2, mv2, rstd2, xn2, s["t2"])

                def step(b):
                    if (b - 1).real():
                        n = b - 1
                        dve.wait_ge(s["scored"], n.count(1, 1))
                        if (n - 2).real():
                            dve.wait_ge(s["prob"], (n - 2).count(1, 1))
                        nc.vector.tensor_reduce(neg_max[n.parity][:, :], bank[0][0:T, 0:S], AX, ALU.max, negate=True).then_inc(s["maxed"], 1)
                    if (b + 1).real():
                        norm(b + 1, 2, stats2, mv2, rstd2, xn2, s["t2"])
                    if (b - 1).real():
                        n = b - 1
                        dve.wait_ge(s["prob"], n.count(1, 1))
                        nc.vector.reciprocal(inverse[n.parity][:, :], total[n.parity][:, :]).then_inc(s["inverse"], 1)
                        dve.wait_ge(s["tp"], n.count(1, 1))
                        if (n - 2).real():
                            dve.wait_ge(s["mix_mm"], (n - 2).count(1, 1))
                        nc.vector.tensor_copy(prob_t[n.parity][:, :, :], bank[4][0:KC, 0:NC * T].rearrange("p (c t) -> p c t", c=NC)).then_inc(s["prob_t"], 1)
                    if (b - 2).real():
                        n = b - 2
                        dve.wait_ge(s["out_mm"], n.count(1, 1))
                        dve.wait_ge(s["inverse"], n.count(1, 1))
                        dve.wait_ge(s["xc"], n.count(1, 1))
                        stream = xs[:, n.at(), :].rearrange("t o d -> t (o d)")
                        nc.vector.scalar_tensor_tensor(out=stream, in0=bank[5][0:T, 0:D], scalar=inverse[n.parity][:, :], in1=stream,
                                                       op0=ALU.mult, op1=ALU.add).then_inc(s["x3"], 1)
                        dve.wait_ge(s["x3"], n.count(1, 1))
                        dve.sem_inc(s["dve_turns"], 1)
                        norm(n, 3, stats3, mv3, rstd3, xn3, s["t3"], s["rows"])

                steps(dve, step, B, 4, B - 2, B + 3)

            @block.tensor
            def _(pe):
                pe.wait_ge(s["loaded"], 16 * 10)
                for k in range(K2):
                    for m in range(K2):
                        last = nc.tensor.transpose(bank[0][:, k * D + m * P:k * D + (m + 1) * P], weights["Wo"][:, m, k * P:(k + 1) * P], ident[:, :])
                last.then_inc(s["setup_mm"], 1)

                def product(to, left, right):
                    for m in range(K2):
                        for k in range(K2):
                            last = nc.tensor.matmul(to[:, m * D:(m + 1) * D], left[:, k, m * P:(m + 1) * P], right[:, k, :],
                                                    start=(k == 0), stop=(k == K2 - 1))
                    return last

                product(bank[1], weights["Wq"], weights["Wk"]).then_inc(s["setup_mm"], 1)
                for m in range(K2):
                    for k in range(K2):
                        last = nc.tensor.matmul(bank[3][:, m:m + 1], weights["Wk"][:, k, m * P:(m + 1) * P], bq[:, k:k + 1],
                                                start=(k == 0), stop=(k == K2 - 1))
                last.then_inc(s["setup_mm"], 1)
                pe.wait_ge(s["setup_copy"], 2)
                product(bank[2], weights["Wv"], wo_t).then_inc(s["setup_mm"], 1)
                for k in range(K2):
                    last = nc.tensor.matmul(bank[4][0:T, 0:D], bv_wide[:, k, :], wo_t[:, k, :], start=(k == 0), stop=(k == K2 - 1))
                last.then_inc(s["setup_mm"], 1)
                pe.wait_ge(s["setup_copy"], SETUP)

                def step(b):
                    if (b - 1).real():
                        n = b - 1
                        pe.wait_ge(s_ct[n.parity], n.turn(16, 16))
                        pe.wait_ge(s["q"], n.count(2, 2))
                        if (n - 1).real():
                            pe.wait_ge(s["prob"], (n - 1).count(1, 1))
                        for h in range(2):
                            last = nc.tensor.matmul(bank[0][0:T, 0:S], q[n.parity][:, h, :], ct[n.parity][:, h, :], start=(h == 0), stop=(h == 1))
                        last.then_inc(s["scored"], 1)
                    if (b - 2).real():
                        n = b - 2
                        pe.wait_ge(s_cin[n.parity], n.turn(16, 16))
                        pe.wait_ge(s["prob_t"], n.count(1, 1))
                        if (n - 1).real():
                            pe.wait_ge(s["mix"], (n - 1).count(1, 1))
                        for h in range(2):
                            for c in range(NC):
                                last = nc.tensor.matmul(bank[1][:, h * T:(h + 1) * T], cin[n.parity][:, c, h * P:(h + 1) * P], prob_t[n.parity][:, c, :],
                                                        start=(c == 0), stop=(c == NC - 1))
                        last.then_inc(s["mix_mm"], 1)
                    if b.real():
                        pe.wait_ge(s["xn2"], b.count(1, 1))
                        if (b - 1).real():
                            pe.wait_ge(s["xt2"], (b - 1).count(1, 1))
                        for h in range(2):
                            last = nc.tensor.transpose(bank[2][:, h * T:(h + 1) * T], xn2[b.parity][:, h * P:(h + 1) * P], ident[0:T, 0:T])
                        last.then_inc(s["t2"], 1)
                    if (b - 3).real():
                        n = b - 3
                        pe.wait_ge(s["xn3"], n.count(1, 1))
                        if (n - 1).real():
                            pe.wait_ge(s["xt3"], (n - 1).count(1, 1))
                        for h in range(2):
                            last = nc.tensor.transpose(bank[3][:, h * T:(h + 1) * T], xn3[n.parity][:, h * P:(h + 1) * P], ident[0:T, 0:T])
                        last.then_inc(s["t3"], 1)
                    if (b - 1).real():
                        n = b - 1
                        pe.wait_ge(s["prob"], n.count(1, 1))
                        if (n - 1).real():
                            pe.wait_ge(s["prob_t"], (n - 1).count(1, 1))
                        for c in range(NC):
                            last = nc.tensor.transpose(bank[4][0:KC, c * T:(c + 1) * T], prob[n.parity][:, c * KC:(c + 1) * KC], ident[0:T, 0:T])
                        last.then_inc(s["tp"], 1)
                    if (b - 2).real():
                        n = b - 2
                        pe.wait_ge(s["mix"], n.count(1, 1))
                        if (n - 1).real():
                            pe.wait_ge(s["x3"], (n - 1).count(1, 1))
                        for h in range(2):
                            last = nc.tensor.matmul(bank[5][0:T, 0:D], mix[n.parity][:, h, :], w_vo[:, h, :], start=(h == 0), stop=(h == 1))
                        last.then_inc(s["out_mm"], 1)
                    if b.real():
                        pe.wait_ge(s["xt2"], b.count(1, 1))
                        if (b - 1).real():
                            pe.wait_ge(s["q"], (b - 1).count(2, 2))
                        for h in range(2):
                            for k in range(2):
                                last = nc.tensor.matmul(bank[6][:, h * T:(h + 1) * T], w_qk[:, k, h * P:(h + 1) * P], xt2[b.parity][:, k, :],
                                                        start=(k == 0), stop=(k == 1))
                        last.then_inc(s["q_mm"], 1)
                    if (b - 3).real():
                        n = b - 3
                        pe.wait_ge(s["xt3"], n.count(1, 1))
                        for h in range(2):
                            last = nc.tensor.matmul(bank[7][0:T, n.rows(E1)], xt3[n.parity][:, h, :], wg[:, h, :], start=(h == 0), stop=(h == 1))
                        last.then_inc(s["logits_mm"], 1)

                attention_steps(pe, step)


def load_w(nc, sp, a, g, e, which):
    k = e.quarter
    if which == 1:
        src = a["L1_ffn_w1"][e.at()].rearrange("o (k p) f -> p (o k) f", p=P)
        sp.dma_start(g.ring1[k][:, :, :], src).then_inc(g.s_ring1[k], 16)
    else:
        src = a["L1_ffn_w2"][e.at()].rearrange("o (k p) d -> p (o k) d", p=P)
        sp.dma_start(g.ring2[k][:, :, :], src).then_inc(g.s_ring2[k], 16)


def ffn1(nc, a, out, g):
    bank, xs = g.bank, g.xs
    KF = F1 // P
    with ExitStack() as phase:
        def sb(name, shape, dt=F32):
            return g.sb("f1_" + name, shape, dt, phase)

        shifted = sb("shifted", [T, B, E1])
        sums = sb("sums", [T, B])
        gate = sb("gate", [T, B])
        valid = sb("valid", [T, B])
        spare = sb("spare", [T, B])
        taken = sb("taken", [T, B])
        lost = sb("lost", [T, B])
        target = sb("target", [T, B])
        target_i = sb("target_i", [T, B], I32)
        source_i = sb("source_i", [T, B], I32)
        s = {n: g.sem("f1_" + n) for n in """made logits step counted shifted expd placed scattered x_mm x_copy up hid_a hid_v
            down down_copy sp_turns done""".split()}
        s_in = [g.sem(f"f1_rows_loaded{p}") for p in range(2)]
        s_out = [g.sem(f"f1_rows_stored{p}") for p in range(2)]
        r = routing(nc, g, phase, E1, "_1")
        block = nc.Block()
        with block:
            @block.gpsimd
            def _(pool):
                r.constants(pool, s["made"])
                nc.gpsimd.iota(spare[:, :], [[T, B]], base=E1 * C1, channel_multiplier=1,
                               allow_small_or_imprecise_dtypes=True).then_inc(s["made"], 1)
                pool.wait_ge(s["placed"], 1)
                for b in range(B):
                    pool.indirect_dma_start(out=g.sorted1, out_offset=bass.IndirectOffsetOnAxis(target_i[:, b:b + 1], 0),
                                            in_=g.rows1[:, b, :], in_offset=None).then_inc(s["scattered"], 16)
                pool.wait_ge(s["scattered"], 16 * B)

            @block.scalar
            def _(act):
                act.wait_ge(s["shifted"], 1)
                nc.scalar.activation(shifted[:, :, :], shifted[:, :, :], ACT.Exp).then_inc(s["expd"], 1)

            @block.vector
            def _(dve):
                step = s["step"]
                nc.vector.tensor_copy(r.logits[:, :, :], bank[7][0:T, 0:B * E1].rearrange("t (b e) -> t b e", b=B)).then_inc(s["logits"], 1)
                dve.wait_ge(s["logits"], 1)
                dve.wait_ge(s["made"], 7)
                r.choose(dve, step)
                nc.vector.tensor_tensor(shifted[:, :, :], r.logits[:, :, :], r.best[:, :].rearrange("t (b o) -> t b o", o=1).broadcast_to((T, B, E1)),
                                        ALU.subtract).then_inc(s["shifted"], 1)
                r.rank_rows(dve, step, s["counted"])
                r.pick(dve, r.place[:, :], step, 9)
                nc.vector.tensor_scalar(valid[:, :], r.place[:, :], float(C1), None, ALU.is_lt).then_inc(step, 1)
                dve.wait_ge(step, 12)
                nc.vector.tensor_scalar(r.place[:, :], r.place[:, :], float(C1 - 1), None, ALU.min).then_inc(step, 1)
                dve.wait_ge(step, 13)
                nc.vector.scalar_tensor_tensor(out=r.place[:, :], in0=r.which[:, :], scalar=float(C1), in1=r.place[:, :],
                                               op0=ALU.mult, op1=ALU.add).then_inc(step, 1)
                dve.wait_ge(step, 14)
                nc.vector.tensor_copy(source_i[:, :], r.place[:, :]).then_inc(step, 1)
                nc.vector.tensor_tensor(taken[:, :], r.place[:, :], valid[:, :], ALU.mult).then_inc(step, 1)
                nc.vector.tensor_tensor(lost[:, :], spare[:, :], valid[:, :], ALU.mult).then_inc(step, 1)
                dve.wait_ge(step, 17)
                nc.vector.tensor_tensor(lost[:, :], spare[:, :], lost[:, :], ALU.subtract).then_inc(step, 1)
                dve.wait_ge(step, 18)
                nc.vector.tensor_tensor(target[:, :], taken[:, :], lost[:, :], ALU.add).then_inc(step, 1)
                dve.wait_ge(step, 19)
                nc.vector.tensor_copy(target_i[:, :], target[:, :]).then_inc(s["placed"], 1)
                dve.wait_ge(s["expd"], 1)
                nc.vector.tensor_reduce(sums[:, :], shifted[:, :, :], AX, ALU.add).then_inc(step, 1)
                dve.wait_ge(step, 20)
                nc.vector.reciprocal(gate[:, :], sums[:, :]).then_inc(step, 1)
                dve.wait_ge(step, 21)
                nc.vector.tensor_tensor(gate[:, :], gate[:, :], valid[:, :], ALU.mult).then_inc(step, 1)
                dve.wait_ge(step, 22)

            @block.tensor
            def _(pe):
                pe.wait_ge(s["made"], 7)
                r.count_rows(pe, s["step"], s["counted"])

        with ExitStack() as experts:
            def tb(name, shape, dt=F32):
                return [g.sb(f"e1_{name}{p}", shape, dt, experts) for p in range(2)]

            x_in, xt, hid, y = tb("x_in", [C1, D]), tb("xt", [P, 2, C1]), tb("hid", [P, KF, C1]), tb("y", [C1, D])
            block = nc.Block()
            with block:
                @block.sync
                def _(sp):
                    def load(e):
                        sp.dma_start(x_in[e.parity][:, :], g.sorted1[e.rows(C1), :]).then_inc(s_in[e.parity], 16)

                    load(Item(0, 0, E1, 4))
                    load(Item(0, 1, E1, 4))

                    def step(e):
                        if (e + 2).real():
                            sp.wait_ge(s["x_mm"], e.count(1, 1))
                            sp.sem_inc(s["sp_turns"], 1)
                            load(e + 2)
                        if (e + 4).real():
                            sp.wait_ge(s["up"], e.count(2, 2))
                            sp.sem_inc(s["sp_turns"], 1)
                            load_w(nc, sp, a, g, e + 4, 1)
                        if (e - 1).real():
                            n = e - 1
                            sp.wait_ge(s["down_copy"], n.count(1, 1))
                            sp.sem_inc(s["sp_turns"], 1)
                            sp.dma_start(g.made1[n.rows(C1), :], y[n.parity][:, :]).then_inc(s_out[n.parity], 16)
                            if (n + 4).real():
                                load_w(nc, sp, a, g, n + 4, 2)

                    steps(sp, step, E1, 1, E1 - 5, E1 + 1, 4)
                    for p in range(2):
                        sp.wait_ge(s_out[p], 16 * E1 // 2)

                @block.scalar
                def _(act):
                    def step(e):
                        if e.real():
                            act.wait_ge(s["x_mm"], e.count(1, 1))
                            if (e - 2).real():
                                act.wait_ge(s["up"], (e - 2).count(2, 2))
                            nc.scalar.copy(xt[e.parity][:, :, :], bank[4 + e.parity][:, 0:2 * C1].rearrange("p (k t) -> p k t", k=2)).then_inc(s["x_copy"], 1)
                        if (e - 1).real():
                            n = e - 1
                            act.wait_ge(s["up"], n.count(2, 1))
                            if (n - 2).real():
                                act.wait_ge(s["down"], (n - 2).count(1, 1))
                            nc.scalar.activation(hid[n.parity][:, 0:KF // 2, :], bank[2 * n.parity][:, 0:4 * C1].rearrange("p (f t) -> p f t", f=KF // 2),
                                                 ACT.Relu).then_inc(s["hid_a"], 1)

                    steps(act, step, E1, 3, E1 - 2, E1 + 1, 4)

                @block.vector
                def _(dve):
                    def step(e):
                        if (e - 2).real():
                            n = e - 2
                            dve.wait_ge(s["down"], n.count(1, 1))
                            if (n - 2).real():
                                dve.wait_ge(s_out[n.parity], (n - 2).turn(16, 16))
                            nc.vector.tensor_copy(y[n.parity][:, :], bank[6 + n.parity][0:C1, 0:D]).then_inc(s["down_copy"], 1)
                        if (e - 1).real():
                            n = e - 1
                            dve.wait_ge(s["up"], n.count(2, 2))
                            if (n - 2).real():
                                dve.wait_ge(s["down"], (n - 2).count(1, 1))
                            nc.vector.tensor_scalar(hid[n.parity][:, KF // 2:KF, :], bank[2 * n.parity + 1][:, 0:4 * C1].rearrange("p (f t) -> p f t", f=KF // 2),
                                                    0.0, None, ALU.max).then_inc(s["hid_v"], 1)

                    steps(dve, step, E1, 4, E1 - 1, E1 + 2, 4)

                @block.tensor
                def _(pe):
                    def transpose_in(e):
                        pe.wait_ge(s_in[e.parity], e.turn(16, 16))
                        if (e - 2).real():
                            pe.wait_ge(s["x_copy"], (e - 2).count(1, 1))
                        for h in range(2):
                            last = nc.tensor.transpose(bank[4 + e.parity][:, h * C1:(h + 1) * C1], x_in[e.parity][:, h * P:(h + 1) * P], g.ident[0:C1, 0:C1])
                        last.then_inc(s["x_mm"], 1)

                    transpose_in(Item(0, 0, E1, 4))

                    def step(e):
                        if e.real():
                            pe.wait_ge(s["x_copy"], e.count(1, 1))
                            pe.wait_ge(g.s_ring1[e.quarter], e.turn(16, 16, 4))
                            if (e - 2).real():
                                pe.wait_ge(s["hid_a"], (e - 2).count(1, 1))
                                pe.wait_ge(s["hid_v"], (e - 2).count(1, 1))
                            for f in range(KF):
                                for k in range(2):
                                    last = nc.tensor.matmul(bank[2 * e.parity + f // 4][:, f % 4 * C1:(f % 4 + 1) * C1],
                                                            g.ring1[e.quarter][:, k, f * P:(f + 1) * P], xt[e.parity][:, k, :], start=(k == 0), stop=(k == 1))
                                if f % 4 == 3:
                                    last.then_inc(s["up"], 1)
                        if (e + 1).real():
                            transpose_in(e + 1)
                        if (e - 1).real():
                            n = e - 1
                            pe.wait_ge(g.s_ring2[n.quarter], n.turn(16, 16, 4))
                            pe.wait_ge(s["hid_a"], n.count(1, 1))
                            pe.wait_ge(s["hid_v"], n.count(1, 1))
                            if (n - 2).real():
                                pe.wait_ge(s["down_copy"], (n - 2).count(1, 1))
                            for f in range(KF):
                                last = nc.tensor.matmul(bank[6 + n.parity][0:C1, 0:D], hid[n.parity][:, f, :], g.ring2[n.quarter][:, f, :],
                                                        start=(f == 0), stop=(f == KF - 1))
                            last.then_inc(s["down"], 1)

                    steps(pe, step, E1, 3, E1 - 2, E1 + 1, 4)

        with ExitStack() as back:
            got = g.sb("got1", [T, B, D], F32, back)
            s_got = [g.sem(f"gathered{b}") for b in range(B)]
            block = nc.Block()
            with block:
                @block.gpsimd
                def _(pool):
                    for b in range(B):
                        pool.indirect_dma_start(out=got[:, b, :], out_offset=None, in_=g.made1,
                                                in_offset=bass.IndirectOffsetOnAxis(source_i[:, b:b + 1], 0)).then_inc(s_got[b], 16)

                @block.vector
                def _(dve):
                    for b in range(B):
                        dve.wait_ge(s_got[b], 16)
                        nc.vector.scalar_tensor_tensor(out=xs[:, b, :], in0=got[:, b, :], scalar=gate[:, b:b + 1], in1=xs[:, b, :],
                                                       op0=ALU.mult, op1=ALU.add).then_inc(s["step"], 1)

                @block.sync
                def _(sp):
                    for b in range(B):
                        sp.wait_ge(s["step"], 22 + b + 1)
                        sp.dma_start(out[b], xs[:, b, :]).then_inc(s["done"], 16)
                    sp.wait_ge(s["done"], 16 * B)


def kernel(**inputs):
    import numpy as np
    from concourse import bacc
    from concourse.bass_utils import run_bass_kernel_spmd

    nc = bacc.Bacc("TRN2", target_bir_lowering=False, num_devices=1)
    arrays, args = {}, {}
    for name, value in inputs.items():
        array = np.ascontiguousarray(value)
        arrays[f"in_{name}"] = array
        args[name] = nc.dram_tensor(f"in_{name}", array.shape, mybir.dt.from_np(array.dtype), kind="ExternalInput").ap()
    out = nc.dram_tensor("out", (B, T, D), F32, kind="ExternalOutput").ap()
    program(nc, args, out)
    return run_bass_kernel_spmd(nc, [arrays], core_ids=[0]).results[0]["out"]
```

```python
from contextlib import ExitStack

import concourse.bass as bass
from concourse import mybir

F32 = mybir.dt.float32
BF16 = mybir.dt.bfloat16
I32 = mybir.dt.int32
ALU = mybir.AluOpType
ACT = mybir.ActivationFunctionType
AX = mybir.AxisListType.X

B, T, D = 16, 112, 256
S = 375
H, DH = 16, 16
KC, NC = 125, 3
KV = S + T
EPS = 1e-5
TERMS_Q = (0, 0, 1, 0, 2, 1)
TERMS_K = (0, 1, 0, 2, 0, 1)
NT = len(TERMS_Q)
QK = NT * DH
ROWS = QK + 6
HG = 4
P = 128
E0, F0 = 8, 512
ROW_TILES = B * T // P
TILES = ROW_TILES + E0 - 1
E1, F1 = 16, 1024
C1 = (B * T) // E1
FAR = 1024.0


class Item:

    def __init__(self, i, c, n, unroll=2):
        self.i, self.c, self.n, self.unroll = i, c, n, unroll
        self.parity = c % 2
        self.quarter = c % 4

    def __sub__(self, k):
        return Item(self.i, self.c - k, self.n, self.unroll)

    def __add__(self, k):
        return Item(self.i, self.c + k, self.n, self.unroll)

    def number(self, per=1):
        return per * self.c if isinstance(self.i, int) else self.i * (self.unroll * per) + per * self.c

    def count(self, per=1, plus=0):
        const = per * self.c + plus
        assert const > (0 if self.looped() else -1)
        return const if isinstance(self.i, int) else self.i * (self.unroll * per) + const

    def looped(self):
        return not isinstance(self.i, int)

    def turn(self, per=16, plus=0, of=2):
        const = per * (self.c // of) + plus
        assert const > (0 if self.looped() else -1)
        return const if isinstance(self.i, int) else self.i * (self.unroll // of * per) + const

    def at(self):
        return bass.ds(self.number(), 1)

    def rows(self, size):
        return bass.ds(self.number(size), size)

    def real(self):
        return self.looped() or 0 <= self.c < self.n


def steps(engine, step, n, first, last, end, unroll=2):
    loops = (last - first + 1) // unroll
    for c in range(first):
        step(Item(0, c, n))
    with engine.Fori(0, loops) as i:
        for c in range(unroll):
            step(Item(i, first + c, n, unroll))
    for c in range(first + loops * unroll, end):
        step(Item(0, c, n))


def attention_steps(engine, step):
    steps(engine, step, B, 5, B - 2, B + 3)


class Shared:
    pass


def program(nc, a, out):
    with ExitStack() as ctx:
        g = Shared()
        g.nc = nc

        def sb(name, shape, dt=F32, where=ctx):
            return where.enter_context(nc.sbuf_tensor(name, shape, dt))

        def sem(name):
            handle = nc.alloc_semaphore(name=name)
            if g.phase_sems is not None:
                g.phase_sems.append(handle)
            return handle

        g.phase_sems = None

        def phase(run, *args):
            g.phase_sems = []
            run(*args)
            nc.all_engine_barrier()
            nc.clear_and_free_semaphores(g.phase_sems)
            nc.all_engine_barrier()
            g.phase_sems = None

        def dram(name, shape, dt=F32):
            return nc.dram_tensor(name, shape, dt, kind="Internal").ap()

        g.sb, g.sem, g.dram = sb, sem, dram
        g.psum = ctx.enter_context(nc.psum_tensor("psum", [P, 8, 512], F32))
        g.bank = [g.psum[:, k, :] for k in range(8)]
        g.xs = sb("xs", [T, B, D])
        g.ident = sb("ident", [P, P])
        g.ident16 = sb("ident16", [P, P], BF16)
        g.neg_half = sb("neg_half", [P, 1])
        g.eps = sb("eps", [P, 1])
        g.ct_dram = dram("ct_dram", (B, P, 2, S))
        g.sorted0 = dram("sorted0", (TILES * P, D))
        g.made0 = dram("made0", (TILES * P, D))
        g.sorted1 = dram("sorted1", (2 * E1 * C1, D))
        g.made1 = dram("made1", (E1 * C1, D))
        g.s_w0 = sem("experts0_loaded")
        g.s_zero = sem("sorted_cleared")
        with ExitStack() as layer0:
            g.w1 = sb("w1", [P, E0, 2, F0], F32, layer0)
            g.w2 = sb("w2", [P, E0, F0 // P, D], F32, layer0)
            g.b1 = sb("b1", [P, E0, F0 // P], F32, layer0)
            phase(attention0, nc, a, g)
            phase(ffn0, nc, a, g)
        with ExitStack() as layer1:
            g.ring1 = [sb(f"ring1_{k}", [P, 2, F1], F32, layer1) for k in range(4)]
            g.ring2 = [sb(f"ring2_{k}", [P, F1 // P, D], F32, layer1) for k in range(4)]
            g.s_ring1 = [sem(f"w1_loaded{k}") for k in range(4)]
            g.s_ring2 = [sem(f"w2_loaded{k}") for k in range(4)]
            g.rows1_buffer = sb("rows1", [T, B, D], F32, layer1)
            phase(attention1, nc, a, g)
            phase(ffn1, nc, a, out, g)


def attention0(nc, a, g_):
    sem, dram, psum, bank, xs, ident, ident16 = g_.sem, g_.dram, g_.psum, g_.bank, g_.xs, g_.ident, g_.ident16
    neg_half, eps = g_.neg_half, g_.eps
    with ExitStack() as phase:
        def sb(name, shape, dt=F32):
            return g_.sb(name, shape, dt, phase)

        w_x = sb("w_x", [P, 2, 3 * D])
        w_aux = sb("w_aux", [P, 2, 2 * D])
        wo = sb("wo", [P, 2, D])
        bias_t = sb("bias_t", [P, 6])
        g_wide = sb("g_wide", [KC, H])
        inv_gate = sb("inv_gate", [KC, 2, H])
        gate = sb("gate", [KC, 2, H])
        bv = sb("bv", [T, 2, D])
        bv_mix = sb("bv_mix", [T, D])
        bv_t = sb("bv_t", [P, 2, T])
        bo_wide = sb("bo_wide", [T, D])
        sides = sb("sides", [ROWS, KV], BF16)
        clear = sb("clear", [P, D])
        c_wide = sb("c_wide", [T, D])
        ctx_in = [sb(f"ctx_in{p}", [KC, NC, D]) for p in range(2)]
        ln_stats = sb("ln_stats", [T, 6])
        ln_mv = sb("ln_mv", [T, 2])
        ln_rstd = sb("ln_rstd", [T, 2])
        xn = [sb(f"xn{p}", [T, D]) for p in range(2)]
        xt = [sb(f"xt{p}", [P, 2, T]) for p in range(2)]
        ct = [sb(f"ct{p}", [P, 2, S]) for p in range(2)]
        parts = [sb(f"parts{p}", [P, 3, 2, KV + T], BF16) for p in range(2)]
        rest = sb("rest", [P, 2, KV + T])
        k_stack = [sb(f"k_stack{p}", [ROWS, H, KV], BF16) for p in range(2)]
        q_stack = [sb(f"q_stack{p}", [ROWS, H, T], BF16) for p in range(2)]
        v = [sb(f"v{p}", [KC, NC + 1, H, 2 * DH]) for p in range(2)]
        neg_max = sb("neg_max", [T, 2, H])
        max_rest = sb("max_rest", [T, 2, H])
        max_parts = sb("max_parts", [T, 2, 3, H], BF16)
        mt = sb("mt", [QK, T], BF16)
        probs = [sb(f"probs{k}", [KC, 4, T]) for k in range(4)]
        pv = [sb(f"pv{u}", [P, 2, 2, T]) for u in range(2)]
        inv_sum = [sb(f"inv_sum{u}", [T, H]) for u in range(2)]
        normed = sb("normed", [T, 2, 2, P // 2])
        mixed_rows = sb("mixed_rows", [T, 2, P])
        mixed = sb("mixed", [P, 2, T])

        parts_dram = [dram(f"parts_dram{p}", (6, P, KV + T), BF16) for p in range(2)]
        max_dram = [dram(f"max_dram{p}", (QK, T), BF16) for p in range(2)]

        s = {n: sem(n) for n in """consts zeroed w_loaded x0_loaded x1_loaded x2_loaded bias_loaded out_loaded sides_made sides_ready
            g_limit g_exp gate_step inv_gate_ready bv_mix bv_mm bv_t c_mm c_ready
            ln_stats_ready ln_mv_ready ln_eps_ready ln_rstd_ready xn_ready xc_ready
            xt_mm ct_mm xt_ready ct_ready v01_mm v23_mm v_ready qk_mm ka0_mm ka1_mm
            high_done rest_done mid_done low_done scored max_done msplit mt_mm mt_ready
            logits_mm exp_done pv_done pv_out turned_mm inverted scaled mixed_made mixed_mm mixed_ready wo_mm x1_ready
            dve_turns pool_turns sp_turns done""".split()}
        s_spill = [sem(f"ct_spilled{p}") for p in range(2)]
        s_ctx = [sem(f"ctx_loaded{p}") for p in range(2)]
        s_parts = [sem(f"parts_written{p}") for p in range(2)]
        s_stack = [sem(f"stack_ready{p}") for p in range(2)]
        s_mw = [sem(f"max_written{p}") for p in range(2)]
        s_mr = [sem(f"max_ready{p}") for p in range(2)]
        block = phase.enter_context(nc.Block())

        @block.sync
        def _(sp):
            sp.dma_start(xs[:, 0, :], a["x"][0]).then_inc(s["x0_loaded"], 16)
            sp.dma_start(ctx_in[0][:, :, :], a["ctx_1024"][0].rearrange("(c k) d -> k c d", k=KC)).then_inc(s_ctx[0], 16)
            sp.dma_start(w_x[:, :, :], a["L0_xattn_Wqkv"].rearrange("(a p) n -> p a n", p=P)).then_inc(s["w_loaded"], 16)
            sp.dma_start(w_aux[:, :, :], a["L0_xattn_Wqkv_aux"][:, D:3 * D].rearrange("(a p) n -> p a n", p=P)).then_inc(s["w_loaded"], 16)
            for k in range(4):
                src = a["L0_xattn_bqkv"][k * P:(k + 1) * P].rearrange("(p o) -> p o", o=1)
                sp.dma_start(bias_t[:, k:k + 1], src).then_inc(s["bias_loaded"], 16)
            for k in range(2):
                src = a["L0_xattn_bqkv_aux"][D + k * P:D + (k + 1) * P].rearrange("(p o) -> p o", o=1)
                sp.dma_start(bias_t[:, 4 + k:5 + k], src).then_inc(s["bias_loaded"], 16)
            sp.dma_start(xs[:, 1, :], a["x"][1]).then_inc(s["x1_loaded"], 16)
            sp.dma_start(xs[:, 2:B, :], a["x"][2:B].rearrange("b t d -> t b d")).then_inc(s["x2_loaded"], 16)
            g_row = a["L0_xattn_g"].rearrange("(o h) -> o h", o=1)
            sp.dma_start(g_wide[:, :], g_row.broadcast_to((KC, H))).then_inc(s["out_loaded"], 16)

            def load_output():
                bo = a["L0_xattn_bo"].rearrange("(o n) -> o n", o=1)
                sp.dma_start(wo[:, :, :], a["L0_xattn_Wo"].rearrange("(a p) n -> p a n", p=P)).then_inc(s["out_loaded"], 16)
                sp.dma_start(bo_wide[:, :], bo.broadcast_to((T, D))).then_inc(s["out_loaded"], 16)
                for o, name in enumerate(("L0_xattn_bqkv", "L0_xattn_bqkv_aux")):
                    row = a[name][2 * D:3 * D].rearrange("(o n) -> o n", o=1)
                    sp.dma_start(bv[:, o, :], row.broadcast_to((T, D))).then_inc(s["out_loaded"], 16)

            def load_experts(experts):
                for e in experts:
                    sp.dma_start(g_.w1[:, e, :, :], a["L0_ffn_W1"][e].rearrange("(k p) f -> p k f", p=P)).then_inc(g_.s_w0, 16)
                    sp.dma_start(g_.w2[:, e, :, :], a["L0_ffn_W2"][e].rearrange("(k p) d -> p k d", p=P)).then_inc(g_.s_w0, 16)
                    for f in range(F0 // P):
                        sp.dma_start(g_.b1[:, e, f:f + 1], a["L0_ffn_b1"][e, f * P:(f + 1) * P].rearrange("(p o) -> p o", o=1)).then_inc(g_.s_w0, 16)

            def clear_rows(rows, lo, hi):
                for k in range(lo, hi):
                    sp.dma_start(rows[k * P:(k + 1) * P, :], clear[:, :]).then_inc(g_.s_zero, 16)

            def step(b):
                if (b + 1).real():
                    if not isinstance(b.i, int) or b.c >= 1:
                        sp.wait_ge(s["ct_mm"], b.count())
                        sp.sem_inc(s["sp_turns"], 1)
                    src = a["ctx_1024"][(b + 1).at()].rearrange("o (c k) d -> k (o c) d", k=KC)
                    sp.dma_start(ctx_in[(b + 1).parity][:, :, :], src).then_inc(s_ctx[(b + 1).parity], 16)
                if (b - 1).real():
                    n = b - 1
                    sp.wait_ge(s_parts[n.parity], n.turn(16, 16))
                    sp.sem_inc(s["sp_turns"], 1)
                    if (b - 3).real():
                        sp.wait_ge(s["pv_done"], (b - 3).count(16, 16))
                    src = parts_dram[n.parity].rearrange("(t a) p n -> t (a p) n", a=2)
                    for t in range(NT):
                        rows = slice(DH * t, DH * t + DH)
                        k_src = src[TERMS_K[t]][:, 0:KV].rearrange("(h d) n -> d h n", d=DH)
                        q_src = src[TERMS_Q[t]][:, KV:KV + T].rearrange("(h d) n -> d h n", d=DH)
                        sp.dma_start(k_stack[n.parity][rows, :, :], k_src).then_inc(s_stack[n.parity], 16)
                        sp.dma_start(q_stack[n.parity][rows, :, :], q_src).then_inc(s_stack[n.parity], 16)
                if (b - 2).real():
                    n = b - 2
                    sp.wait_ge(s["mt_ready"], n.count(1, 1))
                    sp.dma_start(max_dram[n.parity], mt[:, :]).then_inc(s_mw[n.parity], 16)
                    sp.wait_ge(s_mw[n.parity], n.turn(16, 16))
                    sp.dma_start(q_stack[n.parity][QK:ROWS, :, :],
                                 max_dram[n.parity].rearrange("(k h) n -> k h n", h=H)).then_inc(s_mr[n.parity], 16)
                if b.real():
                    sp.wait_ge(s["ct_ready"], b.count(2, 2))
                    spill = g_.ct_dram[b.at()].rearrange("o p a n -> p (o a) n")
                    sp.sem_inc(s["sp_turns"], 1)
                    sp.dma_start(spill, ct[b.parity][:, :, :]).then_inc(s_spill[b.parity], 16)
                    sp.wait_ge(s["low_done"], b.count(2, 2))
                    sp.dma_start(parts_dram[b.parity].rearrange("g p n -> p g n"),
                                 parts[b.parity][:, :, :, :].rearrange("p t a n -> p (t a) n")).then_inc(s_parts[b.parity], 16)
                if b.looped():
                    return
                if b.c == 0:
                    load_output()
                if 1 <= b.c <= 4:
                    load_experts(range(2 * b.c - 2, 2 * b.c))
                if b.c == B - 1:
                    sp.wait_ge(s["zeroed"], 1)
                    clear_rows(g_.sorted0, 0, TILES)
                if b.c == B:
                    clear_rows(g_.sorted1, 0, E1 * C1 // P)

            attention_steps(sp, step)
            for p in range(2):
                sp.wait_ge(s_spill[p], 16 * B // 2)
            sp.wait_ge(g_.s_w0, 16 * E0 * 6)
            sp.wait_ge(g_.s_zero, 16 * (TILES + E1 * C1 // P))

        @block.gpsimd
        def _(pool):
            def ln(b):
                pool.wait_ge(s["ln_mv_ready"], b.count(1, 1))
                nc.gpsimd.tensor_tensor(ln_rstd[:, 0:1], ln_mv[:, 1:2], eps[0:T, :], ALU.add).then_inc(s["ln_eps_ready"], 1)
                pool.wait_ge(s["ln_eps_ready"], b.count(1, 1))
                nc.gpsimd.tensor_tensor(ln_rstd[:, 1:2], ln_rstd[:, 0:1], neg_half[0:T, :], ALU.pow).then_inc(s["ln_rstd_ready"], 1)

            pool.memset(neg_half[:, :], -0.5).then_inc(s["consts"], 1)
            pool.memset(eps[:, :], EPS).then_inc(s["consts"], 1)
            pool.memset(ident[:, :], 0.0).then_inc(s["consts"], 1)
            pool.memset(ident16[:, :], 0.0).then_inc(s["consts"], 1)
            pool.wait_ge(s["consts"], 4)
            for m in (ident, ident16):
                pool.affine_select(out=m[:, :], in_=m[:, :], compare_op=ALU.not_equal, fill=1.0, base=0,
                                   pattern=[[-1, P]], channel_multiplier=1).then_inc(s["consts"], 1)
            ln(Item(0, 0, B))
            pool.memset(clear[:, :], 0.0).then_inc(s["zeroed"], 1)
            pool.wait_ge(s["zeroed"], 1)
            own, other = sides[QK:ROWS, S:KV], sides[QK:ROWS, 0:S]
            pool.memset(sides[QK:ROWS, :], 0.0).then_inc(s["sides_made"], 1)
            pool.wait_ge(s["sides_made"], 1)
            pool.affine_select(out=other, in_=other, compare_op=ALU.is_ge, fill=1.0, base=-3,
                               pattern=[[0, S]], channel_multiplier=1).then_inc(s["sides_made"], 1)
            pool.affine_select(out=own, in_=own, compare_op=ALU.is_ge, fill=1.0, base=2,
                               pattern=[[0, T]], channel_multiplier=-1).then_inc(s["sides_made"], 1)
            pool.wait_ge(s["sides_made"], 3)

            def add_c(b):
                pool.wait_ge(s["xn_ready"], b.count(1, 1))
                row = xs[:, b.at(), :].rearrange("t o d -> t (o d)")
                nc.gpsimd.tensor_tensor(row, row, c_wide[:, :], ALU.add).then_inc(s["xc_ready"], 1)

            def step(b):
                if (b + 1).real():
                    ln(b + 1)
                if (b - 2).real():
                    if not b.looped() and b.c == 2:
                        pool.wait_ge(s["c_ready"], 1)
                    add_c(b - 2)
                if b.real():
                    for k, (lo, hi, need) in enumerate(((S, KV + T, 5), (0, S, 6))):
                        pool.wait_ge(s["rest_done"], b.count(6, need))
                        pool.sem_inc(s["pool_turns"], 1)
                        nc.gpsimd.tensor_copy(parts[b.parity][:, 1, :, lo:hi], rest[:, :, lo:hi]).then_inc(s["mid_done"], 1)
                        pool.wait_ge(s["mid_done"], b.count(2, k + 1))
                        nc.gpsimd.tensor_tensor(parts[b.parity][:, 2, :, lo:hi], rest[:, :, lo:hi],
                                                parts[b.parity][:, 1, :, lo:hi], ALU.subtract).then_inc(s["low_done"], 1)

            attention_steps(pool, step)

        @block.scalar
        def _(act):
            def mixed_out(n, u):
                act.wait_ge(s["mixed_mm"], n.count(2, u + 1))
                if (n - 1).real():
                    act.wait_ge(s["wo_mm"], (n - 1).count(1, 1))
                nc.scalar.copy(mixed[:, u, :], bank[6 + u][:, 0:T]).then_inc(s["mixed_ready"], 1)

            def high_k(b, h):
                nc.scalar.activation(parts[b.parity][:, 0, h, 0:S], bank[(0, 3)[h]][:, 0:S], ACT.Identity,
                                     bias=bias_t[:, 4 + h:5 + h]).then_inc(s["high_done"], 1)

            def step(b):
                if (b - 3).real():
                    n = b - 3
                    for k in range(16):
                        keys = T if k % 4 == 0 else KC
                        act.wait_ge(s["logits_mm"], n.count(16, k + 1))
                        act.wait_ge(s["pv_done"], n.count(16, max(k - 3, 0)))
                        src = bank[4 + k % 2][0:keys, 0:4 * T].rearrange("p (j q) -> p j q", j=4)
                        nc.scalar.activation(probs[k % 4][0:keys, :, :], src, ACT.Exp, scale=DH ** -0.5).then_inc(s["exp_done"], 1)
                        if k in (10, 15):
                            u = 0 if k == 10 else 1
                            act.wait_ge(s["pv_done"], n.count(16, 8 * (u + 1)))
                            if (n - 1).real():
                                act.wait_ge(s["turned_mm"], (n - 1).count(2, u + 1))
                            nc.scalar.copy(pv[u][:, :, :, :].rearrange("p g s t -> p (g s t)"), bank[6 + u][:, 0:4 * T]).then_inc(s["pv_out"], 1)
                    mixed_out(n, 0)
                if b.real():
                    act.wait_ge(s["xt_mm"], b.count(1, 1))
                    if (b - 2).real():
                        act.wait_ge(s["v23_mm"], (b - 2).count(1, 1))
                    nc.scalar.copy(xt[b.parity][:, :, :], bank[0][:, 0:2 * T].rearrange("p (a t) -> p a t", a=2)).then_inc(s["xt_ready"], 1)
                    act.wait_ge(s["ct_mm"], b.count(1, 1))
                    if (b - 2).real():
                        act.wait_ge(s_spill[b.parity], (b - 2).turn(16, 16))
                    for h in range(2):
                        nc.scalar.copy(ct[b.parity][:, h, :], bank[1 + h][:, 0:S]).then_inc(s["ct_ready"], 1)
                if (b - 2).real():
                    n = b - 2
                    act.wait_ge(s["mt_mm"], n.count(1, 1))
                    if (b - 3).real():
                        act.wait_ge(s_mw[(b - 3).parity], (b - 3).turn(16, 16))
                    nc.scalar.copy(mt[:, :], bank[3][0:QK, 256:256 + T // 2].bitcast(BF16)).then_inc(s["mt_ready"], 1)
                if (b - 1).real():
                    n = b - 1
                    act.wait_ge(s["v01_mm"], n.count(1, 1))
                    nc.scalar.copy(v[n.parity][:, 0:2, :, 0:DH],
                                   bank[0][0:KC, :].rearrange("p (c h d) -> p c h d", c=2, h=H)).then_inc(s["v_ready"], 1)
                    act.wait_ge(s["v23_mm"], n.count(1, 1))
                    nc.scalar.copy(v[n.parity][:, 2, :, 0:DH],
                                   bank[1][0:KC, 0:D].rearrange("p (h d) -> p h d", h=H)).then_inc(s["v_ready"], 1)
                    nc.scalar.copy(v[n.parity][0:T, 3, :, 0:DH],
                                   bank[1][0:T, D:2 * D].rearrange("p (h d) -> p h d", h=H)).then_inc(s["v_ready"], 1)
                if (b - 3).real():
                    mixed_out(b - 3, 1)
                if b.real():
                    if (b - 2).real():
                        act.wait_ge(s_parts[b.parity], (b - 2).turn(16, 16))
                    if not b.looped() and b.c == 0:
                        act.wait_ge(s["bias_loaded"], 16 * 6)
                    act.wait_ge(s["ka1_mm"], b.count(1, 1))
                    high_k(b, 1)
                    act.wait_ge(s["qk_mm"], b.count(1, 1))
                    for h in range(2):
                        for o, col in enumerate((S, KV)):
                            nc.scalar.activation(parts[b.parity][:, 0, h, col:col + T], bank[2][:, (2 * h + o) * T:(2 * h + o + 1) * T],
                                                 ACT.Identity, bias=bias_t[:, (2, 0)[o] + h:(2, 0)[o] + h + 1]).then_inc(s["high_done"], 1)
                    act.wait_ge(s["ka0_mm"], b.count(1, 1))
                    high_k(b, 0)
                    if not b.looped() and b.c == 0:
                        act.wait_ge(s["g_limit"], 1)
                        for o, sign in enumerate((1.0, -1.0)):
                            nc.scalar.activation(inv_gate[:, o, :], g_wide[:, :], ACT.Exp, scale=sign).then_inc(s["g_exp"], 1)
                        act.wait_ge(s["bv_mm"], 1)
                        nc.scalar.copy(bv_t[:, :, :], bank[4][:, 0:2 * T].rearrange("p (a t) -> p a t", a=2)).then_inc(s["bv_t"], 1)
                        act.wait_ge(s["sides_made"], 3)
                        for p in range(2):
                            wide = sides[QK:ROWS, :].rearrange("k (o n) -> k o n", o=1).broadcast_to((ROWS - QK, H, KV))
                            nc.scalar.copy(k_stack[p][QK:ROWS, :, :], wide).then_inc(s["sides_ready"], 1)

            attention_steps(act, step)

        @block.vector
        def _(dve):
            def ln(b):
                if not b.looped() and b.c <= 2:
                    dve.wait_ge(s[f"x{b.c}_loaded"], 16)
                row = xs[:, b.at(), :].rearrange("t o d -> t (o d)")
                nc.vector.bn_stats(ln_stats[:, :], row).then_inc(s["ln_stats_ready"], 1)
                dve.wait_ge(s["ln_stats_ready"], b.count(1, 1))
                dve.sem_inc(s["dve_turns"], 1)
                nc.vector.bn_aggr(ln_mv[:, :], ln_stats[:, :]).then_inc(s["ln_mv_ready"], 1)
                dve.wait_ge(s["ln_rstd_ready"], b.count(1, 1))
                if (b - 2).real():
                    dve.wait_ge(s["xt_mm"], (b - 2).count(1, 1))
                nc.vector.tensor_scalar(xn[b.parity][:, :], row, ln_mv[:, 0:1], ln_rstd[:, 1:2],
                                        ALU.subtract, ALU.mult).then_inc(s["xn_ready"], 1)

            ln(Item(0, 0, B))

            def gates():
                dve.wait_ge(s["out_loaded"], 16 * 5)
                nc.vector.tensor_scalar(g_wide[:, :], g_wide[:, :], -80.0, 80.0, ALU.max, ALU.min).then_inc(s["g_limit"], 1)
                dve.wait_ge(s["g_exp"], 2)
                nc.vector.tensor_scalar(inv_gate[:, :, :], inv_gate[:, :, :], 1.0, None, ALU.add).then_inc(s["inv_gate_ready"], 1)
                dve.wait_ge(s["inv_gate_ready"], 1)
                nc.vector.reciprocal(gate[:, :, :], inv_gate[:, :, :]).then_inc(s["gate_step"], 1)
                dve.wait_ge(s["gate_step"], 1)
                heads = "t s (h d) -> t (s h) d"
                wide = gate[0:T, :, :].rearrange("t s (h o) -> t (s h) o", o=1).broadcast_to((T, 2 * H, DH))
                nc.vector.tensor_tensor(bv[:, :, :].rearrange(heads, h=H), bv[:, :, :].rearrange(heads, h=H), wide, ALU.mult).then_inc(s["gate_step"], 1)
                dve.wait_ge(s["gate_step"], 2)
                nc.vector.tensor_tensor(bv_mix[:, :], bv[:, 0, :], bv[:, 1, :], ALU.add).then_inc(s["bv_mix"], 1)
                for p in range(2):
                    for c in range(NC + 1):
                        o = 0 if c == NC else 1
                        nc.vector.tensor_copy(v[p][:, c, :, DH:2 * DH], inv_gate[:, o, :].rearrange("k (h o) -> k h o", o=1).broadcast_to((KC, H, DH))).then_inc(s["inv_gate_ready"], 1)

            def normalise(n, u):
                dve.wait_ge(s["turned_mm"], n.count(2, u + 1))
                if (n - 1).real():
                    dve.wait_ge(s["mixed_mm"], n.count(2))
                dve.sem_inc(s["dve_turns"], 1)
                turned = bank[6 + u][0:T, :].rearrange("t (k d) -> t k d", k=H)
                nc.vector.reciprocal(inv_sum[u][:, :].rearrange("t (k o) -> t k o", o=1), turned[:, :, DH:DH + 1]).then_inc(s["inverted"], 1)
                dve.wait_ge(s["inverted"], n.count(2, u + 1))
                nc.vector.tensor_tensor(normed[:, :, :, :].rearrange("t g s (j d) -> t (g s j) d", d=DH), turned[:, :, 0:DH],
                                        inv_sum[u][:, :].rearrange("t (k o) -> t k o", o=1).broadcast_to((T, H, DH)), ALU.mult).then_inc(s["scaled"], 1)
                dve.wait_ge(s["scaled"], n.count(2, u + 1))
                nc.vector.tensor_tensor(mixed_rows[:, u, :].rearrange("t (g d) -> t g d", g=2), normed[:, :, 0, :], normed[:, :, 1, :],
                                        ALU.add).then_inc(s["mixed_made"], 1)

            def rest_k(b, h):
                nc.vector.scalar_tensor_tensor(out=rest[:, h, 0:S], in0=bank[(0, 3)[h]][:, 0:S], scalar=bias_t[:, 4 + h:5 + h],
                                               in1=parts[b.parity][:, 0, h, 0:S], op0=ALU.add, op1=ALU.subtract).then_inc(s["rest_done"], 1)

            def rest_qk(b):
                for h in range(2):
                    for o, col in enumerate((S, KV)):
                        nc.vector.scalar_tensor_tensor(out=rest[:, h, col:col + T], in0=bank[2][:, (2 * h + o) * T:(2 * h + o + 1) * T],
                                                       scalar=bias_t[:, (2, 0)[o] + h:(2, 0)[o] + h + 1], in1=parts[b.parity][:, 0, h, col:col + T],
                                                       op0=ALU.add, op1=ALU.subtract).then_inc(s["rest_done"], 1)

            def step(b):
                for k in range(8):
                    if (b - 2).real():
                        n = b - 2
                        dve.wait_ge(s["scored"], n.count(8, k + 1))
                        if k == 0 and (n - 1).real():
                            dve.wait_ge(s["msplit"], n.count(4))
                        pair, h = 2 - 2 * (k % 2), 2 * k
                        nc.vector.tensor_reduce(neg_max[:, 0, h:h + 2], psum[0:T, pair:pair + 2, 0:S], AX, ALU.max, negate=True)
                        nc.vector.tensor_reduce(neg_max[:, 1, h:h + 2], psum[0:T, pair:pair + 2, S:KV], AX, ALU.max, negate=True).then_inc(s["max_done"], 1)
                    if (b - 3).real():
                        if k == 6:
                            normalise(b - 3, 0)
                if (b - 2).real():
                    n = b - 2
                    dve.wait_ge(s["max_done"], n.count(8, 8))
                    if (n - 1).real():
                        dve.wait_ge(s["mt_mm"], n.count())
                    nc.vector.tensor_copy(max_parts[:, :, 0, :], neg_max[:, :, :]).then_inc(s["msplit"], 1)
                    dve.wait_ge(s["msplit"], n.count(4, 1))
                    nc.vector.tensor_tensor(max_rest[:, :, :], neg_max[:, :, :], max_parts[:, :, 0, :], ALU.subtract).then_inc(s["msplit"], 1)
                    dve.wait_ge(s["msplit"], n.count(4, 2))
                    nc.vector.tensor_copy(max_parts[:, :, 1, :], max_rest[:, :, :]).then_inc(s["msplit"], 1)
                    dve.wait_ge(s["msplit"], n.count(4, 3))
                    nc.vector.tensor_tensor(max_parts[:, :, 2, :], max_rest[:, :, :], max_parts[:, :, 1, :], ALU.subtract).then_inc(s["msplit"], 1)
                if (b - 3).real():
                    normalise(b - 3, 1)
                if (b + 1).real():
                    ln(b + 1)
                if b.real():
                    if (b - 1).real():
                        dve.wait_ge(s["low_done"], b.count(2))
                    for h in (1, 0):
                        if h == 1:
                            dve.wait_ge(s["high_done"], b.count(6, 1))
                        else:
                            dve.wait_ge(s["high_done"], b.count(6, 6))
                        rest_k(b, h)
                        if h == 1:
                            dve.wait_ge(s["high_done"], b.count(6, 5))
                            rest_qk(b)
                if (b - 3).real():
                    n = b - 3
                    dve.wait_ge(s["wo_mm"], n.count(1, 1))
                    dve.wait_ge(s["xc_ready"], n.count(1, 1))
                    row = xs[:, n.at(), :].rearrange("t o d -> t (o d)")
                    nc.vector.tensor_tensor(row, bank[1][0:T, 0:D], row, ALU.add).then_inc(s["x1_ready"], 1)
                if not b.looped() and b.c == 0:
                    gates()
                    dve.wait_ge(s["c_mm"], 1)
                    nc.vector.tensor_tensor(c_wide[:, :], bank[5][0:T, 0:D], bo_wide[:, :], ALU.add).then_inc(s["c_ready"], 1)

            attention_steps(dve, step)

        @block.tensor
        def _(pe):
            pe.wait_ge(s["consts"], 6)

            def constant_row():
                pe.wait_ge(s["bv_mix"], 1)
                for h in range(2):
                    last = nc.tensor.transpose(bank[4][:, h * T:(h + 1) * T], bv_mix[:, h * P:(h + 1) * P], ident[0:T, 0:T])
                last.then_inc(s["bv_mm"], 1)
                pe.wait_ge(s["bv_t"], 1)
                for h in range(2):
                    last = nc.tensor.matmul(bank[5][0:T, 0:D], bv_t[:, h, :], wo[:, h, :], start=(h == 0), stop=(h == 1))
                last.then_inc(s["c_mm"], 1)

            def turn(n, u):
                pe.wait_ge(s["pv_out"], n.count(2, u + 1))
                for g in range(2):
                    for o in range(2):
                        k = 2 * g + o
                        last = nc.tensor.transpose(bank[6 + u][0:T, k * P:(k + 1) * P], pv[u][:, g, o, :], ident[:, :])
                last.then_inc(s["turned_mm"], 1)

            def turn_back(n, u):
                pe.wait_ge(s["mixed_made"], n.count(2, u + 1))
                nc.tensor.transpose(bank[6 + u][:, 0:T], mixed_rows[:, u, :], ident[0:T, 0:T]).then_inc(s["mixed_mm"], 1)

            def max_scores(n, k):
                if k == 0:
                    pe.wait_ge(s_stack[n.parity], n.turn(192, 192))
                    if (n + 1).real():
                        pe.wait_ge(s["rest_done"], n.count(6, 11))
                if k == 1:
                    if (n + 1).real():
                        pe.wait_ge(s["rest_done"], n.count(6, 12))
                    pe.wait_ge(s["v_ready"], n.count(3, 3))
                    if (n - 2).real():
                        pe.wait_ge(s["x1_ready"], (n - 2).count(1, 1))
                if k >= 2:
                    pe.wait_ge(s["max_done"], n.count(8, k - 1))
                for j in range(2):
                    h = 2 * k + j
                    last = nc.tensor.matmul(bank[2 - 2 * (k % 2) + j][0:T, 0:KV], q_stack[n.parity][0:QK, h, :],
                                            k_stack[n.parity][0:QK, h, :], start=True, stop=True)
                last.then_inc(s["scored"], 1)

            def logits(n, k):
                g, c = k // 4, k % 4
                if k >= 2:
                    pe.wait_ge(s["exp_done"], n.count(16, k - 1))
                lo, keys = (S, T) if c == 0 else ((c - 1) * KC, KC)
                for j in range(4):
                    h = 4 * g + j
                    last = nc.tensor.matmul(bank[4 + k % 2][0:keys, j * T:(j + 1) * T], k_stack[n.parity][:, h, lo:lo + keys],
                                            q_stack[n.parity][:, h, :], start=True, stop=True)
                last.then_inc(s["logits_mm"], 1)

            def values(n, k):
                g, c = k // 4, k % 4
                pe.wait_ge(s["exp_done"], n.count(16, k + 1))
                if k in (0, 8) and (n - 1).real():
                    pe.wait_ge(s["mixed_ready"], (n - 1).count(2, k // 8 + 1))
                keys, chunk, o = (T, 3, 0) if c == 0 else (KC, c - 1, 1)
                for j in range(4):
                    h = 4 * g + j
                    col = (2 * (g % 2) + o) * T
                    last = nc.tensor.matmul(bank[6 + g // 2][32 * j:32 * j + 32, col:col + T], v[n.parity][0:keys, chunk, h, :],
                                            probs[k % 4][0:keys, j, :], start=(c <= 1), stop=(c == 0 or c == 3))
                last.then_inc(s["pv_done"], 1)

            def keys_of(b, h):
                for a_ in range(2):
                    last = nc.tensor.matmul(bank[(0, 3)[h]][:, 0:S], w_aux[:, a_, h * P:(h + 1) * P], ct[b.parity][:, a_, :],
                                            start=(a_ == 0), stop=(a_ == 1))
                last.then_inc(s[f"ka{h}_mm"], 1)

            def step(b):
                if (b - 3).real():
                    n = b - 3
                    if not b.looped() and b.c == 3:
                        pe.wait_ge(s["c_ready"], 1)
                        pe.wait_ge(s["sides_ready"], 2)
                        pe.wait_ge(s["inv_gate_ready"], 9)
                    pe.wait_ge(s_mr[n.parity], n.turn(16, 16))
                for k in range(16):
                    if (b - 3).real():
                        logits(b - 3, k)
                    if (b - 2).real() and k % 2 == 0:
                        max_scores(b - 2, k // 2)
                    if (b - 3).real() and k >= 1:
                        values(b - 3, k - 1)
                        if k == 12:
                            turn(b - 3, 0)
                if (b - 3).real():
                    values(b - 3, 15)
                    turn_back(b - 3, 0)
                if b.real():
                    pe.wait_ge(s["xn_ready"], b.count(1, 1))
                    if (b - 2).real():
                        pe.wait_ge(s["max_done"], (b - 2).count(8, 8))
                    elif (b - 1).real():
                        pe.wait_ge(s["rest_done"], 6)
                    for h in range(2):
                        last = nc.tensor.transpose(bank[0][:, h * T:(h + 1) * T], xn[b.parity][:, h * P:(h + 1) * P], ident[0:T, 0:T])
                    last.then_inc(s["xt_mm"], 1)
                    pe.wait_ge(s_ctx[b.parity], b.turn(16, 16))
                    for h in range(2):
                        for c in range(NC):
                            last = nc.tensor.transpose(bank[1 + h][:, c * KC:(c + 1) * KC], ctx_in[b.parity][:, c, h * P:(h + 1) * P],
                                                       ident[0:KC, 0:KC])
                    last.then_inc(s["ct_mm"], 1)
                if (b - 2).real():
                    n = b - 2
                    pe.wait_ge(s["msplit"], n.count(4, 4))
                    pe.wait_ge(s["max_done"], n.count(8, 8))
                    nc.tensor.transpose(bank[3][0:QK, 256:256 + T // 2].bitcast(BF16), max_parts[:, :, :, :].rearrange("t s k h -> t (s k h)"),
                                        ident16[0:T, 0:T]).then_inc(s["mt_mm"], 1)
                if (b - 3).real():
                    turn(b - 3, 1)
                if (b - 1).real():
                    n = b - 1
                    if b.real():
                        pe.wait_ge(s["xt_ready"], b.count(1, 1))
                        pe.wait_ge(s["ct_ready"], b.count(2, 1))
                    else:
                        pe.wait_ge(s["max_done"], (b - 2).count(8, 8))
                    for c in range(2):
                        for h in range(2):
                            last = nc.tensor.matmul(bank[0][0:KC, c * D:(c + 1) * D], ct[n.parity][:, h, c * KC:(c + 1) * KC],
                                                    w_aux[:, h, D:2 * D], start=(h == 0), stop=(h == 1))
                    last.then_inc(s["v01_mm"], 1)
                    for h in range(2):
                        nc.tensor.matmul(bank[1][0:KC, 0:D], ct[n.parity][:, h, 2 * KC:3 * KC], w_aux[:, h, D:2 * D],
                                         start=(h == 0), stop=(h == 1))
                    for h in range(2):
                        last = nc.tensor.matmul(bank[1][0:T, D:2 * D], xt[n.parity][:, h, :], w_x[:, h, 2 * D:3 * D],
                                                start=(h == 0), stop=(h == 1))
                    last.then_inc(s["v23_mm"], 1)
                if (b - 3).real():
                    turn_back(b - 3, 1)
                if b.real():
                    pe.wait_ge(s["xt_ready"], b.count(1, 1))
                    pe.wait_ge(s["ct_ready"], b.count(2, 2))
                    if (b - 2).real():
                        pe.wait_ge(s["mt_ready"], (b - 2).count(1, 1))
                    if not b.looped() and b.c == 0:
                        pe.wait_ge(s["w_loaded"], 32)
                    keys_of(b, 1)
                    for h in range(2):
                        for o in range(2):
                            col = (1 - o) * D + h * P
                            for a_ in range(2):
                                last = nc.tensor.matmul(bank[2][:, (2 * h + o) * T:(2 * h + o + 1) * T], w_x[:, a_, col:col + P],
                                                        xt[b.parity][:, a_, :], start=(a_ == 0), stop=(a_ == 1))
                    last.then_inc(s["qk_mm"], 1)
                    if (b - 1).real():
                        pe.wait_ge(s["v_ready"], (b - 1).count(3, 1))
                    keys_of(b, 0)
                if (b - 3).real():
                    n = b - 3
                    if (b - 1).real():
                        pe.wait_ge(s["v_ready"], (b - 1).count(3, 3))
                    pe.wait_ge(s["mixed_ready"], n.count(2, 2))
                    for h in range(2):
                        last = nc.tensor.matmul(bank[1][0:T, 0:D], mixed[:, h, :], wo[:, h, :], start=(h == 0), stop=(h == 1))
                    last.then_inc(s["wo_mm"], 1)
                if not b.looped() and b.c == 0:
                    constant_row()

            attention_steps(pe, step)


def routing(nc, g, phase, experts, tag):
    def sb(name, shape, dt=F32):
        return g.sb(f"{name}{tag}", shape, dt, phase)

    r = Shared()
    r.logits = sb("logits", [T, B, experts])
    r.best = sb("best", [T, B])
    r.cand = sb("cand", [T, B, experts])
    r.which = sb("which", [T, B])
    r.iota_e = sb("iota_e", [T, experts])
    r.onehot = sb("onehot", [T, experts, B])
    r.before = sb("before", [T, T])
    r.ones = sb("ones", [T, T])
    r.total = sb("total", [T, experts, B])
    r.carry = sb("carry", [T, experts, B])
    r.upto = sb("upto", [T, experts, B])
    r.rank = sb("rank", [T, experts, B])
    r.place = sb("place", [T, B])
    r.place_i = sb("place_i", [T, B], I32)
    r.row_bank, r.total_bank = g.bank[0][0:T, 0:experts * B], g.bank[1][0:T, 0:experts * B]

    def constants(pool, made):
        nc.gpsimd.iota(r.iota_e[:, :], [[1, experts]], base=0, channel_multiplier=0,
                       allow_small_or_imprecise_dtypes=True).then_inc(made, 1)
        nc.gpsimd.memset(r.ones[:, :], 1.0).then_inc(made, 1)
        nc.gpsimd.memset(r.before[:, :], 1.0).then_inc(made, 1)
        nc.gpsimd.memset(r.carry[:, :, :], 1.0).then_inc(made, 1)
        pool.wait_ge(made, 4)
        nc.gpsimd.affine_select(out=r.before[:, :], in_=r.before[:, :], compare_op=ALU.is_gt, fill=0.0, base=0,
                                pattern=[[1, T]], channel_multiplier=-1).then_inc(made, 1)
        pool.wait_ge(made, 5)
        nc.gpsimd.memset(r.carry[:, :, 0:1], 0.0).then_inc(made, 1)
        pool.wait_ge(made, 6)

    def choose(dve, step):
        wide = (T, B, experts)
        best = r.best[:, :].rearrange("t (b o) -> t b o", o=1).broadcast_to(wide)
        nc.vector.tensor_reduce(r.best[:, :], r.logits[:, :, :], AX, ALU.max).then_inc(step, 1)
        dve.wait_ge(step, 1)
        nc.vector.tensor_tensor(r.cand[:, :, :], r.logits[:, :, :], best, ALU.is_lt).then_inc(step, 1)
        dve.wait_ge(step, 2)
        numbers = r.iota_e[:, :].rearrange("t (o e) -> t o e", o=1).broadcast_to(wide)
        nc.vector.scalar_tensor_tensor(out=r.cand[:, :, :], in0=r.cand[:, :, :], scalar=FAR, in1=numbers,
                                       op0=ALU.mult, op1=ALU.add).then_inc(step, 1)
        dve.wait_ge(step, 3)
        nc.vector.tensor_reduce(r.which[:, :], r.cand[:, :, :], AX, ALU.min).then_inc(step, 1)
        dve.wait_ge(step, 4)
        nc.vector.tensor_tensor(r.onehot[:, :, :], r.iota_e[:, :].rearrange("t (e o) -> t e o", o=1).broadcast_to((T, experts, B)),
                                r.which[:, :].rearrange("t (o b) -> t o b", o=1).broadcast_to((T, experts, B)),
                                ALU.is_equal).then_inc(step, 1)

    def count_rows(pe, step, counted):
        pe.wait_ge(step, 5)
        flat = r.onehot[:, :, :].rearrange("t e b -> t (e b)")
        nc.tensor.matmul(r.row_bank, r.before[:, :], flat, start=True, stop=True).then_inc(counted, 1)
        nc.tensor.matmul(r.total_bank, r.ones[:, :], flat, start=True, stop=True).then_inc(counted, 1)

    def rank(dve, step, counted):
        dve.wait_ge(counted, 2)
        flat = "t e b -> t (e b)"
        nc.vector.tensor_copy(r.total[:, :, :].rearrange(flat), r.total_bank).then_inc(step, 1)
        dve.wait_ge(step, 6)
        nc.vector.tensor_tensor_scan(r.upto[:, :, :].rearrange(flat), r.carry[:, :, :].rearrange(flat),
                                     r.total[:, :, :].rearrange(flat), 0.0, ALU.mult, ALU.add).then_inc(step, 1)
        dve.wait_ge(step, 7)
        nc.vector.tensor_tensor(r.rank[:, :, :], r.upto[:, :, :], r.total[:, :, :], ALU.subtract).then_inc(step, 1)
        dve.wait_ge(step, 8)
        nc.vector.tensor_tensor(r.rank[:, :, :].rearrange(flat), r.row_bank, r.rank[:, :, :].rearrange(flat), ALU.add).then_inc(step, 1)
        dve.wait_ge(step, 9)

    def pick(dve, out, step, n):
        nc.vector.tensor_tensor(r.rank[:, :, :], r.rank[:, :, :], r.onehot[:, :, :], ALU.mult).then_inc(step, 1)
        dve.wait_ge(step, n + 1)
        nc.vector.tensor_reduce(out, r.rank[:, :, :].rearrange("t e b -> t b e"), AX, ALU.add).then_inc(step, 1)
        dve.wait_ge(step, n + 2)

    r.constants, r.choose, r.count_rows, r.rank_rows, r.pick = constants, choose, count_rows, rank, pick
    return r


def ffn0(nc, a, g):
    bank, xs = g.bank, g.xs
    K2 = F0 // P
    with ExitStack() as phase:
        def sb(name, shape, dt=F32):
            return g.sb(name, shape, dt, phase)

        def sems(names):
            return {n: g.sem("f0_" + n) for n in names.split()}

        wr = sb("wr", [P, 2, E0])
        br = sb("br", [T, E0])
        b2 = sb("b2", [P, E0, D])
        ln_stats = [sb(f"f0_stats{p}", [T, 6]) for p in range(2)]
        ln_mv = [sb(f"f0_mv{p}", [T, 2]) for p in range(2)]
        ln_rstd = [sb(f"f0_rstd{p}", [T, 2]) for p in range(2)]
        xn = [sb(f"f0_xn{p}", [T, D]) for p in range(2)]
        rows = sb("f0_rows", [T, B, D])
        xt = [sb(f"f0_xt{p}", [P, 2, T]) for p in range(2)]
        tile_no = sb("tile_no", [T, TILES])
        edges = sb("edges", [T, ROW_TILES])
        over = sb("over", [T, E0, ROW_TILES])
        tiles_of = sb("tiles_of", [T, E0])
        tiles_to = sb("tiles_to", [T, E0])
        starts = sb("starts", [T, E0])
        passed = sb("passed", [1, TILES, E0])
        owner = sb("owner", [1, TILES])
        owner_i = sb("owner_i", [1, TILES], I32)
        g.place0 = g.sb("place0", [T, B], I32, phase)
        s = sems("""loaded made stats mv eps rstd xn xt_mm xt row logits_mm logits step counted placed scattered
            in_free x_mm x_copy up up_copy back back_copy down down_copy gathered dve_turns sp_turns pool_turns act_turns x2""")
        s_in = [g.sem(f"f0_tile_loaded{p}") for p in range(2)]
        s_out = [g.sem(f"f0_tile_stored{p}") for p in range(2)]
        r = routing(nc, g, phase, E0, "_0")

        block = nc.Block()
        with block:
            @block.sync
            def _(sp):
                sp.dma_start(wr[:, :, :], a["L0_ffn_Wr"].rearrange("(k p) e -> p k e", p=P)).then_inc(s["loaded"], 16)
                sp.dma_start(br[:, :], a["L0_ffn_br"].rearrange("(o e) -> o e", o=1).broadcast_to((T, E0))).then_inc(s["loaded"], 16)
                sp.dma_start(b2[:, :, :], a["L0_ffn_b2"].rearrange("(o e) d -> o e d", o=1).broadcast_to((P, E0, D))).then_inc(s["loaded"], 16)
                sp.wait_ge(s["loaded"], 48)

            @block.gpsimd
            def _(pool):
                r.constants(pool, s["made"])
                nc.gpsimd.iota(tile_no[:, :], [[1, TILES]], base=0, channel_multiplier=0,
                               allow_small_or_imprecise_dtypes=True).then_inc(s["made"], 1)
                nc.gpsimd.iota(edges[:, :], [[P, ROW_TILES]], base=0, channel_multiplier=0,
                               allow_small_or_imprecise_dtypes=True).then_inc(s["made"], 1)
                pool.wait_ge(s["made"], 8)

                def step(b):
                    if b.real():
                        pool.wait_ge(s["mv"], b.count(1, 1))
                        nc.gpsimd.tensor_tensor(ln_rstd[b.parity][:, 0:1], ln_mv[b.parity][:, 1:2], g.eps[0:T, :], ALU.add).then_inc(s["eps"], 1)
                        pool.wait_ge(s["eps"], b.count(1, 1))
                        nc.gpsimd.tensor_tensor(ln_rstd[b.parity][:, 1:2], ln_rstd[b.parity][:, 0:1], g.neg_half[0:T, :], ALU.pow).then_inc(s["rstd"], 1)

                steps(pool, step, B, 0, B - 1, B)
                pool.wait_ge(s["placed"], 1)
                pool.wait_ge(s["row"], B)
                for b in range(B):
                    pool.indirect_dma_start(out=g.sorted0, out_offset=bass.IndirectOffsetOnAxis(g.place0[:, b:b + 1], 0),
                                            in_=rows[:, b, :], in_offset=None).then_inc(s["scattered"], 16)
                pool.wait_ge(s["scattered"], 16 * B)

            @block.scalar
            def _(act):
                def step(b):
                    if b.real():
                        act.wait_ge(s["xn"], b.count(1, 1))
                        nc.scalar.copy(rows[:, b.at(), :].rearrange("t o d -> t (o d)"), xn[b.parity][:, :]).then_inc(s["row"], 1)
                        act.wait_ge(s["xt_mm"], b.count(1, 1))
                        if (b - 2).real():
                            act.wait_ge(s["logits_mm"], (b - 2).count(1, 1))
                        nc.scalar.copy(xt[b.parity][:, :, :], bank[2 + b.parity][:, 0:2 * T].rearrange("p (k t) -> p k t", k=2)).then_inc(s["xt"], 1)

                steps(act, step, B, 2, B - 1, B)

            @block.vector
            def _(dve):
                def step(b):
                    n = b
                    row = xs[:, n.at(), :].rearrange("t o d -> t (o d)")
                    if (n - 2).real():
                        dve.wait_ge(s["xt_mm"], (n - 2).count(1, 1))
                        dve.wait_ge(s["row"], (n - 2).count(1, 1))
                    nc.vector.bn_stats(ln_stats[n.parity][:, :], row).then_inc(s["stats"], 1)
                    dve.wait_ge(s["stats"], n.count(1, 1))
                    dve.sem_inc(s["dve_turns"], 1)
                    nc.vector.bn_aggr(ln_mv[n.parity][:, :], ln_stats[n.parity][:, :]).then_inc(s["mv"], 1)
                    dve.wait_ge(s["rstd"], n.count(1, 1))
                    nc.vector.tensor_scalar(xn[n.parity][:, :], row, ln_mv[n.parity][:, 0:1], ln_rstd[n.parity][:, 1:2],
                                            ALU.subtract, ALU.mult).then_inc(s["xn"], 1)

                steps(dve, step, B, 2, B - 1, B)
                dve.wait_ge(s["logits_mm"], B)
                dve.wait_ge(s["loaded"], 48)
                dve.wait_ge(s["made"], 8)
                nc.vector.tensor_tensor(r.logits[:, :, :], bank[4][0:T, 0:B * E0].rearrange("t (b e) -> t b e", b=B),
                                        br[:, :].rearrange("t (o e) -> t o e", o=1).broadcast_to((T, B, E0)), ALU.add).then_inc(s["logits"], 1)
                dve.wait_ge(s["logits"], 1)
                step_ = s["step"]
                r.choose(dve, step_)
                r.rank_rows(dve, step_, s["counted"])
                count = r.upto[:, :, B - 1:B].broadcast_to((T, E0, ROW_TILES))
                nc.vector.tensor_tensor(over[:, :, :], count, edges[:, :].rearrange("t (o k) -> t o k", o=1).broadcast_to((T, E0, ROW_TILES)),
                                        ALU.is_gt).then_inc(step_, 1)
                dve.wait_ge(step_, 10)
                nc.vector.tensor_reduce(tiles_of[:, :], over[:, :, :], AX, ALU.add).then_inc(step_, 1)
                dve.wait_ge(step_, 11)
                nc.vector.tensor_tensor_scan(tiles_to[:, :], r.ones[:, 0:E0], tiles_of[:, :], 0.0, ALU.mult, ALU.add).then_inc(step_, 1)
                dve.wait_ge(step_, 12)
                nc.vector.tensor_tensor(starts[:, :], tiles_to[:, :], tiles_of[:, :], ALU.subtract).then_inc(step_, 1)
                dve.wait_ge(step_, 13)
                nc.vector.scalar_tensor_tensor(out=r.rank[:, :, :], in0=starts[:, :].rearrange("t (e o) -> t e o", o=1).broadcast_to((T, E0, B)),
                                               scalar=float(P), in1=r.rank[:, :, :], op0=ALU.mult, op1=ALU.add).then_inc(step_, 1)
                dve.wait_ge(step_, 14)
                r.pick(dve, r.place[:, :], step_, 14)
                nc.vector.tensor_copy(g.place0[:, :], r.place[:, :]).then_inc(s["placed"], 1)
                nc.vector.tensor_tensor(passed[:, :, :], tiles_to[0:1, :].rearrange("t (o e) -> t o e", o=1).broadcast_to((1, TILES, E0)),
                                        tile_no[0:1, :].rearrange("t (j o) -> t j o", o=1).broadcast_to((1, TILES, E0)), ALU.is_le).then_inc(step_, 1)
                dve.wait_ge(step_, 17)
                nc.vector.tensor_reduce(owner[:, :], passed[:, :, :], AX, ALU.add).then_inc(step_, 1)
                dve.wait_ge(step_, 18)
                nc.vector.tensor_scalar(owner_i[:, :], owner[:, :], float(E0 - 1), None, ALU.min).then_inc(s["placed"], 1)

            @block.tensor
            def _(pe):
                pe.wait_ge(s["loaded"], 48)

                def step(b):
                    if b.real():
                        pe.wait_ge(s["xn"], b.count(1, 1))
                        if (b - 2).real():
                            pe.wait_ge(s["xt"], (b - 2).count(1, 1))
                        for h in range(2):
                            last = nc.tensor.transpose(bank[2 + b.parity][:, h * T:(h + 1) * T],
                                                       xn[b.parity][:, h * P:(h + 1) * P], g.ident[0:T, 0:T])
                        last.then_inc(s["xt_mm"], 1)
                    if (b - 1).real():
                        n = b - 1
                        pe.wait_ge(s["xt"], n.count(1, 1))
                        for h in range(2):
                            last = nc.tensor.matmul(bank[4][0:T, n.rows(E0)], xt[n.parity][:, h, :], wr[:, h, :],
                                                    start=(h == 0), stop=(h == 1))
                        last.then_inc(s["logits_mm"], 1)

                steps(pe, step, B, 2, B - 1, B + 1)
                pe.wait_ge(s["made"], 8)
                r.count_rows(pe, s["step"], s["counted"])

        with ExitStack() as tiles:
            def tb(name, shape, dt=F32):
                return g.sb(name, shape, dt, tiles)

            x_in = [tb(f"t0_in{p}", [P, D]) for p in range(2)]
            xt2 = [tb(f"t0_xt{p}", [P, 2, P]) for p in range(2)]
            up = [tb(f"t0_up{p}", [P, F0]) for p in range(2)]
            hid = [tb(f"t0_hid{p}", [P, K2, P]) for p in range(2)]
            y = [tb(f"t0_y{p}", [P, D]) for p in range(2)]
            end = TILES + 2

            def tile_steps(engine, step):
                steps(engine, step, TILES, 4, TILES - 3, end)

            block = nc.Block()
            with block:
                @block.sync
                def _(sp):
                    def load(j):
                        sp.dma_start(x_in[j.parity][:, :], g.sorted0[j.rows(P), :]).then_inc(s_in[j.parity], 16)

                    load(Item(0, 0, TILES))
                    load(Item(0, 1, TILES))

                    def step(j):
                        if (j + 2).real():
                            sp.wait_ge(s["x_mm"], j.count(1, 1))
                            sp.sem_inc(s["sp_turns"], 1)
                            load(j + 2)
                        if (j - 2).real():
                            n = j - 2
                            sp.wait_ge(s["down_copy"], n.count(1, 1))
                            sp.sem_inc(s["sp_turns"], 1)
                            sp.dma_start(g.made0[n.rows(P), :], y[n.parity][:, :]).then_inc(s_out[n.parity], 16)

                    tile_steps(sp, step)
                    sp.wait_ge(s_out[0], 16 * ((TILES + 1) // 2))
                    sp.wait_ge(s_out[1], 16 * (TILES // 2))

                @block.scalar
                def _(act):
                    def copy_in(j):
                        act.wait_ge(s["x_mm"], j.count(1, 1))
                        if (j - 2).real():
                            act.wait_ge(s["up"], (j - 2).count(1, 1))
                        nc.scalar.copy(xt2[j.parity][:, :, :], bank[2 + j.parity][:, 0:2 * P].rearrange("p (k t) -> p k t", k=2)).then_inc(s["x_copy"], 1)

                    copy_in(Item(0, 0, TILES))

                    def step(j):
                        if (j + 1).real():
                            copy_in(j + 1)
                        if (j - 1).real():
                            n = j - 1
                            e = act.value_load(owner_i[0:1, n.at()], min_val=0, max_val=E0 - 1)
                            act.wait_ge(s["back"], n.count(1, 1))
                            if (n - 2).real():
                                act.wait_ge(s["down"], (n - 2).count(1, 1))
                            for f in range(K2):
                                bias = g.b1[:, bass.ds(e, 1), f:f + 1].rearrange("p o f -> p (o f)")
                                nc.scalar.activation(hid[n.parity][:, f, :], bank[4 + n.parity][:, f * P:(f + 1) * P], ACT.Relu,
                                                     bias=bias).then_inc(s["back_copy"], 1)

                    tile_steps(act, step)

                @block.vector
                def _(dve):
                    def step(j):
                        if j.real():
                            dve.wait_ge(s["up"], j.count(1, 1))
                            if (j - 2).real():
                                dve.wait_ge(s["back"], (j - 2).count(1, 1))
                            nc.vector.tensor_copy(up[j.parity][:, :], bank[j.parity][:, :]).then_inc(s["up_copy"], 1)
                        if (j - 2).real():
                            n = j - 2
                            e = dve.value_load(owner_i[0:1, n.at()], min_val=0, max_val=E0 - 1)
                            dve.wait_ge(s["down"], n.count(1, 1))
                            if (n - 2).real():
                                dve.wait_ge(s_out[n.parity], (n - 2).turn(16, 16))
                            nc.vector.tensor_tensor(y[n.parity][:, :], bank[6 + n.parity][:, 0:D],
                                                    b2[:, bass.ds(e, 1), :].rearrange("p o d -> p (o d)"), ALU.add).then_inc(s["down_copy"], 1)

                    tile_steps(dve, step)

                @block.tensor
                def _(pe):
                    def transpose_in(j):
                        pe.wait_ge(s_in[j.parity], j.turn(16, 16))
                        if (j - 2).real():
                            pe.wait_ge(s["x_copy"], (j - 2).count(1, 1))
                        for h in range(2):
                            last = nc.tensor.transpose(bank[2 + j.parity][:, h * P:(h + 1) * P], x_in[j.parity][:, h * P:(h + 1) * P], g.ident[:, :])
                        last.then_inc(s["x_mm"], 1)

                    transpose_in(Item(0, 0, TILES))

                    def step(j):
                        if j.real():
                            e = pe.value_load(owner_i[0:1, j.at()], min_val=0, max_val=E0 - 1)
                            pe.wait_ge(s["x_copy"], j.count(1, 1))
                            if (j - 2).real():
                                pe.wait_ge(s["up_copy"], (j - 2).count(1, 1))
                            for h in range(2):
                                last = nc.tensor.matmul(bank[j.parity][:, :], xt2[j.parity][:, h, :],
                                                        g.w1[:, bass.ds(e, 1), h, :].rearrange("p o f -> p (o f)"), start=(h == 0), stop=(h == 1))
                            last.then_inc(s["up"], 1)
                        if (j + 1).real():
                            transpose_in(j + 1)
                        if (j - 2).real():
                            n = j - 2
                            e = pe.value_load(owner_i[0:1, n.at()], min_val=0, max_val=E0 - 1)
                            pe.wait_ge(s["back_copy"], n.count(K2, K2))
                            if (n - 2).real():
                                pe.wait_ge(s["down_copy"], (n - 2).count(1, 1))
                            for f in range(K2):
                                last = nc.tensor.matmul(bank[6 + n.parity][:, 0:D], hid[n.parity][:, f, :],
                                                        g.w2[:, bass.ds(e, 1), f, :].rearrange("p o d -> p (o d)"), start=(f == 0), stop=(f == K2 - 1))
                            last.then_inc(s["down"], 1)
                        if (j - 1).real():
                            n = j - 1
                            pe.wait_ge(s["up_copy"], n.count(1, 1))
                            if (n - 2).real():
                                pe.wait_ge(s["back_copy"], (n - 2).count(K2, K2))
                            for f in range(K2):
                                last = nc.tensor.transpose(bank[4 + n.parity][:, f * P:(f + 1) * P], up[n.parity][:, f * P:(f + 1) * P], g.ident[:, :])
                            last.then_inc(s["back"], 1)

                    tile_steps(pe, step)

        with ExitStack() as back:
            got = g.sb("got0", [T, B, D], F32, back)
            block = nc.Block()
            with block:
                @block.gpsimd
                def _(pool):
                    for b in range(B):
                        pool.indirect_dma_start(out=got[:, b, :], out_offset=None, in_=g.made0,
                                                in_offset=bass.IndirectOffsetOnAxis(g.place0[:, b:b + 1], 0)).then_inc(s["gathered"], 16)
                    pool.wait_ge(s["gathered"], 16 * B)

                @block.vector
                def _(dve):
                    dve.wait_ge(s["gathered"], 16 * B)
                    nc.vector.tensor_tensor(xs[:, :, :], xs[:, :, :], got[:, :, :], ALU.add).then_inc(s["x2"], 1)


def attention1(nc, a, g):
    bank, xs, ident = g.bank, g.xs, g.ident
    K2 = D // P
    with ExitStack() as phase:
        def sb(name, shape, dt=F32):
            return g.sb("a1_" + name, shape, dt, phase)

        def pair(name, shape, dt=F32):
            return [sb(f"{name}{p}", shape, dt) for p in range(2)]

        def psem(name):
            return [g.sem(f"a1_{name}{p}") for p in range(2)]

        weights = {n: sb(n, [P, K2, D]) for n in ("Wk", "Wv", "Wq", "Wo")}
        wo_t = sb("wo_t", [P, K2, D])
        w_qk = sb("w_qk", [P, K2, D])
        w_vo = sb("w_vo", [P, K2, D])
        bq = sb("bq", [P, K2])
        bv = sb("bv", [P, K2])
        bv_wide = sb("bv_wide", [P, K2, T])
        u = sb("u", [P, K2])
        row = sb("row", [T, D])
        xn2, xn3 = pair("xn2", [T, D]), pair("xn3", [T, D])
        xt2, xt3 = pair("xt2", [P, 2, T]), pair("xt3", [P, 2, T])
        stats2, stats3 = sb("stats2", [T, 6]), sb("stats3", [T, 6])
        mv2, mv3 = sb("mv2", [T, 2]), sb("mv3", [T, 2])
        rstd2, rstd3 = sb("rstd2", [T, 2]), sb("rstd3", [T, 2])
        q = pair("q", [P, 2, T])
        ct = pair("ct", [P, 2, S])
        cin = pair("ctx", [KC, NC, D])
        neg_max, total, inverse = pair("neg_max", [T, 1]), pair("total", [T, 1]), pair("inverse", [T, 1])
        prob = pair("prob", [T, S])
        prob_t = pair("prob_t", [KC, NC, T])
        mix = pair("mix", [P, 2, T])
        wg = sb("wg", [P, 2, E1])
        s = {n: g.sem("a1_" + n) for n in """loaded setup_mm setup_copy stats2 mv2 eps2 rstd2 xn2 xc t2 xt2 q_mm q scored maxed
            prob tp prob_t mix_mm mix out_mm inverse x3 stats3 mv3 eps3 rstd3 xn3 rows t3 xt3 logits_mm dve_turns sp_turns""".split()}
        s_ct, s_cin = psem("ct_loaded"), psem("ctx_loaded")
        g.rows1 = g.rows1_buffer
        SETUP = 6
        block = nc.Block()
        with block:
            @block.sync
            def _(sp):
                for n, w in weights.items():
                    sp.dma_start(w[:, :, :], a["L1_xattn_" + n].rearrange("(k p) d -> p k d", p=P)).then_inc(s["loaded"], 16)
                for b_, n in ((bq, "L1_xattn_bq"), (bv, "L1_xattn_bv")):
                    for k in range(K2):
                        sp.dma_start(b_[:, k:k + 1], a[n][k * P:(k + 1) * P].rearrange("(p o) -> p o", o=1)).then_inc(s["loaded"], 16)
                sp.dma_start(row[:, :], a["L1_xattn_bo"].rearrange("(o n) -> o n", o=1).broadcast_to((T, D))).then_inc(s["loaded"], 16)
                sp.dma_start(wg[:, :, :], a["L1_ffn_Wg"].rearrange("(k p) e -> p k e", p=P)).then_inc(s["loaded"], 16)

                def load_cin(b):
                    src = a["ctx_1024"][b.at()].rearrange("o (c k) d -> k (o c) d", k=KC)
                    sp.dma_start(cin[b.parity][:, :, :], src).then_inc(s_cin[b.parity], 16)

                def load_ct(b):
                    sp.dma_start(ct[b.parity][:, :, :], g.ct_dram[b.at()].rearrange("o p k n -> p (o k) n")).then_inc(s_ct[b.parity], 16)

                def step(b):
                    if b.real():
                        if (b - 2).real():
                            sp.wait_ge(s["scored"], (b - 2).count(1, 1))
                            sp.sem_inc(s["sp_turns"], 1)
                        load_ct(b)
                    if (b - 1).real():
                        n = b - 1
                        if (n - 2).real():
                            sp.wait_ge(s["mix_mm"], (n - 2).count(1, 1))
                            sp.sem_inc(s["sp_turns"], 1)
                        load_cin(n)
                    if isinstance(b.i, int) and b.c == 1:
                        for e in range(4):
                            load_w(nc, sp, a, g, Item(0, e, E1, 4), 1)
                            load_w(nc, sp, a, g, Item(0, e, E1, 4), 2)

                steps(sp, step, B, 3, B - 2, B + 1)

            def rstd_of(pool, b, k, mv, rstd):
                pool.wait_ge(s[f"mv{k}"], b.count(1, 1))
                nc.gpsimd.tensor_tensor(rstd[:, 0:1], mv[:, 1:2], g.eps[0:T, :], ALU.add).then_inc(s[f"eps{k}"], 1)
                pool.wait_ge(s[f"eps{k}"], b.count(1, 1))
                nc.gpsimd.tensor_tensor(rstd[:, 1:2], rstd[:, 0:1], g.neg_half[0:T, :], ALU.pow).then_inc(s[f"rstd{k}"], 1)

            @block.gpsimd
            def _(pool):
                def ahead(b):
                    rstd_of(pool, b, 2, mv2, rstd2)
                    pool.wait_ge(s["xn2"], b.count(1, 1))
                    stream = xs[:, b.at(), :].rearrange("t o d -> t (o d)")
                    nc.gpsimd.tensor_tensor(stream, stream, row[:, :], ALU.add).then_inc(s["xc"], 1)

                pool.wait_ge(s["setup_copy"], SETUP)
                ahead(Item(0, 0, B))

                def step(b):
                    if (b + 1).real():
                        ahead(b + 1)
                    if (b - 2).real():
                        rstd_of(pool, b - 2, 3, mv3, rstd3)

                attention_steps(pool, step)


            @block.scalar
            def _(act):
                def step(b):
                    if (b - 1).real():
                        n = b - 1
                        act.wait_ge(s["maxed"], n.count(1, 1))
                        if (n - 2).real():
                            act.wait_ge(s["tp"], (n - 2).count(1, 1))
                            act.wait_ge(s["inverse"], (n - 2).count(1, 1))
                        nc.scalar.activation(prob[n.parity][:, :], bank[0][0:T, 0:S], ACT.Exp, bias=neg_max[n.parity][:, :],
                                             accum_out=total[n.parity][:, :]).then_inc(s["prob"], 1)
                    if (b - 2).real():
                        n = b - 2
                        act.wait_ge(s["mix_mm"], n.count(1, 1))
                        if (n - 2).real():
                            act.wait_ge(s["out_mm"], (n - 2).count(1, 1))
                        nc.scalar.copy(mix[n.parity][:, :, :], bank[1][:, 0:2 * T].rearrange("p (k t) -> p k t", k=2)).then_inc(s["mix"], 1)
                    if b.real():
                        act.wait_ge(s["t2"], b.count(1, 1))
                        if (b - 2).real():
                            act.wait_ge(s["q_mm"], (b - 2).count(1, 1))
                        nc.scalar.copy(xt2[b.parity][:, :, :], bank[2][:, 0:2 * T].rearrange("p (k t) -> p k t", k=2)).then_inc(s["xt2"], 1)
                    if (b - 3).real():
                        n = b - 3
                        act.wait_ge(s["xn3"], n.count(1, 1))
                        nc.scalar.copy(g.rows1[:, n.at(), :].rearrange("t o d -> t (o d)"), xn3[n.parity][:, :]).then_inc(s["rows"], 1)
                        act.wait_ge(s["t3"], n.count(1, 1))
                        if (n - 2).real():
                            act.wait_ge(s["logits_mm"], (n - 2).count(1, 1))
                        nc.scalar.copy(xt3[n.parity][:, :, :], bank[3][:, 0:2 * T].rearrange("p (k t) -> p k t", k=2)).then_inc(s["xt3"], 1)
                    if b.real():
                        act.wait_ge(s["q_mm"], b.count(1, 1))
                        if (b - 2).real():
                            act.wait_ge(s["scored"], (b - 2).count(1, 1))
                        for h in range(2):
                            nc.scalar.activation(q[b.parity][:, h, :], bank[6][:, h * T:(h + 1) * T], ACT.Identity,
                                                 bias=u[:, h:h + 1], scale=D ** -0.5).then_inc(s["q"], 1)

                act.wait_ge(s["setup_copy"], SETUP)
                steps(act, step, B, 5, B - 2, B + 3)

            @block.vector
            def _(dve):
                dve.wait_ge(s["loaded"], 16 * 10)
                nc.vector.tensor_copy(bv_wide[:, :, :], bv[:, :].rearrange("p (k o) -> p k o", o=1).broadcast_to((P, K2, T))).then_inc(s["setup_copy"], 1)
                dve.wait_ge(s["setup_mm"], 1)
                nc.vector.tensor_copy(wo_t[:, :, :], bank[0][:, :].rearrange("p (k d) -> p k d", k=K2)).then_inc(s["setup_copy"], 1)
                dve.wait_ge(s["setup_mm"], 2)
                nc.vector.tensor_copy(w_qk[:, :, :], bank[1][:, :].rearrange("p (k d) -> p k d", k=K2)).then_inc(s["setup_copy"], 1)
                dve.wait_ge(s["setup_mm"], 4)
                nc.vector.tensor_scalar(u[:, :], bank[3][:, 0:K2], D ** -0.5, None, ALU.mult).then_inc(s["setup_copy"], 1)
                nc.vector.tensor_copy(w_vo[:, :, :], bank[2][:, :].rearrange("p (k d) -> p k d", k=K2)).then_inc(s["setup_copy"], 1)
                dve.wait_ge(s["setup_mm"], 5)
                nc.vector.tensor_tensor(row[:, :], bank[4][0:T, 0:D], row[:, :], ALU.add).then_inc(s["setup_copy"], 1)
                dve.wait_ge(s["setup_copy"], 6)

                def norm(b, k, stats, mv, rstd, xn, t_done, row_done=None):
                    stream = xs[:, b.at(), :].rearrange("t o d -> t (o d)")
                    nc.vector.bn_stats(stats[:, :], stream).then_inc(s[f"stats{k}"], 1)
                    dve.wait_ge(s[f"stats{k}"], b.count(1, 1))
                    dve.sem_inc(s["dve_turns"], 1)
                    nc.vector.bn_aggr(mv[:, :], stats[:, :]).then_inc(s[f"mv{k}"], 1)
                    dve.wait_ge(s[f"rstd{k}"], b.count(1, 1))
                    if (b - 2).real():
                        dve.wait_ge(t_done, (b - 2).count(1, 1))
                        if row_done is not None:
                            dve.wait_ge(row_done, (b - 2).count(1, 1))
                    nc.vector.tensor_scalar(xn[b.parity][:, :], stream, mv[:, 0:1], rstd[:, 1:2], ALU.subtract, ALU.mult).then_inc(s[f"xn{k}"], 1)

                norm(Item(0, 0, B), 2, stats2, mv2, rstd2, xn2, s["t2"])

                def step(b):
                    if (b - 1).real():
                        n = b - 1
                        dve.wait_ge(s["scored"], n.count(1, 1))
                        if (n - 2).real():
                            dve.wait_ge(s["prob"], (n - 2).count(1, 1))
                        nc.vector.tensor_reduce(neg_max[n.parity][:, :], bank[0][0:T, 0:S], AX, ALU.max, negate=True).then_inc(s["maxed"], 1)
                    if (b + 1).real():
                        norm(b + 1, 2, stats2, mv2, rstd2, xn2, s["t2"])
                    if (b - 1).real():
                        n = b - 1
                        dve.wait_ge(s["prob"], n.count(1, 1))
                        nc.vector.reciprocal(inverse[n.parity][:, :], total[n.parity][:, :]).then_inc(s["inverse"], 1)
                        dve.wait_ge(s["tp"], n.count(1, 1))
                        if (n - 2).real():
                            dve.wait_ge(s["mix_mm"], (n - 2).count(1, 1))
                        nc.vector.tensor_copy(prob_t[n.parity][:, :, :], bank[4][0:KC, 0:NC * T].rearrange("p (c t) -> p c t", c=NC)).then_inc(s["prob_t"], 1)
                    if (b - 2).real():
                        n = b - 2
                        dve.wait_ge(s["out_mm"], n.count(1, 1))
                        dve.wait_ge(s["inverse"], n.count(1, 1))
                        dve.wait_ge(s["xc"], n.count(1, 1))
                        stream = xs[:, n.at(), :].rearrange("t o d -> t (o d)")
                        nc.vector.scalar_tensor_tensor(out=stream, in0=bank[5][0:T, 0:D], scalar=inverse[n.parity][:, :], in1=stream,
                                                       op0=ALU.mult, op1=ALU.add).then_inc(s["x3"], 1)
                        dve.wait_ge(s["x3"], n.count(1, 1))
                        dve.sem_inc(s["dve_turns"], 1)
                        norm(n, 3, stats3, mv3, rstd3, xn3, s["t3"], s["rows"])

                steps(dve, step, B, 4, B - 2, B + 3)

            @block.tensor
            def _(pe):
                pe.wait_ge(s["loaded"], 16 * 10)
                for k in range(K2):
                    for m in range(K2):
                        last = nc.tensor.transpose(bank[0][:, k * D + m * P:k * D + (m + 1) * P], weights["Wo"][:, m, k * P:(k + 1) * P], ident[:, :])
                last.then_inc(s["setup_mm"], 1)

                def product(to, left, right):
                    for m in range(K2):
                        for k in range(K2):
                            last = nc.tensor.matmul(to[:, m * D:(m + 1) * D], left[:, k, m * P:(m + 1) * P], right[:, k, :],
                                                    start=(k == 0), stop=(k == K2 - 1))
                    return last

                product(bank[1], weights["Wq"], weights["Wk"]).then_inc(s["setup_mm"], 1)
                for m in range(K2):
                    for k in range(K2):
                        last = nc.tensor.matmul(bank[3][:, m:m + 1], weights["Wk"][:, k, m * P:(m + 1) * P], bq[:, k:k + 1],
                                                start=(k == 0), stop=(k == K2 - 1))
                last.then_inc(s["setup_mm"], 1)
                pe.wait_ge(s["setup_copy"], 2)
                product(bank[2], weights["Wv"], wo_t).then_inc(s["setup_mm"], 1)
                for k in range(K2):
                    last = nc.tensor.matmul(bank[4][0:T, 0:D], bv_wide[:, k, :], wo_t[:, k, :], start=(k == 0), stop=(k == K2 - 1))
                last.then_inc(s["setup_mm"], 1)
                pe.wait_ge(s["setup_copy"], SETUP)

                def step(b):
                    if (b - 1).real():
                        n = b - 1
                        pe.wait_ge(s_ct[n.parity], n.turn(16, 16))
                        pe.wait_ge(s["q"], n.count(2, 2))
                        if (n - 1).real():
                            pe.wait_ge(s["prob"], (n - 1).count(1, 1))
                        for h in range(2):
                            last = nc.tensor.matmul(bank[0][0:T, 0:S], q[n.parity][:, h, :], ct[n.parity][:, h, :], start=(h == 0), stop=(h == 1))
                        last.then_inc(s["scored"], 1)
                    if (b - 2).real():
                        n = b - 2
                        pe.wait_ge(s_cin[n.parity], n.turn(16, 16))
                        pe.wait_ge(s["prob_t"], n.count(1, 1))
                        if (n - 1).real():
                            pe.wait_ge(s["mix"], (n - 1).count(1, 1))
                        for h in range(2):
                            for c in range(NC):
                                last = nc.tensor.matmul(bank[1][:, h * T:(h + 1) * T], cin[n.parity][:, c, h * P:(h + 1) * P], prob_t[n.parity][:, c, :],
                                                        start=(c == 0), stop=(c == NC - 1))
                        last.then_inc(s["mix_mm"], 1)
                    if b.real():
                        pe.wait_ge(s["xn2"], b.count(1, 1))
                        if (b - 1).real():
                            pe.wait_ge(s["xt2"], (b - 1).count(1, 1))
                        for h in range(2):
                            last = nc.tensor.transpose(bank[2][:, h * T:(h + 1) * T], xn2[b.parity][:, h * P:(h + 1) * P], ident[0:T, 0:T])
                        last.then_inc(s["t2"], 1)
                    if (b - 3).real():
                        n = b - 3
                        pe.wait_ge(s["xn3"], n.count(1, 1))
                        if (n - 1).real():
                            pe.wait_ge(s["xt3"], (n - 1).count(1, 1))
                        for h in range(2):
                            last = nc.tensor.transpose(bank[3][:, h * T:(h + 1) * T], xn3[n.parity][:, h * P:(h + 1) * P], ident[0:T, 0:T])
                        last.then_inc(s["t3"], 1)
                    if (b - 1).real():
                        n = b - 1
                        pe.wait_ge(s["prob"], n.count(1, 1))
                        if (n - 1).real():
                            pe.wait_ge(s["prob_t"], (n - 1).count(1, 1))
                        for c in range(NC):
                            last = nc.tensor.transpose(bank[4][0:KC, c * T:(c + 1) * T], prob[n.parity][:, c * KC:(c + 1) * KC], ident[0:T, 0:T])
                        last.then_inc(s["tp"], 1)
                    if (b - 2).real():
                        n = b - 2
                        pe.wait_ge(s["mix"], n.count(1, 1))
                        if (n - 1).real():
                            pe.wait_ge(s["x3"], (n - 1).count(1, 1))
                        for h in range(2):
                            last = nc.tensor.matmul(bank[5][0:T, 0:D], mix[n.parity][:, h, :], w_vo[:, h, :], start=(h == 0), stop=(h == 1))
                        last.then_inc(s["out_mm"], 1)
                    if b.real():
                        pe.wait_ge(s["xt2"], b.count(1, 1))
                        if (b - 1).real():
                            pe.wait_ge(s["q"], (b - 1).count(2, 2))
                        for h in range(2):
                            for k in range(2):
                                last = nc.tensor.matmul(bank[6][:, h * T:(h + 1) * T], w_qk[:, k, h * P:(h + 1) * P], xt2[b.parity][:, k, :],
                                                        start=(k == 0), stop=(k == 1))
                        last.then_inc(s["q_mm"], 1)
                    if (b - 3).real():
                        n = b - 3
                        pe.wait_ge(s["xt3"], n.count(1, 1))
                        for h in range(2):
                            last = nc.tensor.matmul(bank[7][0:T, n.rows(E1)], xt3[n.parity][:, h, :], wg[:, h, :], start=(h == 0), stop=(h == 1))
                        last.then_inc(s["logits_mm"], 1)

                attention_steps(pe, step)


def load_w(nc, sp, a, g, e, which):
    k = e.quarter
    if which == 1:
        src = a["L1_ffn_w1"][e.at()].rearrange("o (k p) f -> p (o k) f", p=P)
        sp.dma_start(g.ring1[k][:, :, :], src).then_inc(g.s_ring1[k], 16)
    else:
        src = a["L1_ffn_w2"][e.at()].rearrange("o (k p) d -> p (o k) d", p=P)
        sp.dma_start(g.ring2[k][:, :, :], src).then_inc(g.s_ring2[k], 16)


def ffn1(nc, a, out, g):
    bank, xs = g.bank, g.xs
    KF = F1 // P
    with ExitStack() as phase:
        def sb(name, shape, dt=F32):
            return g.sb("f1_" + name, shape, dt, phase)

        shifted = sb("shifted", [T, B, E1])
        sums = sb("sums", [T, B])
        gate = sb("gate", [T, B])
        valid = sb("valid", [T, B])
        spare = sb("spare", [T, B])
        taken = sb("taken", [T, B])
        lost = sb("lost", [T, B])
        target = sb("target", [T, B])
        target_i = sb("target_i", [T, B], I32)
        source_i = sb("source_i", [T, B], I32)
        s = {n: g.sem("f1_" + n) for n in """made logits step counted shifted expd placed scattered x_mm x_copy up hid_a hid_v
            down down_copy sp_turns done""".split()}
        s_in = [g.sem(f"f1_rows_loaded{p}") for p in range(2)]
        s_out = [g.sem(f"f1_rows_stored{p}") for p in range(2)]
        r = routing(nc, g, phase, E1, "_1")
        block = nc.Block()
        with block:
            @block.gpsimd
            def _(pool):
                r.constants(pool, s["made"])
                nc.gpsimd.iota(spare[:, :], [[T, B]], base=E1 * C1, channel_multiplier=1,
                               allow_small_or_imprecise_dtypes=True).then_inc(s["made"], 1)
                pool.wait_ge(s["placed"], 1)
                for b in range(B):
                    pool.indirect_dma_start(out=g.sorted1, out_offset=bass.IndirectOffsetOnAxis(target_i[:, b:b + 1], 0),
                                            in_=g.rows1[:, b, :], in_offset=None).then_inc(s["scattered"], 16)
                pool.wait_ge(s["scattered"], 16 * B)

            @block.scalar
            def _(act):
                act.wait_ge(s["shifted"], 1)
                nc.scalar.activation(shifted[:, :, :], shifted[:, :, :], ACT.Exp).then_inc(s["expd"], 1)

            @block.vector
            def _(dve):
                step = s["step"]
                nc.vector.tensor_copy(r.logits[:, :, :], bank[7][0:T, 0:B * E1].rearrange("t (b e) -> t b e", b=B)).then_inc(s["logits"], 1)
                dve.wait_ge(s["logits"], 1)
                dve.wait_ge(s["made"], 7)
                r.choose(dve, step)
                nc.vector.tensor_tensor(shifted[:, :, :], r.logits[:, :, :], r.best[:, :].rearrange("t (b o) -> t b o", o=1).broadcast_to((T, B, E1)),
                                        ALU.subtract).then_inc(s["shifted"], 1)
                r.rank_rows(dve, step, s["counted"])
                r.pick(dve, r.place[:, :], step, 9)
                nc.vector.tensor_scalar(valid[:, :], r.place[:, :], float(C1), None, ALU.is_lt).then_inc(step, 1)
                dve.wait_ge(step, 12)
                nc.vector.tensor_scalar(r.place[:, :], r.place[:, :], float(C1 - 1), None, ALU.min).then_inc(step, 1)
                dve.wait_ge(step, 13)
                nc.vector.scalar_tensor_tensor(out=r.place[:, :], in0=r.which[:, :], scalar=float(C1), in1=r.place[:, :],
                                               op0=ALU.mult, op1=ALU.add).then_inc(step, 1)
                dve.wait_ge(step, 14)
                nc.vector.tensor_copy(source_i[:, :], r.place[:, :]).then_inc(step, 1)
                nc.vector.tensor_tensor(taken[:, :], r.place[:, :], valid[:, :], ALU.mult).then_inc(step, 1)
                nc.vector.tensor_tensor(lost[:, :], spare[:, :], valid[:, :], ALU.mult).then_inc(step, 1)
                dve.wait_ge(step, 17)
                nc.vector.tensor_tensor(lost[:, :], spare[:, :], lost[:, :], ALU.subtract).then_inc(step, 1)
                dve.wait_ge(step, 18)
                nc.vector.tensor_tensor(target[:, :], taken[:, :], lost[:, :], ALU.add).then_inc(step, 1)
                dve.wait_ge(step, 19)
                nc.vector.tensor_copy(target_i[:, :], target[:, :]).then_inc(s["placed"], 1)
                dve.wait_ge(s["expd"], 1)
                nc.vector.tensor_reduce(sums[:, :], shifted[:, :, :], AX, ALU.add).then_inc(step, 1)
                dve.wait_ge(step, 20)
                nc.vector.reciprocal(gate[:, :], sums[:, :]).then_inc(step, 1)
                dve.wait_ge(step, 21)
                nc.vector.tensor_tensor(gate[:, :], gate[:, :], valid[:, :], ALU.mult).then_inc(step, 1)
                dve.wait_ge(step, 22)

            @block.tensor
            def _(pe):
                pe.wait_ge(s["made"], 7)
                r.count_rows(pe, s["step"], s["counted"])

        with ExitStack() as experts:
            def tb(name, shape, dt=F32):
                return [g.sb(f"e1_{name}{p}", shape, dt, experts) for p in range(2)]

            x_in, xt, hid, y = tb("x_in", [C1, D]), tb("xt", [P, 2, C1]), tb("hid", [P, KF, C1]), tb("y", [C1, D])
            block = nc.Block()
            with block:
                @block.sync
                def _(sp):
                    def load(e):
                        sp.dma_start(x_in[e.parity][:, :], g.sorted1[e.rows(C1), :]).then_inc(s_in[e.parity], 16)

                    load(Item(0, 0, E1, 4))
                    load(Item(0, 1, E1, 4))

                    def step(e):
                        if (e + 2).real():
                            sp.wait_ge(s["x_mm"], e.count(1, 1))
                            sp.sem_inc(s["sp_turns"], 1)
                            load(e + 2)
                        if (e + 4).real():
                            sp.wait_ge(s["up"], e.count(2, 2))
                            sp.sem_inc(s["sp_turns"], 1)
                            load_w(nc, sp, a, g, e + 4, 1)
                        if (e - 1).real():
                            n = e - 1
                            sp.wait_ge(s["down_copy"], n.count(1, 1))
                            sp.sem_inc(s["sp_turns"], 1)
                            sp.dma_start(g.made1[n.rows(C1), :], y[n.parity][:, :]).then_inc(s_out[n.parity], 16)
                            if (n + 4).real():
                                load_w(nc, sp, a, g, n + 4, 2)

                    steps(sp, step, E1, 1, E1 - 5, E1 + 1, 4)
                    for p in range(2):
                        sp.wait_ge(s_out[p], 16 * E1 // 2)

                @block.scalar
                def _(act):
                    def step(e):
                        if e.real():
                            act.wait_ge(s["x_mm"], e.count(1, 1))
                            if (e - 2).real():
                                act.wait_ge(s["up"], (e - 2).count(2, 2))
                            nc.scalar.copy(xt[e.parity][:, :, :], bank[4 + e.parity][:, 0:2 * C1].rearrange("p (k t) -> p k t", k=2)).then_inc(s["x_copy"], 1)
                        if (e - 1).real():
                            n = e - 1
                            act.wait_ge(s["up"], n.count(2, 1))
                            if (n - 2).real():
                                act.wait_ge(s["down"], (n - 2).count(1, 1))
                            nc.scalar.activation(hid[n.parity][:, 0:KF // 2, :], bank[2 * n.parity][:, 0:4 * C1].rearrange("p (f t) -> p f t", f=KF // 2),
                                                 ACT.Relu).then_inc(s["hid_a"], 1)

                    steps(act, step, E1, 3, E1 - 2, E1 + 1, 4)

                @block.vector
                def _(dve):
                    def step(e):
                        if (e - 2).real():
                            n = e - 2
                            dve.wait_ge(s["down"], n.count(1, 1))
                            if (n - 2).real():
                                dve.wait_ge(s_out[n.parity], (n - 2).turn(16, 16))
                            nc.vector.tensor_copy(y[n.parity][:, :], bank[6 + n.parity][0:C1, 0:D]).then_inc(s["down_copy"], 1)
                        if (e - 1).real():
                            n = e - 1
                            dve.wait_ge(s["up"], n.count(2, 2))
                            if (n - 2).real():
                                dve.wait_ge(s["down"], (n - 2).count(1, 1))
                            nc.vector.tensor_scalar(hid[n.parity][:, KF // 2:KF, :], bank[2 * n.parity + 1][:, 0:4 * C1].rearrange("p (f t) -> p f t", f=KF // 2),
                                                    0.0, None, ALU.max).then_inc(s["hid_v"], 1)

                    steps(dve, step, E1, 4, E1 - 1, E1 + 2, 4)

                @block.tensor
                def _(pe):
                    def transpose_in(e):
                        pe.wait_ge(s_in[e.parity], e.turn(16, 16))
                        if (e - 2).real():
                            pe.wait_ge(s["x_copy"], (e - 2).count(1, 1))
                        for h in range(2):
                            last = nc.tensor.transpose(bank[4 + e.parity][:, h * C1:(h + 1) * C1], x_in[e.parity][:, h * P:(h + 1) * P], g.ident[0:C1, 0:C1])
                        last.then_inc(s["x_mm"], 1)

                    transpose_in(Item(0, 0, E1, 4))

                    def step(e):
                        if e.real():
                            pe.wait_ge(s["x_copy"], e.count(1, 1))
                            pe.wait_ge(g.s_ring1[e.quarter], e.turn(16, 16, 4))
                            if (e - 2).real():
                                pe.wait_ge(s["hid_a"], (e - 2).count(1, 1))
                                pe.wait_ge(s["hid_v"], (e - 2).count(1, 1))
                            for f in range(KF):
                                for k in range(2):
                                    last = nc.tensor.matmul(bank[2 * e.parity + f // 4][:, f % 4 * C1:(f % 4 + 1) * C1],
                                                            g.ring1[e.quarter][:, k, f * P:(f + 1) * P], xt[e.parity][:, k, :], start=(k == 0), stop=(k == 1))
                                if f % 4 == 3:
                                    last.then_inc(s["up"], 1)
                        if (e + 1).real():
                            transpose_in(e + 1)
                        if (e - 1).real():
                            n = e - 1
                            pe.wait_ge(g.s_ring2[n.quarter], n.turn(16, 16, 4))
                            pe.wait_ge(s["hid_a"], n.count(1, 1))
                            pe.wait_ge(s["hid_v"], n.count(1, 1))
                            if (n - 2).real():
                                pe.wait_ge(s["down_copy"], (n - 2).count(1, 1))
                            for f in range(KF):
                                last = nc.tensor.matmul(bank[6 + n.parity][0:C1, 0:D], hid[n.parity][:, f, :], g.ring2[n.quarter][:, f, :],
                                                        start=(f == 0), stop=(f == KF - 1))
                            last.then_inc(s["down"], 1)

                    steps(pe, step, E1, 3, E1 - 2, E1 + 1, 4)

        with ExitStack() as back:
            got = g.sb("got1", [T, B, D], F32, back)
            s_got = [g.sem(f"gathered{b}") for b in range(B)]
            block = nc.Block()
            with block:
                @block.gpsimd
                def _(pool):
                    for b in range(B):
                        pool.indirect_dma_start(out=got[:, b, :], out_offset=None, in_=g.made1,
                                                in_offset=bass.IndirectOffsetOnAxis(source_i[:, b:b + 1], 0)).then_inc(s_got[b], 16)

                @block.vector
                def _(dve):
                    for b in range(B):
                        dve.wait_ge(s_got[b], 16)
                        nc.vector.scalar_tensor_tensor(out=xs[:, b, :], in0=got[:, b, :], scalar=gate[:, b:b + 1], in1=xs[:, b, :],
                                                       op0=ALU.mult, op1=ALU.add).then_inc(s["step"], 1)

                @block.sync
                def _(sp):
                    for b in range(B):
                        sp.wait_ge(s["step"], 22 + b + 1)
                        sp.dma_start(out[b], xs[:, b, :]).then_inc(s["done"], 16)
                    sp.wait_ge(s["done"], 16 * B)


def kernel(**inputs):
    import numpy as np
    from concourse import bacc
    from concourse.bass_utils import run_bass_kernel_spmd

    nc = bacc.Bacc("TRN2", target_bir_lowering=False, num_devices=1)
    arrays, args = {}, {}
    for name, value in inputs.items():
        array = np.ascontiguousarray(value)
        arrays[f"in_{name}"] = array
        args[name] = nc.dram_tensor(f"in_{name}", array.shape, mybir.dt.from_np(array.dtype), kind="ExternalInput").ap()
    out = nc.dram_tensor("out", (B, T, D), F32, kind="ExternalOutput").ap()
    program(nc, args, out)
    return run_bass_kernel_spmd(nc, [arrays], core_ids=[0]).results[0]["out"]
```

```python
from contextlib import ExitStack

import concourse.bass as bass
from concourse import mybir

F32 = mybir.dt.float32
BF16 = mybir.dt.bfloat16
I32 = mybir.dt.int32
ALU = mybir.AluOpType
ACT = mybir.ActivationFunctionType
AX = mybir.AxisListType.X

B, T, D = 16, 112, 256
S = 375
H, DH = 16, 16
KC, NC = 125, 3
CHUNKS = ((0, 128), (128, 128), (256, S - 256))
KV = S + T
EPS = 1e-5
TERMS_Q = (0, 0, 1, 0, 2, 1)
TERMS_K = (0, 1, 0, 2, 0, 1)
NT = len(TERMS_Q)
QK = NT * DH
ROWS = QK + 6
HG = 4
P = 128
E0, F0 = 8, 512
ROW_TILES = B * T // P
TILES = ROW_TILES + E0 - 1
E1, F1 = 16, 1024
C1 = (B * T) // E1
N = B * T
REGION = N + P
ROW0 = D + 1
ROW1 = 2 * D + 2


FIRST = 6
assert (B - 1 - FIRST) // 2 * 2 == E0


class Item:

    def __init__(self, i, c, n, unroll=2):
        self.i, self.c, self.n, self.unroll = i, c, n, unroll
        self.parity = c % 2
        self.quarter = c % 4

    def __sub__(self, k):
        return Item(self.i, self.c - k, self.n, self.unroll)

    def __add__(self, k):
        return Item(self.i, self.c + k, self.n, self.unroll)

    def number(self, per=1):
        return per * self.c if isinstance(self.i, int) else self.i * (self.unroll * per) + per * self.c

    def count(self, per=1, plus=0):
        const = per * self.c + plus
        assert const > (0 if self.looped() else -1)
        return const if isinstance(self.i, int) else self.i * (self.unroll * per) + const

    def looped(self):
        return not isinstance(self.i, int)

    def turn(self, per=16, plus=0, of=2):
        const = per * (self.c // of) + plus
        assert const > (0 if self.looped() else -1)
        return const if isinstance(self.i, int) else self.i * (self.unroll // of * per) + const

    def at(self):
        return bass.ds(self.number(), 1)

    def rows(self, size):
        return bass.ds(self.number(size), size)

    def real(self):
        return self.looped() or 0 <= self.c < self.n


def steps(engine, step, n, first, last, end, unroll=2):
    loops = (last - first + 1) // unroll
    for c in range(first):
        step(Item(0, c, n))
    with engine.Fori(0, loops) as i:
        for c in range(unroll):
            step(Item(i, first + c, n, unroll))
    for c in range(first + loops * unroll, end):
        step(Item(0, c, n))


def attention_steps(engine, step):
    steps(engine, step, B, FIRST, B - 2, B + 5)


class Shared:
    pass


def program(nc, a, out):
    with ExitStack() as ctx:
        g = Shared()
        g.nc = nc

        def sb(name, shape, dt=F32, where=ctx):
            return where.enter_context(nc.sbuf_tensor(name, shape, dt))

        def sem(name):
            handle = nc.alloc_semaphore(name=name)
            if g.phase_sems is not None:
                g.phase_sems.append(handle)
            return handle

        g.phase_sems = None

        def phase(run, *args):
            g.phase_sems = []
            run(*args)
            nc.all_engine_barrier()
            nc.clear_and_free_semaphores(g.phase_sems)
            nc.all_engine_barrier()
            g.phase_sems = None

        def dram(name, shape, dt=F32):
            return nc.dram_tensor(name, shape, dt, kind="Internal").ap()

        g.sb, g.sem, g.dram = sb, sem, dram
        g.psum = ctx.enter_context(nc.psum_tensor("psum", [P, 8, 512], F32))
        g.bank = [g.psum[:, k, :] for k in range(8)]
        g.xs = sb("xs", [T, B, D])
        g.ident = sb("ident", [P, P])
        g.ident16 = sb("ident16", [P, P], BF16)
        g.neg_half = sb("neg_half", [P, 1])
        g.eps = sb("eps", [P, 1])
        g.ct_dram = dram("ct_dram", (B, P, 2, S))
        g.sorted0 = dram("sorted0", (E0 * REGION + P, ROW0))
        g.made0 = dram("made0", (N, D))
        g.sorted1 = dram("sorted1", (E1 * C1, ROW1))
        g.w_qk = sb("a1_w_qk", [P, 2, D])
        g.w_vo = sb("a1_w_vo", [P, 2, D])
        g.u = sb("a1_u", [P, 2])
        g.row = sb("a1_row", [T, D])
        g.wg = sb("a1_wg", [P, 2, E1])
        g.s_w0 = sem("experts0_loaded")
        g.s_zero = sem("sorted_cleared")
        g.acc = [sb(f"counts{p}", [T, E0], BF16) for p in range(2)]
        g.empty = sb("empty", [P, ROW0])
        with ExitStack() as layer0:
            g.w1 = sb("w1", [P, E0, 2, F0], F32, layer0)
            g.w2 = sb("w2", [P, E0, F0 // P, D], F32, layer0)
            phase(attention0, nc, a, g)
            phase(ffn0, nc, a, g)
        with ExitStack() as layer1:
            g.ring1 = [sb(f"ring1_{k}", [P, 2, F1], F32, layer1) for k in range(4)]
            g.ring2 = [sb(f"ring2_{k}", [P, F1 // P, D], F32, layer1) for k in range(4)]
            g.s_ring1 = [sem(f"w1_loaded{k}") for k in range(4)]
            g.s_ring2 = [sem(f"w2_loaded{k}") for k in range(4)]
            phase(attention1, nc, a, out, g)
            phase(ffn1, nc, a, out, g)


def attention0(nc, a, g_):
    sem, dram, psum, bank, xs, ident, ident16 = g_.sem, g_.dram, g_.psum, g_.bank, g_.xs, g_.ident, g_.ident16
    neg_half, eps = g_.neg_half, g_.eps
    with ExitStack() as phase:
        def sb(name, shape, dt=F32):
            return g_.sb(name, shape, dt, phase)

        w_x = sb("w_x", [P, 2, 3 * D])
        w_aux = sb("w_aux", [P, 2, 2 * D])
        wo = sb("wo", [P, 2, D])
        bias_t = sb("bias_t", [P, 6])
        g_wide = sb("g_wide", [P, H])
        inv_gate = sb("inv_gate", [P, 2, H])
        gate = sb("gate", [P, 2, H])
        c_wide = sb("c_wide", [T, D])
        ctx_in = [sb(f"ctx_in{p}", [P, NC, D]) for p in range(2)]
        ln_stats = sb("ln_stats", [T, 6])
        ln_mv = sb("ln_mv", [T, 2])
        ln_rstd = sb("ln_rstd", [T, 2])
        xn = [sb(f"xn{p}", [T, D]) for p in range(2)]
        xt = [sb(f"xt{p}", [P, 2, T]) for p in range(2)]
        ct = [sb(f"ct{p}", [P, 2, S]) for p in range(2)]
        parts = [sb(f"parts{p}", [P, 3, 2, KV + T], BF16) for p in range(2)]
        rest = sb("rest", [P, 2, KV + T])
        k_stack = [sb(f"k_stack{p}", [ROWS, H, KV], BF16) for p in range(2)]
        q_stack = [sb(f"q_stack{p}", [ROWS, H, T], BF16) for p in range(2)]
        v = [sb(f"v{p}", [P, NC + 1, H, 2 * DH]) for p in range(2)]
        neg_max = sb("neg_max", [T, 2, H])
        max_rest = sb("max_rest", [T, 2, H])
        max_parts = sb("max_parts", [T, 2, 3, H], BF16)
        mt = sb("mt", [QK, T], BF16)
        probs = [sb(f"probs{k}", [P, 4, T]) for k in range(4)]
        pv = [sb(f"pv{u}", [P, 2, 2, T]) for u in range(2)]
        inv_sum = [sb(f"inv_sum{u}", [T, H]) for u in range(2)]
        normed = sb("normed", [T, 2, 2, P // 2])
        mixed_rows = sb("mixed_rows", [T, 2, P])
        mixed = sb("mixed", [P, 2, T])
        sides = normed[0:ROWS, :, :, :].rearrange("t g s d -> t (g s d)").bitcast(BF16)[:, 0:KV]
        bv = [probs[o][0:T, :, :].rearrange("t j q -> t (j q)")[:, 0:D] for o in range(2)]
        bv_mix, bv_t = mixed_rows[:, :, :].rearrange("t u d -> t (u d)"), mixed
        r = router0(nc, g_, phase, bank[4], bank[5])

        parts_dram = [dram(f"parts_dram{p}", (6, P, KV + T), BF16) for p in range(2)]
        max_dram = [dram(f"max_dram{p}", (QK, T), BF16) for p in range(2)]

        s = {n: sem(n) for n in """consts w_loaded x0_loaded x1_loaded x2_loaded bias_loaded out_loaded sides_made sides_ready
            g_limit g_exp gate_step inv_gate_ready bv_mix bv_mm bv_t c_mm c_ready
            ln_stats_ready ln_mv_ready ln_eps_ready ln_rstd_ready xn_ready xc_ready
            xt_mm ct_mm xt_ready ct_ready v01_mm v23_mm v_ready qk_mm ka0_mm ka1_mm
            high_done rest_done mid_done low_done scored max_done msplit mt_mm mt_ready
            logits_mm exp_done pv_done pv_out turned_mm inverted scaled mixed_made mixed_mm mixed_ready wo_mm x1_ready
            dve_turns pool_turns sp_turns""".split()}
        s_spill = [sem(f"ct_spilled{p}") for p in range(2)]
        s_ctx = [sem(f"ctx_loaded{p}") for p in range(2)]
        s_parts = [sem(f"parts_written{p}") for p in range(2)]
        s_stack = [sem(f"stack_ready{p}") for p in range(2)]
        s_mw = [sem(f"max_written{p}") for p in range(2)]
        s_mr = [sem(f"max_ready{p}") for p in range(2)]
        block = phase.enter_context(nc.Block())

        @block.sync
        def _(sp):
            def load_context(n):
                rows = a["ctx_1024"][n.at()]
                whole = rows[:, 0:2 * P, :].rearrange("o (c k) d -> k (o c) d", k=P)
                sp.dma_start(ctx_in[n.parity][:, 0:2, :], whole).then_inc(s_ctx[n.parity], 16)
                sp.dma_start(ctx_in[n.parity][0:CHUNKS[2][1], 2, :], rows[:, 2 * P:S, :].rearrange("o k d -> k (o d)")).then_inc(s_ctx[n.parity], 16)

            sp.dma_start(xs[:, 0, :], a["x"][0]).then_inc(s["x0_loaded"], 16)
            load_context(Item(0, 0, B))
            sp.dma_start(w_x[:, :, :], a["L0_xattn_Wqkv"].rearrange("(a p) n -> p a n", p=P)).then_inc(s["w_loaded"], 16)
            sp.dma_start(w_aux[:, :, :], a["L0_xattn_Wqkv_aux"][:, D:3 * D].rearrange("(a p) n -> p a n", p=P)).then_inc(s["w_loaded"], 16)
            for k in range(4):
                src = a["L0_xattn_bqkv"][k * P:(k + 1) * P].rearrange("(p o) -> p o", o=1)
                sp.dma_start(bias_t[:, k:k + 1], src).then_inc(s["bias_loaded"], 16)
            for k in range(2):
                src = a["L0_xattn_bqkv_aux"][D + k * P:D + (k + 1) * P].rearrange("(p o) -> p o", o=1)
                sp.dma_start(bias_t[:, 4 + k:5 + k], src).then_inc(s["bias_loaded"], 16)
            sp.dma_start(xs[:, 1, :], a["x"][1]).then_inc(s["x1_loaded"], 16)
            sp.dma_start(xs[:, 2:B, :], a["x"][2:B].rearrange("b t d -> t b d")).then_inc(s["x2_loaded"], 16)
            g_row = a["L0_xattn_g"].rearrange("(o h) -> o h", o=1)
            sp.dma_start(g_wide[:, :], g_row.broadcast_to((P, H))).then_inc(s["out_loaded"], 16)

            def load_output():
                bo = a["L0_xattn_bo"].rearrange("(o n) -> o n", o=1)
                sp.dma_start(wo[:, :, :], a["L0_xattn_Wo"].rearrange("(a p) n -> p a n", p=P)).then_inc(s["out_loaded"], 16)
                sp.dma_start(c_wide[:, :], bo.broadcast_to((T, D))).then_inc(s["out_loaded"], 16)
                sp.dma_start(r.w[:, :, :], a["L0_ffn_Wr"].rearrange("(k p) e -> p k e", p=P)).then_inc(r.own["loaded"], 16)
                sp.dma_start(r.bias[:, :], a["L0_ffn_br"].rearrange("(o e) -> o e", o=1).broadcast_to((T, E0))).then_inc(r.own["loaded"], 16)
                for o, name in enumerate(("L0_xattn_bqkv", "L0_xattn_bqkv_aux")):
                    row = a[name][2 * D:3 * D].rearrange("(o n) -> o n", o=1)
                    sp.dma_start(bv[o], row.broadcast_to((T, D))).then_inc(s["out_loaded"], 16)

            def load_expert(e):
                to_1 = g_.w1[:, e.at(), :, :].rearrange("p o k f -> p (o k) f")
                sp.dma_start(to_1, a["L0_ffn_W1"][e.at()].rearrange("o (k p) f -> p (o k) f", p=P)).then_inc(g_.s_w0, 16)
                to_2 = g_.w2[:, e.at(), :, :].rearrange("p o k d -> p (o k) d")
                sp.dma_start(to_2, a["L0_ffn_W2"][e.at()].rearrange("o (k p) d -> p (o k) d", p=P)).then_inc(g_.s_w0, 16)

            def clear_places(part, parts):
                per = E1 * C1 // P // parts
                places = g_.sorted1.rearrange("(q p k) (h n) -> q p (k h) n", q=parts, p=P, h=2)
                empty = g_.empty[:, :].rearrange("p (o n) -> p o n", o=1).broadcast_to((P, 2 * per, ROW0))
                sp.dma_start(places[part], empty).then_inc(g_.s_zero, 16)

            def step(b):
                if not b.looped() and b.c == 0:
                    load_output()
                if (b + 1).real():
                    if not isinstance(b.i, int) or b.c >= 1:
                        sp.wait_ge(s["ct_mm"], b.count())
                        sp.sem_inc(s["sp_turns"], 1)
                    load_context(b + 1)
                if (b - 1).real():
                    n = b - 1
                    sp.wait_ge(s_parts[n.parity], n.turn(16, 16))
                    sp.sem_inc(s["sp_turns"], 1)
                    if (b - 3).real():
                        sp.wait_ge(s["pv_done"], (b - 3).count(16, 16))
                    src = parts_dram[n.parity].rearrange("(t a) p n -> t (a p) n", a=2)
                    for t in range(NT):
                        rows = slice(DH * t, DH * t + DH)
                        k_src = src[TERMS_K[t]][:, 0:KV].rearrange("(h d) n -> d h n", d=DH)
                        q_src = src[TERMS_Q[t]][:, KV:KV + T].rearrange("(h d) n -> d h n", d=DH)
                        sp.dma_start(k_stack[n.parity][rows, :, :], k_src).then_inc(s_stack[n.parity], 16)
                        sp.dma_start(q_stack[n.parity][rows, :, :], q_src).then_inc(s_stack[n.parity], 16)
                if (b - 2).real():
                    n = b - 2
                    sp.wait_ge(s["mt_ready"], n.count(1, 1))
                    sp.dma_start(max_dram[n.parity], mt[:, :]).then_inc(s_mw[n.parity], 16)
                    sp.wait_ge(s_mw[n.parity], n.turn(16, 16))
                    sp.dma_start(q_stack[n.parity][QK:ROWS, :, :],
                                 max_dram[n.parity].rearrange("(k h) n -> k h n", h=H)).then_inc(s_mr[n.parity], 16)
                if b.real():
                    sp.wait_ge(s["ct_ready"], b.count(2, 2))
                    spill = g_.ct_dram[b.at()].rearrange("o p a n -> p (o a) n")
                    sp.sem_inc(s["sp_turns"], 1)
                    sp.dma_start(spill, ct[b.parity][:, :, :]).then_inc(s_spill[b.parity], 16)
                    sp.wait_ge(s["low_done"], b.count(2, 2))
                    sp.dma_start(parts_dram[b.parity].rearrange("g p n -> p g n"),
                                 parts[b.parity][:, :, :, :].rearrange("p t a n -> p (t a) n")).then_inc(s_parts[b.parity], 16)
                if b.looped():
                    load_expert(b - FIRST)
                    return
                if b.c == 1:
                    sp.wait_ge(r.own["emptied"], 2)
                    sp.dma_start(g_.sorted0[E0 * REGION:E0 * REGION + P, :], g_.empty[:, :]).then_inc(g_.s_zero, 16)
                if b.c in (4, 5):
                    clear_places(b.c - 4, 2)

            attention_steps(sp, step)
            for p in range(2):
                sp.wait_ge(s_spill[p], 16 * B // 2)
            sp.wait_ge(g_.s_w0, 16 * E0 * 2)
            sp.wait_ge(g_.s_zero, 16 * 3)

        @block.gpsimd
        def _(pool):
            def ln(b):
                pool.wait_ge(s["ln_mv_ready"], b.count(1, 1))
                nc.gpsimd.tensor_tensor(ln_rstd[:, 0:1], ln_mv[:, 1:2], eps[0:T, :], ALU.add).then_inc(s["ln_eps_ready"], 1)
                pool.wait_ge(s["ln_eps_ready"], b.count(1, 1))
                nc.gpsimd.tensor_tensor(ln_rstd[:, 1:2], ln_rstd[:, 0:1], neg_half[0:T, :], ALU.pow).then_inc(s["ln_rstd_ready"], 1)

            pool.memset(neg_half[:, :], -0.5).then_inc(s["consts"], 1)
            pool.memset(eps[:, :], EPS).then_inc(s["consts"], 1)
            pool.memset(ident[:, :], 0.0).then_inc(s["consts"], 1)
            pool.memset(ident16[:, :], 0.0).then_inc(s["consts"], 1)
            pool.wait_ge(s["consts"], 4)
            for m in (ident, ident16):
                pool.affine_select(out=m[:, :], in_=m[:, :], compare_op=ALU.not_equal, fill=1.0, base=0,
                                   pattern=[[-1, P]], channel_multiplier=1).then_inc(s["consts"], 1)
            ln(Item(0, 0, B))
            pool.wait_ge(s["ln_rstd_ready"], 1)
            own, other = sides[QK:ROWS, S:KV], sides[QK:ROWS, 0:S]
            pool.memset(sides[QK:ROWS, :], 0.0).then_inc(s["sides_made"], 1)
            pool.wait_ge(s["sides_made"], 1)
            pool.affine_select(out=other, in_=other, compare_op=ALU.is_ge, fill=1.0, base=-3,
                               pattern=[[0, S]], channel_multiplier=1).then_inc(s["sides_made"], 1)
            pool.affine_select(out=own, in_=own, compare_op=ALU.is_ge, fill=1.0, base=2,
                               pattern=[[0, T]], channel_multiplier=-1).then_inc(s["sides_made"], 1)
            pool.wait_ge(s["sides_made"], 3)
            r.constants(pool)
            r.empty_rows(pool, g_.empty)

            def add_c(b):
                pool.wait_ge(s["xn_ready"], b.count(1, 1))
                row = xs[:, b.at(), :].rearrange("t o d -> t (o d)")
                nc.gpsimd.tensor_tensor(row, row, c_wide[:, :], ALU.add).then_inc(s["xc_ready"], 1)

            def step(b):
                if (b - 4).real():
                    r.rstd(pool, b - 4)
                if (b + 1).real():
                    ln(b + 1)
                if (b - 2).real():
                    if not b.looped() and b.c == 2:
                        pool.wait_ge(s["c_ready"], 1)
                    add_c(b - 2)
                if b.real():
                    for k, (lo, hi, need) in enumerate(((S, KV + T, 5), (0, S, 6))):
                        pool.wait_ge(s["rest_done"], b.count(6, need))
                        pool.sem_inc(s["pool_turns"], 1)
                        nc.gpsimd.tensor_copy(parts[b.parity][:, 1, :, lo:hi], rest[:, :, lo:hi]).then_inc(s["mid_done"], 1)
                        pool.wait_ge(s["mid_done"], b.count(2, k + 1))
                        nc.gpsimd.tensor_tensor(parts[b.parity][:, 2, :, lo:hi], rest[:, :, lo:hi],
                                                parts[b.parity][:, 1, :, lo:hi], ALU.subtract).then_inc(s["low_done"], 1)
                if (b - 4).real():
                    r.scatter(pool, b - 4, r.rows, g_.sorted0, E0 * REGION)

            attention_steps(pool, step)
            r.scattered_all(pool)

        @block.scalar
        def _(act):
            def mixed_out(n, u):
                act.wait_ge(s["mixed_mm"], n.count(2, u + 1))
                if (n - 1).real():
                    act.wait_ge(s["wo_mm"], (n - 1).count(1, 1))
                nc.scalar.copy(mixed[:, u, :], bank[6 + u][:, 0:T]).then_inc(s["mixed_ready"], 1)

            def high_k(b, h):
                nc.scalar.activation(parts[b.parity][:, 0, h, 0:S], bank[(0, 3)[h]][:, 0:S], ACT.Identity,
                                     bias=bias_t[:, 4 + h:5 + h]).then_inc(s["high_done"], 1)

            def step(b):
                if (b - 3).real():
                    n = b - 3
                    for k in range(16):
                        keys = T if k % 4 == 0 else CHUNKS[k % 4 - 1][1]
                        act.wait_ge(s["logits_mm"], n.count(16, k + 1))
                        act.wait_ge(s["pv_done"], n.count(16, max(k - 3, 0)))
                        src = bank[4 + k % 2][0:keys, 0:4 * T].rearrange("p (j q) -> p j q", j=4)
                        nc.scalar.activation(probs[k % 4][0:keys, :, :], src, ACT.Exp, scale=DH ** -0.5).then_inc(s["exp_done"], 1)
                        if k in (10, 15):
                            u = 0 if k == 10 else 1
                            act.wait_ge(s["pv_done"], n.count(16, 8 * (u + 1)))
                            if (n - 1).real():
                                act.wait_ge(s["turned_mm"], (n - 1).count(2, u + 1))
                            nc.scalar.copy(pv[u][:, :, :, :].rearrange("p g s t -> p (g s t)"), bank[6 + u][:, 0:4 * T]).then_inc(s["pv_out"], 1)
                    mixed_out(n, 0)
                if b.real():
                    act.wait_ge(s["xt_mm"], b.count(1, 1))
                    if (b - 2).real():
                        act.wait_ge(s["v23_mm"], (b - 2).count(1, 1))
                    nc.scalar.copy(xt[b.parity][:, :, :], bank[0][:, 0:2 * T].rearrange("p (a t) -> p a t", a=2)).then_inc(s["xt_ready"], 1)
                    act.wait_ge(s["ct_mm"], b.count(1, 1))
                    if (b - 2).real():
                        act.wait_ge(s_spill[b.parity], (b - 2).turn(16, 16))
                    for h in range(2):
                        nc.scalar.copy(ct[b.parity][:, h, :], bank[1 + h][:, 0:S]).then_inc(s["ct_ready"], 1)
                if (b - 4).real():
                    r.copy_in(act, b - 4)
                if (b - 2).real():
                    n = b - 2
                    act.wait_ge(s["mt_mm"], n.count(1, 1))
                    if (b - 3).real():
                        act.wait_ge(s_mw[(b - 3).parity], (b - 3).turn(16, 16))
                    nc.scalar.copy(mt[:, :], bank[3][0:QK, 256:256 + T // 2].bitcast(BF16)).then_inc(s["mt_ready"], 1)
                if (b - 1).real():
                    n = b - 1
                    act.wait_ge(s["v01_mm"], n.count(1, 1))
                    nc.scalar.copy(v[n.parity][:, 0:2, :, 0:DH],
                                   bank[0][:, :].rearrange("p (c h d) -> p c h d", c=2, h=H)).then_inc(s["v_ready"], 1)
                    act.wait_ge(s["v23_mm"], n.count(1, 1))
                    last_rows = CHUNKS[2][1]
                    nc.scalar.copy(v[n.parity][0:last_rows, 2, :, 0:DH],
                                   bank[1][0:last_rows, 0:D].rearrange("p (h d) -> p h d", h=H)).then_inc(s["v_ready"], 1)
                    nc.scalar.copy(v[n.parity][0:T, 3, :, 0:DH],
                                   bank[1][0:T, D:2 * D].rearrange("p (h d) -> p h d", h=H)).then_inc(s["v_ready"], 1)
                if (b - 3).real():
                    mixed_out(b - 3, 1)
                if b.real():
                    if (b - 2).real():
                        act.wait_ge(s_parts[b.parity], (b - 2).turn(16, 16))
                    if not b.looped() and b.c == 0:
                        act.wait_ge(s["bias_loaded"], 16 * 6)
                    act.wait_ge(s["ka1_mm"], b.count(1, 1))
                    high_k(b, 1)
                    act.wait_ge(s["qk_mm"], b.count(1, 1))
                    for h in range(2):
                        for o, col in enumerate((S, KV)):
                            nc.scalar.activation(parts[b.parity][:, 0, h, col:col + T], bank[2][:, (2 * h + o) * T:(2 * h + o + 1) * T],
                                                 ACT.Identity, bias=bias_t[:, (2, 0)[o] + h:(2, 0)[o] + h + 1]).then_inc(s["high_done"], 1)
                    act.wait_ge(s["ka0_mm"], b.count(1, 1))
                    high_k(b, 0)
                    if not b.looped() and b.c == 1:
                        act.wait_ge(s["g_limit"], 1)
                        for o, sign in enumerate((1.0, -1.0)):
                            nc.scalar.activation(inv_gate[:, o, :], g_wide[:, :], ACT.Exp, scale=sign).then_inc(s["g_exp"], 1)
                        act.wait_ge(s["bv_mm"], 1)
                        nc.scalar.copy(bv_t[:, :, :], bank[4][:, 0:2 * T].rearrange("p (a t) -> p a t", a=2)).then_inc(s["bv_t"], 1)
                        act.wait_ge(s["sides_made"], 3)
                        for p in range(2):
                            wide = sides[QK:ROWS, :].rearrange("k (o n) -> k o n", o=1).broadcast_to((ROWS - QK, H, KV))
                            nc.scalar.copy(k_stack[p][QK:ROWS, :, :], wide).then_inc(s["sides_ready"], 1)

            attention_steps(act, step)

        @block.vector
        def _(dve):
            def ln(b):
                if not b.looped() and b.c <= 2:
                    dve.wait_ge(s[f"x{b.c}_loaded"], 16)
                row = xs[:, b.at(), :].rearrange("t o d -> t (o d)")
                nc.vector.bn_stats(ln_stats[:, :], row).then_inc(s["ln_stats_ready"], 1)
                dve.wait_ge(s["ln_stats_ready"], b.count(1, 1))
                dve.sem_inc(s["dve_turns"], 1)
                nc.vector.bn_aggr(ln_mv[:, :], ln_stats[:, :]).then_inc(s["ln_mv_ready"], 1)
                dve.wait_ge(s["ln_rstd_ready"], b.count(1, 1))
                if (b - 2).real():
                    dve.wait_ge(s["xt_mm"], (b - 2).count(1, 1))
                nc.vector.tensor_scalar(xn[b.parity][:, :], row, ln_mv[:, 0:1], ln_rstd[:, 1:2],
                                        ALU.subtract, ALU.mult).then_inc(s["xn_ready"], 1)

            ln(Item(0, 0, B))

            def gates():
                dve.wait_ge(s["out_loaded"], 16 * 5)
                nc.vector.tensor_scalar(g_wide[:, :], g_wide[:, :], -80.0, 80.0, ALU.max, ALU.min).then_inc(s["g_limit"], 1)
                dve.wait_ge(s["g_exp"], 2)
                nc.vector.tensor_scalar(inv_gate[:, :, :], inv_gate[:, :, :], 1.0, None, ALU.add).then_inc(s["inv_gate_ready"], 1)
                dve.wait_ge(s["inv_gate_ready"], 1)
                nc.vector.reciprocal(gate[:, :, :], inv_gate[:, :, :]).then_inc(s["gate_step"], 1)
                dve.wait_ge(s["gate_step"], 1)
                for o in range(2):
                    row = bv[o].rearrange("t (h d) -> t h d", h=H)
                    wide = gate[0:T, o, :].rearrange("t (h o) -> t h o", o=1).broadcast_to((T, H, DH))
                    nc.vector.tensor_tensor(row, row, wide, ALU.mult).then_inc(s["gate_step"], 1)
                dve.wait_ge(s["gate_step"], 3)
                nc.vector.tensor_tensor(bv_mix[:, :], bv[0], bv[1], ALU.add).then_inc(s["bv_mix"], 1)
                for p in range(2):
                    for c in range(NC + 1):
                        o = 0 if c == NC else 1
                        nc.vector.tensor_copy(v[p][:, c, :, DH:2 * DH], inv_gate[:, o, :].rearrange("k (h o) -> k h o", o=1).broadcast_to((P, H, DH))).then_inc(s["inv_gate_ready"], 1)

            def normalise(n, u):
                dve.wait_ge(s["turned_mm"], n.count(2, u + 1))
                if (n - 1).real():
                    dve.wait_ge(s["mixed_mm"], n.count(2))
                dve.sem_inc(s["dve_turns"], 1)
                turned = bank[6 + u][0:T, :].rearrange("t (k d) -> t k d", k=H)
                nc.vector.reciprocal(inv_sum[u][:, :].rearrange("t (k o) -> t k o", o=1), turned[:, :, DH:DH + 1]).then_inc(s["inverted"], 1)
                dve.wait_ge(s["inverted"], n.count(2, u + 1))
                nc.vector.tensor_tensor(normed[:, :, :, :].rearrange("t g s (j d) -> t (g s j) d", d=DH), turned[:, :, 0:DH],
                                        inv_sum[u][:, :].rearrange("t (k o) -> t k o", o=1).broadcast_to((T, H, DH)), ALU.mult).then_inc(s["scaled"], 1)
                dve.wait_ge(s["scaled"], n.count(2, u + 1))
                nc.vector.tensor_tensor(mixed_rows[:, u, :].rearrange("t (g d) -> t g d", g=2), normed[:, :, 0, :], normed[:, :, 1, :],
                                        ALU.add).then_inc(s["mixed_made"], 1)

            def rest_k(b, h):
                nc.vector.scalar_tensor_tensor(out=rest[:, h, 0:S], in0=bank[(0, 3)[h]][:, 0:S], scalar=bias_t[:, 4 + h:5 + h],
                                               in1=parts[b.parity][:, 0, h, 0:S], op0=ALU.add, op1=ALU.subtract).then_inc(s["rest_done"], 1)

            def rest_qk(b):
                for h in range(2):
                    for o, col in enumerate((S, KV)):
                        nc.vector.scalar_tensor_tensor(out=rest[:, h, col:col + T], in0=bank[2][:, (2 * h + o) * T:(2 * h + o + 1) * T],
                                                       scalar=bias_t[:, (2, 0)[o] + h:(2, 0)[o] + h + 1], in1=parts[b.parity][:, 0, h, col:col + T],
                                                       op0=ALU.add, op1=ALU.subtract).then_inc(s["rest_done"], 1)

            def step(b):
                for k in range(8):
                    if (b - 2).real():
                        n = b - 2
                        dve.wait_ge(s["scored"], n.count(8, k + 1))
                        if k == 0 and (n - 1).real():
                            dve.wait_ge(s["msplit"], n.count(4))
                        pair, h = 2 - 2 * (k % 2), 2 * k
                        nc.vector.tensor_reduce(neg_max[:, 0, h:h + 2], psum[0:T, pair:pair + 2, 0:S], AX, ALU.max, negate=True)
                        nc.vector.tensor_reduce(neg_max[:, 1, h:h + 2], psum[0:T, pair:pair + 2, S:KV], AX, ALU.max, negate=True).then_inc(s["max_done"], 1)
                    if (b - 3).real():
                        if k == 6:
                            normalise(b - 3, 0)
                    if (b - 4).real():
                        if k == 1:
                            r.stats(dve, b - 4, xs, s["x1_ready"])
                        if k == 5:
                            r.norm(dve, b - 4, xs)
                if (b - 2).real():
                    n = b - 2
                    dve.wait_ge(s["max_done"], n.count(8, 8))
                    if (n - 1).real():
                        dve.wait_ge(s["mt_mm"], n.count())
                    nc.vector.tensor_copy(max_parts[:, :, 0, :], neg_max[:, :, :]).then_inc(s["msplit"], 1)
                    dve.wait_ge(s["msplit"], n.count(4, 1))
                    nc.vector.tensor_tensor(max_rest[:, :, :], neg_max[:, :, :], max_parts[:, :, 0, :], ALU.subtract).then_inc(s["msplit"], 1)
                    dve.wait_ge(s["msplit"], n.count(4, 2))
                    nc.vector.tensor_copy(max_parts[:, :, 1, :], max_rest[:, :, :]).then_inc(s["msplit"], 1)
                    dve.wait_ge(s["msplit"], n.count(4, 3))
                    nc.vector.tensor_tensor(max_parts[:, :, 2, :], max_rest[:, :, :], max_parts[:, :, 1, :], ALU.subtract).then_inc(s["msplit"], 1)
                if (b - 3).real():
                    normalise(b - 3, 1)
                if (b + 1).real():
                    ln(b + 1)
                if (b - 4).real():
                    r.choose(dve, b - 4, r.bias[:, :])
                if b.real():
                    if (b - 1).real():
                        dve.wait_ge(s["low_done"], b.count(2))
                    for h in (1, 0):
                        if h == 1:
                            dve.wait_ge(s["high_done"], b.count(6, 1))
                        else:
                            dve.wait_ge(s["high_done"], b.count(6, 6))
                        rest_k(b, h)
                        if h == 1:
                            dve.wait_ge(s["high_done"], b.count(6, 5))
                            rest_qk(b)
                if (b - 4).real():
                    r.place_rows(dve, b - 4)
                    r.place_done(b - 4)
                if (b - 3).real():
                    n = b - 3
                    dve.wait_ge(s["wo_mm"], n.count(1, 1))
                    dve.wait_ge(s["xc_ready"], n.count(1, 1))
                    row = xs[:, n.at(), :].rearrange("t o d -> t (o d)")
                    nc.vector.tensor_tensor(row, bank[1][0:T, 0:D], row, ALU.add).then_inc(s["x1_ready"], 1)
                if not b.looped() and b.c == 1:
                    gates()
                    dve.wait_ge(s["c_mm"], 1)
                    nc.vector.tensor_tensor(c_wide[:, :], bank[5][0:T, 0:D], c_wide[:, :], ALU.add).then_inc(s["c_ready"], 1)

            attention_steps(dve, step)

        @block.tensor
        def _(pe):
            pe.wait_ge(s["consts"], 6)

            def constant_row():
                pe.wait_ge(s["bv_mix"], 1)
                for h in range(2):
                    last = nc.tensor.transpose(bank[4][:, h * T:(h + 1) * T], bv_mix[:, h * P:(h + 1) * P], ident[0:T, 0:T])
                last.then_inc(s["bv_mm"], 1)
                pe.wait_ge(s["bv_t"], 1)
                for h in range(2):
                    last = nc.tensor.matmul(bank[5][0:T, 0:D], bv_t[:, h, :], wo[:, h, :], start=(h == 0), stop=(h == 1))
                last.then_inc(s["c_mm"], 1)

            def turn(n, u):
                pe.wait_ge(s["pv_out"], n.count(2, u + 1))
                for g in range(2):
                    for o in range(2):
                        k = 2 * g + o
                        last = nc.tensor.transpose(bank[6 + u][0:T, k * P:(k + 1) * P], pv[u][:, g, o, :], ident[:, :])
                last.then_inc(s["turned_mm"], 1)

            def turn_back(n, u):
                pe.wait_ge(s["mixed_made"], n.count(2, u + 1))
                nc.tensor.transpose(bank[6 + u][:, 0:T], mixed_rows[:, u, :], ident[0:T, 0:T]).then_inc(s["mixed_mm"], 1)

            def max_scores(n, k):
                if k == 0:
                    pe.wait_ge(s_stack[n.parity], n.turn(192, 192))
                    if (n + 1).real():
                        pe.wait_ge(s["rest_done"], n.count(6, 11))
                if k == 1:
                    if (n + 1).real():
                        pe.wait_ge(s["rest_done"], n.count(6, 12))
                    pe.wait_ge(s["v_ready"], n.count(3, 3))
                    if (n - 2).real():
                        pe.wait_ge(s["x1_ready"], (n - 2).count(1, 1))
                if k >= 2:
                    pe.wait_ge(s["max_done"], n.count(8, k - 1))
                for j in range(2):
                    h = 2 * k + j
                    last = nc.tensor.matmul(bank[2 - 2 * (k % 2) + j][0:T, 0:KV], q_stack[n.parity][0:QK, h, :],
                                            k_stack[n.parity][0:QK, h, :], start=True, stop=True)
                last.then_inc(s["scored"], 1)

            def logits(n, k):
                g, c = k // 4, k % 4
                if k < 2 and (n - 2).real():
                    pe.wait_ge(*(r.logits_read(n - 2) if k == 0 else r.counts_read(n - 2)))
                if k >= 2:
                    pe.wait_ge(s["exp_done"], n.count(16, k - 1))
                lo, keys = (S, T) if c == 0 else CHUNKS[c - 1]
                for j in range(4):
                    h = 4 * g + j
                    last = nc.tensor.matmul(bank[4 + k % 2][0:keys, j * T:(j + 1) * T], k_stack[n.parity][:, h, lo:lo + keys],
                                            q_stack[n.parity][:, h, :], start=True, stop=True)
                last.then_inc(s["logits_mm"], 1)

            def values(n, k):
                g, c = k // 4, k % 4
                pe.wait_ge(s["exp_done"], n.count(16, k + 1))
                if k in (0, 8) and (n - 1).real():
                    pe.wait_ge(s["mixed_ready"], (n - 1).count(2, k // 8 + 1))
                keys, chunk, o = (T, 3, 0) if c == 0 else (CHUNKS[c - 1][1], c - 1, 1)
                for j in range(4):
                    h = 4 * g + j
                    col = (2 * (g % 2) + o) * T
                    last = nc.tensor.matmul(bank[6 + g // 2][32 * j:32 * j + 32, col:col + T], v[n.parity][0:keys, chunk, h, :],
                                            probs[k % 4][0:keys, j, :], start=(c <= 1), stop=(c == 0 or c == 3))
                last.then_inc(s["pv_done"], 1)

            def turn_context(b, h):
                for c, (lo, keys) in enumerate(CHUNKS):
                    last = nc.tensor.transpose(bank[1 + h][:, lo:lo + keys], ctx_in[b.parity][0:keys, c, h * P:(h + 1) * P],
                                               ident[0:keys, 0:keys])
                return last

            def keys_of(b, h):
                for a_ in range(2):
                    last = nc.tensor.matmul(bank[(0, 3)[h]][:, 0:S], w_aux[:, a_, h * P:(h + 1) * P], ct[b.parity][:, a_, :],
                                            start=(a_ == 0), stop=(a_ == 1))
                last.then_inc(s[f"ka{h}_mm"], 1)

            def step(b):
                if (b - 3).real():
                    n = b - 3
                    if not b.looped() and b.c == 3:
                        pe.wait_ge(s["c_ready"], 1)
                        pe.wait_ge(s["sides_ready"], 1)
                        pe.wait_ge(s["inv_gate_ready"], 9)
                    if not b.looped() and b.c == 4:
                        pe.wait_ge(s["sides_ready"], 2)
                    pe.wait_ge(s_mr[n.parity], n.turn(16, 16))
                for k in range(16):
                    if (b - 3).real():
                        logits(b - 3, k)
                    if (b - 2).real() and k % 2 == 0:
                        max_scores(b - 2, k // 2)
                    if (b - 3).real() and k >= 1:
                        values(b - 3, k - 1)
                        if k == 12:
                            turn(b - 3, 0)
                if b.real():
                    if (b - 2).real():
                        pe.wait_ge(s["max_done"], (b - 2).count(8, 7))
                    elif (b - 1).real():
                        pe.wait_ge(s["rest_done"], 6)
                    pe.wait_ge(s_ctx[b.parity], b.turn(32, 32))
                    turn_context(b, 1)
                if (b - 4).real():
                    if (b - 3).real():
                        pe.wait_ge(s["exp_done"], (b - 3).count(16, 15))
                    r.turn(pe, b - 4, ident)
                if (b - 3).real():
                    values(b - 3, 15)
                    turn_back(b - 3, 0)
                if b.real():
                    pe.wait_ge(s["xn_ready"], b.count(1, 1))
                    if (b - 2).real():
                        pe.wait_ge(s["max_done"], (b - 2).count(8, 8))
                    elif (b - 1).real():
                        pe.wait_ge(s["rest_done"], 6)
                    for h in range(2):
                        last = nc.tensor.transpose(bank[0][:, h * T:(h + 1) * T], xn[b.parity][:, h * P:(h + 1) * P], ident[0:T, 0:T])
                    last.then_inc(s["xt_mm"], 1)
                    turn_context(b, 0).then_inc(s["ct_mm"], 1)
                if (b - 2).real():
                    n = b - 2
                    pe.wait_ge(s["msplit"], n.count(4, 4))
                    pe.wait_ge(s["max_done"], n.count(8, 8))
                    nc.tensor.transpose(bank[3][0:QK, 256:256 + T // 2].bitcast(BF16), max_parts[:, :, :, :].rearrange("t s k h -> t (s k h)"),
                                        ident16[0:T, 0:T]).then_inc(s["mt_mm"], 1)
                if (b - 3).real():
                    turn(b - 3, 1)
                if (b - 1).real():
                    n = b - 1
                    if b.real():
                        pe.wait_ge(s["xt_ready"], b.count(1, 1))
                        pe.wait_ge(s["ct_ready"], b.count(2, 1))
                    else:
                        pe.wait_ge(s["max_done"], (b - 2).count(8, 8))
                    for c in range(2):
                        for h in range(2):
                            last = nc.tensor.matmul(bank[0][:, c * D:(c + 1) * D], ct[n.parity][:, h, c * P:(c + 1) * P],
                                                    w_aux[:, h, D:2 * D], start=(h == 0), stop=(h == 1))
                    last.then_inc(s["v01_mm"], 1)
                    for h in range(2):
                        nc.tensor.matmul(bank[1][0:CHUNKS[2][1], 0:D], ct[n.parity][:, h, 2 * P:S], w_aux[:, h, D:2 * D],
                                         start=(h == 0), stop=(h == 1))
                    for h in range(2):
                        last = nc.tensor.matmul(bank[1][0:T, D:2 * D], xt[n.parity][:, h, :], w_x[:, h, 2 * D:3 * D],
                                                start=(h == 0), stop=(h == 1))
                    last.then_inc(s["v23_mm"], 1)
                if (b - 4).real():
                    r.score(pe, b - 4)
                if (b - 3).real():
                    turn_back(b - 3, 1)
                if b.real():
                    pe.wait_ge(s["xt_ready"], b.count(1, 1))
                    pe.wait_ge(s["ct_ready"], b.count(2, 2))
                    if (b - 2).real():
                        pe.wait_ge(s["mt_ready"], (b - 2).count(1, 1))
                    if not b.looped() and b.c == 0:
                        pe.wait_ge(s["w_loaded"], 32)
                    keys_of(b, 1)
                    for h in range(2):
                        for o in range(2):
                            col = (1 - o) * D + h * P
                            for a_ in range(2):
                                last = nc.tensor.matmul(bank[2][:, (2 * h + o) * T:(2 * h + o + 1) * T], w_x[:, a_, col:col + P],
                                                        xt[b.parity][:, a_, :], start=(a_ == 0), stop=(a_ == 1))
                    last.then_inc(s["qk_mm"], 1)
                    if (b - 1).real():
                        pe.wait_ge(s["v_ready"], (b - 1).count(3, 1))
                    keys_of(b, 0)
                if (b - 4).real():
                    r.count(pe, b - 4)
                if (b - 3).real():
                    n = b - 3
                    if (b - 1).real():
                        pe.wait_ge(s["v_ready"], (b - 1).count(3, 3))
                    pe.wait_ge(s["mixed_ready"], n.count(2, 2))
                    for h in range(2):
                        last = nc.tensor.matmul(bank[1][0:T, 0:D], mixed[:, h, :], wo[:, h, :], start=(h == 0), stop=(h == 1))
                    last.then_inc(s["wo_mm"], 1)
                if not b.looped() and b.c == 1:
                    constant_row()

            attention_steps(pe, step)


def batch_routing(nc, g, phase, experts, region, tag, scores, scored, counts, acc):
    def sb(name, shape, dt=F32):
        return g.sb(f"{tag}_{name}", shape, dt, phase)

    r = Shared()
    r.number = sb("number", [T, B])
    r.down = sb("down", [T, experts])
    r.before = sb("before", [T, T], BF16)
    r.ones = sb("ones", [T, T], BF16)
    r.logits = sb("logits", [T, experts])
    r.best = sb("best", [T, 1])
    r.cand = sb("cand", [T, experts])
    r.first = sb("first", [T, 1])
    r.onehot = sb("onehot", [T, experts], BF16)
    r.mine = sb("mine", [T, experts])
    r.over = sb("over", [T, 1])
    r.start = sb("start", [T, 1])
    r.place = sb("place", [T, 1])
    r.place_i = [sb(f"place_i{p}", [T, 1], I32) for p in range(2)]
    s = {n: g.sem(f"{tag}_{n}") for n in "made steps chosen started counted placed placing over pool_turns".split()}
    scattered = [g.sem(f"{tag}_scattered{p}") for p in range(2)]
    r.s, r.scattered = s, scattered
    CHOICE, PLACING = 4, 3

    def constants(pool):
        nc.gpsimd.iota(r.number[:, :], [[T, B]], base=0, channel_multiplier=1,
                       allow_small_or_imprecise_dtypes=True).then_inc(s["made"], 1)
        nc.gpsimd.iota(r.down[:, :], [[-1, experts]], base=experts, channel_multiplier=0,
                       allow_small_or_imprecise_dtypes=True).then_inc(s["made"], 1)
        nc.gpsimd.memset(r.ones[:, :], 1.0).then_inc(s["made"], 1)
        nc.gpsimd.memset(r.before[:, :], 1.0).then_inc(s["made"], 1)
        pool.wait_ge(s["made"], 4)
        nc.gpsimd.affine_select(out=r.before[:, :], in_=r.before[:, :], compare_op=ALU.is_gt, fill=0.0, base=0,
                                pattern=[[1, T]], channel_multiplier=-1).then_inc(s["made"], 1)
        nc.gpsimd.memset(acc[0][:, :], 0.0).then_inc(s["made"], 1)
        pool.wait_ge(s["made"], 6)

    def choose(dve, n, bias=None):
        if not n.looped() and n.c == 0:
            dve.wait_ge(s["made"], 6)
        dve.wait_ge(scored, n.count(1, 1))
        if bias is None:
            nc.vector.tensor_copy(r.logits[:, :], scores(n)).then_inc(s["steps"], 1)
        else:
            nc.vector.tensor_tensor(r.logits[:, :], scores(n), bias, ALU.add).then_inc(s["steps"], 1)
        dve.wait_ge(s["steps"], n.count(CHOICE, 1))
        nc.vector.tensor_reduce(r.best[:, :], r.logits[:, :], AX, ALU.max).then_inc(s["steps"], 1)
        dve.wait_ge(s["steps"], n.count(CHOICE, 2))
        nc.vector.scalar_tensor_tensor(out=r.cand[:, :], in0=r.logits[:, :], scalar=r.best[:, :], in1=r.down[:, :],
                                       op0=ALU.is_ge, op1=ALU.mult).then_inc(s["steps"], 1)
        dve.wait_ge(s["steps"], n.count(CHOICE, 3))
        nc.vector.tensor_reduce(r.first[:, :], r.cand[:, :], AX, ALU.max).then_inc(s["steps"], 1)
        dve.wait_ge(s["steps"], n.count(CHOICE, 4))
        nc.vector.tensor_scalar(r.onehot[:, :], r.down[:, :], r.first[:, :], None, ALU.is_equal).then_inc(s["chosen"], 1)
        nc.vector.tensor_scalar(r.start[:, :], r.first[:, :], -float(region), float(experts * region), ALU.mult, ALU.add).then_inc(s["started"], 1)

    def count(pe, n):
        pe.wait_ge(s["chosen"], n.count(1, 1))
        if (n - 1).real():
            pe.wait_ge(s["placing"], (n - 1).count(PLACING, 2))
        nc.tensor.matmul(counts, r.before[:, :], r.onehot[:, :], start=True, stop=False)
        nc.tensor.matmul(counts, r.ones[:, :], acc[n.parity][:, :], start=False, stop=True).then_inc(s["counted"], 1)

    def place_rows(dve, n, limit=None):
        dve.wait_ge(s["counted"], n.count(1, 1))
        nc.vector.tensor_tensor(acc[1 - n.parity][:, :], acc[n.parity][:, :], r.onehot[:, :], ALU.add).then_inc(s["placing"], 1)
        nc.vector.tensor_tensor(r.mine[:, :], counts, r.onehot[:, :], ALU.mult).then_inc(s["placing"], 1)
        dve.wait_ge(s["placing"], n.count(PLACING, 2))
        nc.vector.tensor_reduce(r.place[:, :], r.mine[:, :], AX, ALU.add).then_inc(s["placing"], 1)
        dve.wait_ge(s["placing"], n.count(PLACING, 3))
        dve.wait_ge(s["started"], n.count(1, 1))
        if limit is not None:
            nc.vector.tensor_scalar(r.over[:, :], r.place[:, :], float(limit), float(experts * region), ALU.is_ge, ALU.mult).then_inc(s["over"], 1)
            dve.wait_ge(s["over"], n.count(2, 1))
            nc.vector.tensor_tensor(r.start[:, :], r.start[:, :], r.over[:, :], ALU.add).then_inc(s["over"], 1)
            dve.wait_ge(s["over"], n.count(2, 2))

    def place_done(n):
        nc.vector.tensor_tensor(r.place_i[n.parity][:, :], r.place[:, :], r.start[:, :], ALU.add).then_inc(s["placed"], 1)

    def scatter(pool, n, rows, to, places):
        pool.wait_ge(s["placed"], n.count(1, 1))
        pool.sem_inc(s["pool_turns"], 1)
        pool.indirect_dma_start(out=to, out_offset=bass.IndirectOffsetOnAxis(r.place_i[n.parity][:, 0:1], 0),
                                in_=rows[n.parity][:, :], in_offset=None, bounds_check=places - 1,
                                oob_is_err=False).then_inc(scattered[n.parity], 16)

    def scattered_all(pool):
        for p in range(2):
            pool.wait_ge(scattered[p], 16 * B // 2)

    r.constants, r.choose, r.count, r.place_rows, r.place_done = constants, choose, count, place_rows, place_done
    r.scatter, r.scattered_all = scatter, scattered_all
    r.logits_read = lambda n: (s["steps"], n.count(CHOICE, 1))
    r.counts_read = lambda n: (s["placing"], n.count(PLACING, 2))
    return r


def router0(nc, g, phase, turn_bank, count_bank):
    def sb(name, shape, dt=F32):
        return g.sb(f"r0_{name}", shape, dt, phase)

    s = {n: g.sem(f"r0_{n}") for n in "loaded emptied stats mv eps rstd normed turned xt scored dve_turns".split()}
    scores = turn_bank[0:T, 2 * T:2 * T + E0]
    r = batch_routing(nc, g, phase, E0, REGION, "r0", lambda n: scores, s["scored"], count_bank[0:T, 0:E0], g.acc)
    r.w = sb("w", [P, 2, E0])
    r.bias = sb("bias", [T, E0])
    r.stat = sb("stat", [T, 6])
    r.mv = sb("mv", [T, 2])
    r.deviation = sb("deviation", [T, 2])
    r.rows = [sb(f"rows{p}", [T, ROW0]) for p in range(2)]
    r.xt = sb("xt", [P, 2, T])
    r.own = s
    acc, width = g.acc, ROW0

    def empty_rows(pool, empty):
        nc.gpsimd.memset(empty[:, 0:width - 1], 0.0).then_inc(s["emptied"], 1)
        nc.gpsimd.memset(empty[:, width - 1:width], float(N)).then_inc(s["emptied"], 1)
        pool.wait_ge(s["emptied"], 2)

    def stats(dve, n, xs, x_ready):
        dve.wait_ge(x_ready, n.count(1, 1))
        dve.sem_inc(s["dve_turns"], 1)
        nc.vector.bn_stats(r.stat[:, :], xs[:, n.at(), :].rearrange("t o d -> t (o d)")).then_inc(s["stats"], 1)
        dve.wait_ge(s["stats"], n.count(1, 1))
        dve.sem_inc(s["dve_turns"], 1)
        nc.vector.bn_aggr(r.mv[:, :], r.stat[:, :]).then_inc(s["mv"], 1)

    def rstd(pool, n):
        pool.wait_ge(s["mv"], n.count(1, 1))
        nc.gpsimd.tensor_tensor(r.deviation[:, 0:1], r.mv[:, 1:2], g.eps[0:T, :], ALU.add).then_inc(s["eps"], 1)
        pool.wait_ge(s["eps"], n.count(1, 1))
        nc.gpsimd.tensor_tensor(r.deviation[:, 1:2], r.deviation[:, 0:1], g.neg_half[0:T, :], ALU.pow).then_inc(s["rstd"], 1)

    def norm(dve, n, xs):
        dve.wait_ge(s["rstd"], n.count(1, 1))
        if (n - 2).real():
            dve.wait_ge(r.scattered[n.parity], (n - 2).turn(16, 16))
            dve.wait_ge(s["turned"], (n - 2).count(1, 1))
        nc.vector.tensor_scalar(r.rows[n.parity][:, 0:D], xs[:, n.at(), :].rearrange("t o d -> t (o d)"), r.mv[:, 0:1], r.deviation[:, 1:2],
                                ALU.subtract, ALU.mult).then_inc(s["normed"], 1)
        nc.vector.tensor_copy(r.rows[n.parity][:, width - 1:width], r.number[:, n.at()])

    def turn(pe, n, ident):
        pe.wait_ge(s["normed"], n.count(1, 1))
        for h in range(2):
            last = nc.tensor.transpose(turn_bank[:, h * T:(h + 1) * T], r.rows[n.parity][:, h * P:(h + 1) * P], ident[0:T, 0:T])
        last.then_inc(s["turned"], 1)

    def copy_in(act, n):
        act.wait_ge(s["turned"], n.count(1, 1))
        if (n - 1).real():
            act.wait_ge(s["scored"], (n - 1).count(1, 1))
        nc.scalar.copy(r.xt[:, :, :], turn_bank[:, 0:2 * T].rearrange("p (k t) -> p k t", k=2)).then_inc(s["xt"], 1)

    def score(pe, n):
        if not n.looped() and n.c == 0:
            pe.wait_ge(s["loaded"], 32)
        pe.wait_ge(s["xt"], n.count(1, 1))
        for h in range(2):
            last = nc.tensor.matmul(scores, r.xt[:, h, :], r.w[:, h, :], start=(h == 0), stop=(h == 1))
        last.then_inc(s["scored"], 1)

    r.empty_rows, r.stats, r.rstd, r.norm, r.turn, r.copy_in, r.score = empty_rows, stats, rstd, norm, turn, copy_in, score
    return r


def ffn0(nc, a, g):
    bank = g.bank
    K2 = F0 // P
    with ExitStack() as phase:
        def sb(name, shape, dt=F32):
            return g.sb("f0_" + name, shape, dt, phase)

        weights = {n: sb(n, [P, 2, D]) for n in ("Wk", "Wv", "Wq", "Wo")}
        wo_t = sb("wo_t", [P, 2, D])
        bq = sb("bq", [P, 2])
        bv = sb("bv", [P, 2])
        bv_wide = sb("bv_wide", [P, 2, T])
        TABLE = 15
        SETUP = 5
        b2 = sb("b2", [P, E0, D])
        b1_rows = sb("b1_rows", [E0 * K2, P])
        b1 = sb("b1", [P, E0, K2])
        ones = sb("ones", [T, 1], BF16)
        tile_no = sb("tile_no", [1, TILES])
        edges = sb("edges", [1, ROW_TILES])
        regions = sb("regions", [1, E0])
        nexts = sb("nexts", [1, E0])
        nexts_i = sb("nexts_i", [1, E0], I32)
        taken = sb("taken", [1, E0])
        over = sb("over", [1, E0, ROW_TILES])
        one_row = sb("one_row", [1, E0])
        tiles_of = sb("tiles_of", [1, E0])
        tiles_to = sb("tiles_to", [1, E0])
        passed = sb("passed", [1, TILES, E0])
        ends = sb("ends", [1, TILES, E0])
        owner = sb("owner", [1, TILES])
        start = sb("start", [1, TILES])
        local = sb("local", [1, TILES])
        inside = sb("inside", [1, TILES])
        offset = sb("offset", [1, TILES])
        owner_i = sb("owner_i", [1, TILES], I32)
        offset_i = sb("offset_i", [1, TILES], I32)
        s = {n: g.sem("f0_" + n) for n in """qk_loaded vo_loaded biases_loaded b1_loaded b1_mm b1_made setup_mm setup_copy row_made loaded made summed step nexts_ready padded x_mm x_copy up up_copy back back_copy down down_copy
            index_ready sp_turns pool_turns""".split()}
        s_in = [g.sem(f"f0_tile_loaded{p}") for p in range(2)]
        s_out = [g.sem(f"f0_tile_stored{p}") for p in range(2)]

        def lay_out_pool(pool):
            for t, step, n in ((tile_no, 1, TILES), (edges, P, ROW_TILES), (regions, REGION, E0)):
                nc.gpsimd.iota(t[:, :], [[step, n]], base=0, channel_multiplier=0,
                               allow_small_or_imprecise_dtypes=True).then_inc(s["made"], 1)
            nc.gpsimd.memset(one_row[:, :], 1.0).then_inc(s["made"], 1)
            nc.gpsimd.memset(ones[:, :], 1.0).then_inc(s["made"], 1)
            for b_, n in ((bq, "L1_xattn_bq"), (bv, "L1_xattn_bv")):
                for k in range(2):
                    pool.dma_start(b_[:, k:k + 1], a[n][k * P:(k + 1) * P].rearrange("(p o) -> p o", o=1)).then_inc(s["biases_loaded"], 16)
            pool.dma_start(g.row[:, :], a["L1_xattn_bo"].rearrange("(o n) -> o n", o=1).broadcast_to((T, D))).then_inc(s["biases_loaded"], 16)
            pool.dma_start(g.wg[:, :, :], a["L1_ffn_Wg"].rearrange("(k p) e -> p k e", p=P)).then_inc(s["biases_loaded"], 16)
            pool.dma_start(b1_rows[:, :], a["L0_ffn_b1"].rearrange("e (f p) -> (e f) p", p=P)).then_inc(s["b1_loaded"], 16)
            pool.dma_start(b2[:, :, :], a["L0_ffn_b2"].rearrange("(o e) d -> o e d", o=1).broadcast_to((P, E0, D))).then_inc(s["loaded"], 16)

        def lay_out_pe(pe):
            pe.wait_ge(s["made"], 5)
            nc.tensor.matmul(bank[5][0:1, 0:E0], ones[:, :], g.acc[B % 2][:, :], start=True, stop=True).then_inc(s["summed"], 1)

            def product(to, left, right):
                for m in range(2):
                    for k in range(2):
                        last = nc.tensor.matmul(to[:, m * D:(m + 1) * D], left[:, k, m * P:(m + 1) * P], right[:, k, :],
                                                start=(k == 0), stop=(k == 1))
                return last

            pe.wait_ge(s["qk_loaded"], 32)
            product(bank[1], weights["Wq"], weights["Wk"]).then_inc(s["setup_mm"], 1)
            pe.wait_ge(s["vo_loaded"], 32)
            for k in range(2):
                for m in range(2):
                    last = nc.tensor.transpose(bank[0][:, k * D + m * P:k * D + (m + 1) * P], weights["Wo"][:, m, k * P:(k + 1) * P], g.ident[:, :])
            last.then_inc(s["setup_mm"], 1)
            pe.wait_ge(s["biases_loaded"], 16 * 6)
            for m in range(2):
                for k in range(2):
                    last = nc.tensor.matmul(bank[3][:, m:m + 1], weights["Wk"][:, k, m * P:(m + 1) * P], bq[:, k:k + 1],
                                            start=(k == 0), stop=(k == 1))
            last.then_inc(s["setup_mm"], 1)
            pe.wait_ge(s["setup_copy"], 1)
            product(bank[2], weights["Wv"], wo_t).then_inc(s["setup_mm"], 1)
            pe.wait_ge(s["setup_copy"], 3)
            for k in range(2):
                last = nc.tensor.matmul(bank[4][0:T, 0:D], bv_wide[:, k, :], wo_t[:, k, :], start=(k == 0), stop=(k == 1))
            last.then_inc(s["setup_mm"], 1)
            pe.wait_ge(s["b1_loaded"], 16)
            nc.tensor.transpose(bank[6][:, 0:E0 * K2], b1_rows[:, :], g.ident[0:E0 * K2, 0:E0 * K2]).then_inc(s["b1_mm"], 1)
            pe.wait_ge(s["step"], TABLE)
            pe.wait_ge(s["b1_made"], 1)
            pe.wait_ge(s["setup_copy"], SETUP)
            pe.wait_ge(s["row_made"], 1)

        def pad(engine, experts):
            engine.wait_ge(s["nexts_ready"], 1)
            for e in experts:
                at = engine.value_load(nexts_i[0:1, e:e + 1], min_val=0, max_val=E0 * REGION - P)
                engine.dma_start(g.sorted0[bass.ds(at, P), :], g.empty[:, :]).then_inc(s["padded"], 16)

        def lay_out_sp(sp):
            for n in ("Wq", "Wk", "Wo", "Wv"):
                loaded = s["qk_loaded"] if n in ("Wq", "Wk") else s["vo_loaded"]
                sp.dma_start(weights[n][:, :, :], a["L1_xattn_" + n].rearrange("(k p) d -> p k d", p=P)).then_inc(loaded, 16)
            pad(sp, range(0, E0 // 2))
            sp.wait_ge(s["padded"], 16 * E0)
            sp.wait_ge(s["step"], TABLE)

        def lay_out_act(act):
            pad(act, range(E0 // 2, E0))
            act.wait_ge(s["setup_mm"], 2)
            nc.scalar.copy(wo_t[:, :, :], bank[0][:, :].rearrange("p (k d) -> p k d", k=2)).then_inc(s["setup_copy"], 1)
            nc.scalar.copy(g.w_qk[:, :, :], bank[1][:, :].rearrange("p (k d) -> p k d", k=2)).then_inc(s["setup_copy"], 1)
            act.wait_ge(s["biases_loaded"], 16 * 6)
            nc.scalar.copy(bv_wide[:, :, :], bv[:, :].rearrange("p (k o) -> p k o", o=1).broadcast_to((P, 2, T))).then_inc(s["setup_copy"], 1)
            act.wait_ge(s["setup_mm"], 4)
            nc.scalar.mul(g.u[:, :], bank[3][:, 0:2], D ** -0.5).then_inc(s["setup_copy"], 1)
            nc.scalar.copy(g.w_vo[:, :, :], bank[2][:, :].rearrange("p (k d) -> p k d", k=2)).then_inc(s["setup_copy"], 1)
            act.wait_ge(s["setup_copy"], SETUP)
            act.wait_ge(s["step"], TABLE)
            act.wait_ge(s["b1_made"], 1)

        def lay_out_dve(dve):
            step = s["step"]
            vec = nc.vector

            def wide(t, rows, to):
                pattern = "t (o e) -> t o e" if rows else "t (j o) -> t j o"
                return t[:, :].rearrange(pattern, o=1).broadcast_to(to)

            dve.wait_ge(s["made"], 5)
            dve.wait_ge(s["summed"], 1)
            vec.tensor_tensor(nexts[:, :], bank[5][0:1, 0:E0], regions[:, :], ALU.add).then_inc(step, 1)
            dve.wait_ge(step, 1)
            vec.tensor_copy(nexts_i[:, :], nexts[:, :]).then_inc(s["nexts_ready"], 1)
            vec.tensor_copy(taken[:, :], bank[5][0:1, 0:E0]).then_inc(step, 1)
            dve.wait_ge(step, 2)
            vec.tensor_tensor(over[:, :, :], wide(taken, False, (1, E0, ROW_TILES)), wide(edges, True, (1, E0, ROW_TILES)),
                              ALU.is_gt).then_inc(step, 1)
            dve.wait_ge(step, 3)
            vec.tensor_reduce(tiles_of[:, :], over[:, :, :], AX, ALU.add).then_inc(step, 1)
            dve.wait_ge(step, 4)
            vec.tensor_tensor_scan(tiles_to[:, :], one_row[:, :], tiles_of[:, :], 0.0, ALU.mult, ALU.add).then_inc(step, 1)
            dve.wait_ge(step, 5)
            vec.tensor_tensor(passed[:, :, :], wide(tiles_to, True, (1, TILES, E0)), wide(tile_no, False, (1, TILES, E0)),
                              ALU.is_le).then_inc(step, 1)
            dve.wait_ge(step, 6)
            vec.tensor_reduce(owner[:, :], passed[:, :, :], AX, ALU.add).then_inc(step, 1)
            vec.tensor_tensor(ends[:, :, :], passed[:, :, :], wide(tiles_to, True, (1, TILES, E0)), ALU.mult).then_inc(step, 1)
            dve.wait_ge(step, 8)
            vec.tensor_reduce(start[:, :], ends[:, :, :], AX, ALU.max).then_inc(step, 1)
            vec.tensor_scalar(inside[:, :], owner[:, :], float(E0), float(P), ALU.is_lt, ALU.mult).then_inc(step, 1)
            vec.tensor_scalar(owner_i[:, :], owner[:, :], float(E0 - 1), None, ALU.min).then_inc(step, 1)
            dve.wait_ge(step, 9)
            vec.tensor_tensor(local[:, :], tile_no[:, :], start[:, :], ALU.subtract).then_inc(step, 1)
            dve.wait_ge(step, 12)
            vec.tensor_tensor(local[:, :], local[:, :], inside[:, :], ALU.mult).then_inc(step, 1)
            dve.wait_ge(step, 13)
            vec.scalar_tensor_tensor(out=offset[:, :], in0=owner[:, :], scalar=float(REGION), in1=local[:, :],
                                     op0=ALU.mult, op1=ALU.add).then_inc(step, 1)
            dve.wait_ge(step, 14)
            vec.tensor_copy(offset_i[:, :], offset[:, :]).then_inc(step, 1)
            dve.wait_ge(step, 15)
            dve.wait_ge(s["b1_mm"], 1)
            vec.tensor_copy(b1[:, :, :], bank[6][:, 0:E0 * K2].rearrange("p (e f) -> p e f", e=E0)).then_inc(s["b1_made"], 1)
            dve.wait_ge(s["b1_made"], 1)
            dve.wait_ge(s["setup_mm"], 5)
            vec.tensor_tensor(g.row[:, :], bank[4][0:T, 0:D], g.row[:, :], ALU.add).then_inc(s["row_made"], 1)
            dve.wait_ge(s["row_made"], 1)

        with ExitStack() as tiles:
            def tb(name, shape, dt=F32):
                return g.sb(name, shape, dt, tiles)

            x_in = [tb(f"t0_in{p}", [P, ROW0]) for p in range(2)]
            index = [tb(f"t0_index{p}", [P, 1], I32) for p in range(4)]
            xt2 = [tb(f"t0_xt{p}", [P, 2, P]) for p in range(2)]
            up = [tb(f"t0_up{p}", [P, F0]) for p in range(2)]
            hid = [tb(f"t0_hid{p}", [P, K2, P]) for p in range(2)]
            y = [tb(f"t0_y{p}", [P, D]) for p in range(2)]
            end = TILES + 2

            def tile_steps(engine, step):
                steps(engine, step, TILES, 6, TILES - 3, end, 4)

            block = nc.Block()
            with block:
                @block.sync
                def _(sp):
                    def load(j):
                        at = sp.value_load(offset_i[0:1, j.at()], min_val=0, max_val=E0 * REGION)
                        if (j - 2).real():
                            sp.wait_ge(s["x_mm"], (j - 2).count(1, 1))
                            sp.sem_inc(s["sp_turns"], 1)
                            sp.wait_ge(s["index_ready"], (j - 2).count(1, 1))
                            sp.sem_inc(s["sp_turns"], 1)
                        sp.dma_start(x_in[j.parity][:, :], g.sorted0[bass.ds(at, P), :]).then_inc(s_in[j.parity], 16)

                    lay_out_sp(sp)
                    load(Item(0, 0, TILES))
                    load(Item(0, 1, TILES))

                    def step(j):
                        if (j + 2).real():
                            load(j + 2)

                    tile_steps(sp, step)

                @block.gpsimd
                def _(pool):
                    def step(j):
                        if j.real():
                            pool.wait_ge(s_in[j.parity], j.turn(16, 16))
                            pool.sem_inc(s["pool_turns"], 1)
                            if (j - 4).real():
                                pool.wait_ge(s_out[j.parity], (j - 4).turn(16, 16))
                                pool.sem_inc(s["pool_turns"], 1)
                            nc.gpsimd.tensor_copy(index[j.quarter][:, :], x_in[j.parity][:, D:D + 1]).then_inc(s["index_ready"], 1)
                        if (j - 2).real():
                            n = j - 2
                            pool.wait_ge(s["index_ready"], n.count(1, 1))
                            pool.wait_ge(s["down_copy"], n.count(1, 1))
                            pool.sem_inc(s["pool_turns"], 1)
                            pool.indirect_dma_start(out=g.made0, out_offset=bass.IndirectOffsetOnAxis(index[n.quarter][:, 0:1], 0),
                                                    in_=y[n.parity][:, :], in_offset=None, bounds_check=N - 1,
                                                    oob_is_err=False).then_inc(s_out[n.parity], 16)

                    lay_out_pool(pool)
                    tile_steps(pool, step)
                    pool.wait_ge(s_out[0], 16 * ((TILES + 1) // 2))
                    pool.wait_ge(s_out[1], 16 * (TILES // 2))

                @block.scalar
                def _(act):
                    def copy_in(j):
                        act.wait_ge(s["x_mm"], j.count(1, 1))
                        if (j - 2).real():
                            act.wait_ge(s["up"], (j - 2).count(1, 1))
                        nc.scalar.copy(xt2[j.parity][:, :, :], bank[2 + j.parity][:, 0:2 * P].rearrange("p (k t) -> p k t", k=2)).then_inc(s["x_copy"], 1)

                    lay_out_act(act)
                    copy_in(Item(0, 0, TILES))

                    def step(j):
                        if (j + 1).real():
                            copy_in(j + 1)
                        if (j - 1).real():
                            n = j - 1
                            e = act.value_load(owner_i[0:1, n.at()], min_val=0, max_val=E0 - 1)
                            act.wait_ge(s["back"], n.count(1, 1))
                            if (n - 2).real():
                                act.wait_ge(s["down"], (n - 2).count(1, 1))
                            for f in range(K2):
                                bias = b1[:, bass.ds(e, 1), f:f + 1].rearrange("p o f -> p (o f)")
                                nc.scalar.activation(hid[n.parity][:, f, :], bank[4 + n.parity][:, f * P:(f + 1) * P], ACT.Relu,
                                                     bias=bias).then_inc(s["back_copy"], 1)

                    tile_steps(act, step)

                @block.vector
                def _(dve):
                    def step(j):
                        if j.real():
                            dve.wait_ge(s["up"], j.count(1, 1))
                            if (j - 2).real():
                                dve.wait_ge(s["back"], (j - 2).count(1, 1))
                            nc.vector.tensor_copy(up[j.parity][:, :], bank[j.parity][:, :]).then_inc(s["up_copy"], 1)
                        if not j.looped() and j.c == 2:
                            dve.wait_ge(s["loaded"], 16)
                        if (j - 2).real():
                            n = j - 2
                            e = dve.value_load(owner_i[0:1, n.at()], min_val=0, max_val=E0 - 1)
                            dve.wait_ge(s["down"], n.count(1, 1))
                            if (n - 2).real():
                                dve.wait_ge(s_out[n.parity], (n - 2).turn(16, 16))
                            nc.vector.tensor_tensor(y[n.parity][:, :], bank[6 + n.parity][:, 0:D],
                                                    b2[:, bass.ds(e, 1), :].rearrange("p o d -> p (o d)"), ALU.add).then_inc(s["down_copy"], 1)

                    lay_out_dve(dve)
                    tile_steps(dve, step)

                @block.tensor
                def _(pe):
                    def transpose_in(j):
                        pe.wait_ge(s_in[j.parity], j.turn(16, 16))
                        if (j - 2).real():
                            pe.wait_ge(s["x_copy"], (j - 2).count(1, 1))
                        for h in range(2):
                            last = nc.tensor.transpose(bank[2 + j.parity][:, h * P:(h + 1) * P], x_in[j.parity][:, h * P:(h + 1) * P], g.ident[:, :])
                        last.then_inc(s["x_mm"], 1)

                    lay_out_pe(pe)
                    transpose_in(Item(0, 0, TILES))

                    def step(j):
                        if j.real():
                            e = pe.value_load(owner_i[0:1, j.at()], min_val=0, max_val=E0 - 1)
                            pe.wait_ge(s["x_copy"], j.count(1, 1))
                            if (j - 2).real():
                                pe.wait_ge(s["up_copy"], (j - 2).count(1, 1))
                            for h in range(2):
                                last = nc.tensor.matmul(bank[j.parity][:, :], xt2[j.parity][:, h, :],
                                                        g.w1[:, bass.ds(e, 1), h, :].rearrange("p o f -> p (o f)"), start=(h == 0), stop=(h == 1))
                            last.then_inc(s["up"], 1)
                        if (j + 1).real():
                            transpose_in(j + 1)
                        if (j - 2).real():
                            n = j - 2
                            e = pe.value_load(owner_i[0:1, n.at()], min_val=0, max_val=E0 - 1)
                            pe.wait_ge(s["back_copy"], n.count(K2, K2))
                            if (n - 2).real():
                                pe.wait_ge(s["down_copy"], (n - 2).count(1, 1))
                            for f in range(K2):
                                last = nc.tensor.matmul(bank[6 + n.parity][:, 0:D], hid[n.parity][:, f, :],
                                                        g.w2[:, bass.ds(e, 1), f, :].rearrange("p o d -> p (o d)"), start=(f == 0), stop=(f == K2 - 1))
                            last.then_inc(s["down"], 1)
                        if (j - 1).real():
                            n = j - 1
                            pe.wait_ge(s["up_copy"], n.count(1, 1))
                            if (n - 2).real():
                                pe.wait_ge(s["back_copy"], (n - 2).count(K2, K2))
                            for f in range(K2):
                                last = nc.tensor.transpose(bank[4 + n.parity][:, f * P:(f + 1) * P], up[n.parity][:, f * P:(f + 1) * P], g.ident[:, :])
                            last.then_inc(s["back"], 1)

                    tile_steps(pe, step)


def attention1(nc, a, out, g):
    bank, xs, ident = g.bank, g.xs, g.ident
    with ExitStack() as phase:
        def sb(name, shape, dt=F32):
            return g.sb("a1_" + name, shape, dt, phase)

        def pair(name, shape, dt=F32):
            return [sb(f"{name}{p}", shape, dt) for p in range(2)]

        def psem(name):
            return [g.sem(f"a1_{name}{p}") for p in range(2)]

        made = pair("made", [T, D])
        xn2, xn3 = pair("xn2", [T, D]), pair("xn3", [T, D])
        xt2, xt3 = pair("xt2", [P, 2, T]), pair("xt3", [P, 2, T])
        stats2, stats3 = sb("stats2", [T, 6]), sb("stats3", [T, 6])
        mv2, mv3 = sb("mv2", [T, 2]), sb("mv3", [T, 2])
        rstd2, rstd3 = sb("rstd2", [T, 2]), sb("rstd3", [T, 2])
        q = pair("q", [P, 2, T])
        ct = pair("ct", [P, 2, S])
        cin = pair("ctx", [KC, NC, D])
        w_qk, w_vo, u, row, wg = g.w_qk, g.w_vo, g.u, g.row, g.wg
        neg_max, total, inverse = pair("neg_max", [T, 1]), pair("total", [T, 1]), pair("inverse", [T, 1])
        prob = pair("prob", [T, S])
        prob_t = pair("prob_t", [KC, NC, T])
        mix = pair("mix", [P, 2, T])
        s = {n: g.sem("a1_" + n) for n in """x2 stats2 mv2 eps2 rstd2 xn2 xc t2 xt2 q_mm q scored maxed
            prob tp prob_t mix_mm mix out_mm inverse x3 stats3 mv3 eps3 rstd3 xn3 x3_stored rows shifted expd t3 xt3 logits_mm dve_turns sp_turns""".split()}
        s_ct, s_cin, s_made = psem("ct_loaded"), psem("ctx_loaded"), psem("made_loaded")
        acc = pair("acc", [T, E1], BF16)
        rows = pair("rows", [T, ROW1])
        shifted = sb("shifted", [T, E1])
        expd, sums = sb("expd", [T, E1]), sb("sums", [T, 1])
        r = batch_routing(nc, g, phase, E1, C1, "r1", lambda n: bank[7][0:T, n.rows(E1)], s["logits_mm"], bank[6][0:T, 2 * T:2 * T + E1], acc)
        block = nc.Block()
        with block:
            @block.sync
            def _(sp):
                def load_cin(b):
                    src = a["ctx_1024"][b.at()].rearrange("o (c k) d -> k (o c) d", k=KC)
                    sp.dma_start(cin[b.parity][:, :, :], src).then_inc(s_cin[b.parity], 16)

                def load_made(b):
                    if (b - 2).real():
                        sp.wait_ge(s["x2"], (b - 2).count(1, 1))
                        sp.sem_inc(s["sp_turns"], 1)
                    sp.dma_start(made[b.parity][:, :], g.made0[b.rows(T), :]).then_inc(s_made[b.parity], 16)

                def load_ct(b):
                    sp.dma_start(ct[b.parity][:, :, :], g.ct_dram[b.at()].rearrange("o p k n -> p (o k) n")).then_inc(s_ct[b.parity], 16)

                ring_loads = dict(zip((1, 2, 3, 4, 5, B - 2, B - 1, B), ((e, which) for e in range(4) for which in (1, 2))))
                load_made(Item(0, 0, B))

                def step(b):
                    if (b + 1).real():
                        load_made(b + 1)
                    if b.real():
                        if (b - 2).real():
                            sp.wait_ge(s["scored"], (b - 2).count(1, 1))
                            sp.sem_inc(s["sp_turns"], 1)
                        load_ct(b)
                    if (b - 1).real():
                        n = b - 1
                        if (n - 2).real():
                            sp.wait_ge(s["mix_mm"], (n - 2).count(1, 1))
                            sp.sem_inc(s["sp_turns"], 1)
                        load_cin(n)
                    if not b.looped() and b.c in ring_loads:
                        e, which = ring_loads[b.c]
                        load_w(nc, sp, a, g, Item(0, e, E1, 4), which)
                    if (b - 3).real():
                        sp.wait_ge(s["x3"], (b - 3).count(1, 1))
                        sp.sem_inc(s["sp_turns"], 1)
                        sp.dma_start(out[(b - 3).at()].rearrange("o t d -> t (o d)"), xs[:, (b - 3).at(), :].rearrange("t o d -> t (o d)")).then_inc(s["x3_stored"], 16)

                steps(sp, step, B, FIRST, B - 2, B + 3)
                sp.wait_ge(s["x3_stored"], 16 * B)

            def rstd_of(pool, b, k, mv, rstd):
                pool.wait_ge(s[f"mv{k}"], b.count(1, 1))
                nc.gpsimd.tensor_tensor(rstd[:, 0:1], mv[:, 1:2], g.eps[0:T, :], ALU.add).then_inc(s[f"eps{k}"], 1)
                pool.wait_ge(s[f"eps{k}"], b.count(1, 1))
                nc.gpsimd.tensor_tensor(rstd[:, 1:2], rstd[:, 0:1], g.neg_half[0:T, :], ALU.pow).then_inc(s[f"rstd{k}"], 1)

            @block.gpsimd
            def _(pool):
                def ahead(b):
                    rstd_of(pool, b, 2, mv2, rstd2)
                    pool.wait_ge(s["xn2"], b.count(1, 1))
                    stream = xs[:, b.at(), :].rearrange("t o d -> t (o d)")
                    nc.gpsimd.tensor_tensor(stream, stream, row[:, :], ALU.add).then_inc(s["xc"], 1)

                r.constants(pool)
                ahead(Item(0, 0, B))

                def step(b):
                    if (b + 1).real():
                        ahead(b + 1)
                    if (b - 2).real():
                        rstd_of(pool, b - 2, 3, mv3, rstd3)
                    if (b - 4).real():
                        r.scatter(pool, b - 4, rows, g.sorted1, E1 * C1)

                attention_steps(pool, step)
                r.scattered_all(pool)

            @block.scalar
            def _(act):
                def step(b):
                    if b.real():
                        act.wait_ge(s["t2"], b.count(1, 1))
                        if (b - 2).real():
                            act.wait_ge(s["q_mm"], (b - 2).count(1, 1))
                        nc.scalar.copy(xt2[b.parity][:, :, :], bank[2][:, 0:2 * T].rearrange("p (k t) -> p k t", k=2)).then_inc(s["xt2"], 1)
                    if (b - 1).real():
                        n = b - 1
                        act.wait_ge(s["maxed"], n.count(1, 1))
                        if (n - 2).real():
                            act.wait_ge(s["tp"], (n - 2).count(1, 1))
                            act.wait_ge(s["inverse"], (n - 2).count(1, 1))
                        nc.scalar.activation(prob[n.parity][:, :], bank[0][0:T, 0:S], ACT.Exp, bias=neg_max[n.parity][:, :],
                                             accum_out=total[n.parity][:, :]).then_inc(s["prob"], 1)
                    if (b - 2).real():
                        n = b - 2
                        act.wait_ge(s["mix_mm"], n.count(1, 1))
                        if (n - 2).real():
                            act.wait_ge(s["out_mm"], (n - 2).count(1, 1))
                        nc.scalar.copy(mix[n.parity][:, :, :], bank[1][:, 0:2 * T].rearrange("p (k t) -> p k t", k=2)).then_inc(s["mix"], 1)
                    if b.real():
                        act.wait_ge(s["q_mm"], b.count(1, 1))
                        if (b - 2).real():
                            act.wait_ge(s["scored"], (b - 2).count(1, 1))
                        for h in range(2):
                            nc.scalar.activation(q[b.parity][:, h, :], bank[6][:, h * T:(h + 1) * T], ACT.Identity,
                                                 bias=u[:, h:h + 1], scale=D ** -0.5).then_inc(s["q"], 1)
                    if (b - 3).real():
                        n = b - 3
                        act.wait_ge(s["t3"], n.count(1, 1))
                        if (n - 2).real():
                            act.wait_ge(s["logits_mm"], (n - 2).count(1, 1))
                        nc.scalar.copy(xt3[n.parity][:, :, :], bank[3][:, 0:2 * T].rearrange("p (k t) -> p k t", k=2)).then_inc(s["xt3"], 1)
                    if (b - 1).real():
                        n = b - 1
                        act.wait_ge(s["tp"], n.count(1, 1))
                        if (n - 2).real():
                            act.wait_ge(s["mix_mm"], (n - 2).count(1, 1))
                        nc.scalar.copy(prob_t[n.parity][:, :, :], bank[4][0:KC, 0:NC * T].rearrange("p (c t) -> p c t", c=NC)).then_inc(s["prob_t"], 1)
                    if (b - 4).real():
                        act.wait_ge(s["shifted"], (b - 4).count(1, 1))
                        nc.scalar.activation(expd[:, :], shifted[:, :], ACT.Exp, accum_out=sums[:, :]).then_inc(s["expd"], 1)
                    if (b - 3).real():
                        n = b - 3
                        act.wait_ge(s["xn3"], n.count(1, 1))
                        if (n - 2).real():
                            act.wait_ge(r.scattered[n.parity], (n - 2).turn(16, 16))
                        nc.scalar.copy(rows[n.parity][:, 0:D], xn3[n.parity][:, :])
                        nc.scalar.copy(rows[n.parity][:, D:2 * D], xs[:, n.at(), :].rearrange("t o d -> t (o d)")).then_inc(s["rows"], 1)

                attention_steps(act, step)

            @block.vector
            def _(dve):
                def mean(b, k, stats, mv):
                    stream = xs[:, b.at(), :].rearrange("t o d -> t (o d)")
                    nc.vector.bn_stats(stats[:, :], stream).then_inc(s[f"stats{k}"], 1)
                    dve.wait_ge(s[f"stats{k}"], b.count(1, 1))
                    dve.sem_inc(s["dve_turns"], 1)
                    nc.vector.bn_aggr(mv[:, :], stats[:, :]).then_inc(s[f"mv{k}"], 1)

                def norm(b, k, mv, rstd, xn, t_done, row_done=None):
                    stream = xs[:, b.at(), :].rearrange("t o d -> t (o d)")
                    dve.wait_ge(s[f"rstd{k}"], b.count(1, 1))
                    if (b - 2).real():
                        dve.wait_ge(t_done, (b - 2).count(1, 1))
                        if row_done is not None:
                            dve.wait_ge(row_done, (b - 2).count(1, 1))
                    nc.vector.tensor_scalar(xn[b.parity][:, :], stream, mv[:, 0:1], rstd[:, 1:2], ALU.subtract, ALU.mult).then_inc(s[f"xn{k}"], 1)

                def add_made(b):
                    stream = xs[:, b.at(), :].rearrange("t o d -> t (o d)")
                    dve.wait_ge(s_made[b.parity], b.turn(16, 16))
                    nc.vector.tensor_tensor(stream, stream, made[b.parity][:, :], ALU.add).then_inc(s["x2"], 1)
                    dve.wait_ge(s["x2"], b.count(1, 1))
                    dve.sem_inc(s["dve_turns"], 1)
                    mean(b, 2, stats2, mv2)

                add_made(Item(0, 0, B))
                norm(Item(0, 0, B), 2, mv2, rstd2, xn2, s["t2"])

                def step(b):
                    if (b - 1).real():
                        n = b - 1
                        dve.wait_ge(s["scored"], n.count(1, 1))
                        if (n - 2).real():
                            dve.wait_ge(s["prob"], (n - 2).count(1, 1))
                        nc.vector.tensor_reduce(neg_max[n.parity][:, :], bank[0][0:T, 0:S], AX, ALU.max, negate=True).then_inc(s["maxed"], 1)
                    if (b + 1).real():
                        add_made(b + 1)
                    if (b - 4).real():
                        n = b - 4
                        r.choose(dve, n)
                        if (n - 1).real():
                            dve.wait_ge(s["expd"], (n - 1).count(1, 1))
                        nc.vector.tensor_scalar(shifted[:, :], r.logits[:, :], r.best[:, :], None, ALU.subtract).then_inc(s["shifted"], 1)
                    if (b + 1).real():
                        norm(b + 1, 2, mv2, rstd2, xn2, s["t2"])
                    if (b - 2).real():
                        n = b - 2
                        dve.wait_ge(s["out_mm"], n.count(1, 1))
                        dve.wait_ge(s["inverse"], n.count(1, 1))
                        dve.wait_ge(s["xc"], n.count(1, 1))
                        stream = xs[:, n.at(), :].rearrange("t o d -> t (o d)")
                        nc.vector.scalar_tensor_tensor(out=stream, in0=bank[5][0:T, 0:D], scalar=inverse[n.parity][:, :], in1=stream,
                                                       op0=ALU.mult, op1=ALU.add).then_inc(s["x3"], 1)
                        dve.wait_ge(s["x3"], n.count(1, 1))
                        dve.sem_inc(s["dve_turns"], 1)
                        mean(n, 3, stats3, mv3)
                    if (b - 1).real():
                        n = b - 1
                        dve.wait_ge(s["prob"], n.count(1, 1))
                        nc.vector.reciprocal(inverse[n.parity][:, :], total[n.parity][:, :]).then_inc(s["inverse"], 1)
                    if (b - 4).real():
                        n = b - 4
                        r.place_rows(dve, n, C1)
                        dve.wait_ge(s["expd"], n.count(1, 1))
                        dve.wait_ge(s["rows"], n.count(1, 1))
                        nc.vector.reciprocal(rows[n.parity][:, 2 * D:2 * D + 1], sums[:, :])
                        nc.vector.tensor_copy(rows[n.parity][:, 2 * D + 1:ROW1], r.number[:, n.at()])
                        r.place_done(n)
                    if (b - 2).real():
                        norm(b - 2, 3, mv3, rstd3, xn3, s["t3"], s["rows"])

                attention_steps(dve, step)

            @block.tensor
            def _(pe):
                def step(b):
                    if b.real():
                        pe.wait_ge(s["xn2"], b.count(1, 1))
                        if (b - 1).real():
                            pe.wait_ge(s["xt2"], (b - 1).count(1, 1))
                        for h in range(2):
                            last = nc.tensor.transpose(bank[2][:, h * T:(h + 1) * T], xn2[b.parity][:, h * P:(h + 1) * P], ident[0:T, 0:T])
                        last.then_inc(s["t2"], 1)
                    if (b - 1).real():
                        n = b - 1
                        pe.wait_ge(s_ct[n.parity], n.turn(16, 16))
                        pe.wait_ge(s["q"], n.count(2, 2))
                        if (n - 1).real():
                            pe.wait_ge(s["prob"], (n - 1).count(1, 1))
                        for h in range(2):
                            last = nc.tensor.matmul(bank[0][0:T, 0:S], q[n.parity][:, h, :], ct[n.parity][:, h, :], start=(h == 0), stop=(h == 1))
                        last.then_inc(s["scored"], 1)
                    if (b - 2).real():
                        n = b - 2
                        pe.wait_ge(s_cin[n.parity], n.turn(16, 16))
                        pe.wait_ge(s["prob_t"], n.count(1, 1))
                        if (n - 1).real():
                            pe.wait_ge(s["mix"], (n - 1).count(1, 1))
                        for h in range(2):
                            for c in range(NC):
                                last = nc.tensor.matmul(bank[1][:, h * T:(h + 1) * T], cin[n.parity][:, c, h * P:(h + 1) * P], prob_t[n.parity][:, c, :],
                                                        start=(c == 0), stop=(c == NC - 1))
                        last.then_inc(s["mix_mm"], 1)
                    if b.real():
                        pe.wait_ge(s["xt2"], b.count(1, 1))
                        if (b - 1).real():
                            pe.wait_ge(s["q"], (b - 1).count(2, 2))
                        if (b - 5).real():
                            pe.wait_ge(*r.counts_read(b - 5))
                        for h in range(2):
                            for k in range(2):
                                last = nc.tensor.matmul(bank[6][:, h * T:(h + 1) * T], w_qk[:, k, h * P:(h + 1) * P], xt2[b.parity][:, k, :],
                                                        start=(k == 0), stop=(k == 1))
                        last.then_inc(s["q_mm"], 1)
                    if (b - 3).real():
                        n = b - 3
                        pe.wait_ge(s["xn3"], n.count(1, 1))
                        if (n - 1).real():
                            pe.wait_ge(s["xt3"], (n - 1).count(1, 1))
                        for h in range(2):
                            last = nc.tensor.transpose(bank[3][:, h * T:(h + 1) * T], xn3[n.parity][:, h * P:(h + 1) * P], ident[0:T, 0:T])
                        last.then_inc(s["t3"], 1)
                    if (b - 1).real():
                        n = b - 1
                        pe.wait_ge(s["prob"], n.count(1, 1))
                        if (n - 1).real():
                            pe.wait_ge(s["prob_t"], (n - 1).count(1, 1))
                        for c in range(NC):
                            last = nc.tensor.transpose(bank[4][0:KC, c * T:(c + 1) * T], prob[n.parity][:, c * KC:(c + 1) * KC], ident[0:T, 0:T])
                        last.then_inc(s["tp"], 1)
                    if (b - 2).real():
                        n = b - 2
                        pe.wait_ge(s["mix"], n.count(1, 1))
                        if (n - 1).real():
                            pe.wait_ge(s["x3"], (n - 1).count(1, 1))
                        for h in range(2):
                            last = nc.tensor.matmul(bank[5][0:T, 0:D], mix[n.parity][:, h, :], w_vo[:, h, :], start=(h == 0), stop=(h == 1))
                        last.then_inc(s["out_mm"], 1)
                    if (b - 4).real():
                        if b.real():
                            pe.wait_ge(s["q"], b.count(2, 2))
                        r.count(pe, b - 4)
                    if (b - 3).real():
                        n = b - 3
                        if (n - 1).real():
                            pe.wait_ge(*r.logits_read(n - 1))
                        pe.wait_ge(s["xt3"], n.count(1, 1))
                        for h in range(2):
                            last = nc.tensor.matmul(bank[7][0:T, n.rows(E1)], xt3[n.parity][:, h, :], wg[:, h, :], start=(h == 0), stop=(h == 1))
                        last.then_inc(s["logits_mm"], 1)

                attention_steps(pe, step)


def load_w(nc, sp, a, g, e, which):
    k = e.quarter
    if which == 1:
        src = a["L1_ffn_w1"][e.at()].rearrange("o (k p) f -> p (o k) f", p=P)
        sp.dma_start(g.ring1[k][:, :, :], src).then_inc(g.s_ring1[k], 16)
    else:
        src = a["L1_ffn_w2"][e.at()].rearrange("o (k p) d -> p (o k) d", p=P)
        sp.dma_start(g.ring2[k][:, :, :], src).then_inc(g.s_ring2[k], 16)


def ffn1(nc, a, out, g):
    bank = g.bank
    KF = F1 // P
    out_rows = out.rearrange("b t d -> (b t) d")
    s = {n: g.sem("f1_" + n) for n in "x_mm x_copy up hid_a hid_v down down_copy index_ready sp_turns pool_turns".split()}
    s_in = [g.sem(f"f1_rows_loaded{p}") for p in range(2)]
    s_out = [g.sem(f"f1_rows_stored{p}") for p in range(2)]
    with ExitStack() as experts:
        def tb(name, shape, dt=F32):
            return [g.sb(f"e1_{name}{p}", shape, dt, experts) for p in range(2)]

        x_in = [g.sb(f"e1_x_in{k}", [C1, ROW1], F32, experts) for k in range(4)]
        index = [g.sb(f"e1_index{k}", [C1, 1], I32, experts) for k in range(4)]
        xt, hid, y = tb("xt", [P, 2, C1]), tb("hid", [P, KF, C1]), tb("y", [C1, D])
        block = nc.Block()
        with block:
            @block.sync
            def _(sp):
                def load(e):
                    if (e - 4).real():
                        sp.wait_ge(s["index_ready"], (e - 4).count(1, 1))
                        sp.sem_inc(s["sp_turns"], 1)
                        sp.wait_ge(s["down_copy"], (e - 4).count(1, 1))
                        sp.sem_inc(s["sp_turns"], 1)
                    sp.dma_start(x_in[e.quarter][:, :], g.sorted1[e.rows(C1), :]).then_inc(s_in[e.parity], 16)

                load(Item(0, 0, E1, 4))
                load(Item(0, 1, E1, 4))

                def step(e):
                    if (e + 2).real():
                        sp.wait_ge(s["x_mm"], e.count(1, 1))
                        sp.sem_inc(s["sp_turns"], 1)
                        load(e + 2)
                    if (e + 4).real():
                        sp.wait_ge(s["up"], e.count(2, 2))
                        sp.sem_inc(s["sp_turns"], 1)
                        load_w(nc, sp, a, g, e + 4, 1)
                    if (e - 1).real() and (e + 3).real():
                        sp.wait_ge(s["down"], (e - 1).count(1, 1))
                        sp.sem_inc(s["sp_turns"], 1)
                        load_w(nc, sp, a, g, e + 3, 2)

                steps(sp, step, E1, 2, E1 - 5, E1 + 1, 4)

            @block.gpsimd
            def _(pool):
                def step(e):
                    if e.real():
                        pool.wait_ge(s_in[e.parity], e.turn(16, 16))
                        pool.sem_inc(s["pool_turns"], 1)
                        if (e - 4).real():
                            pool.wait_ge(s_out[e.parity], (e - 4).turn(16, 16))
                            pool.sem_inc(s["pool_turns"], 1)
                        nc.gpsimd.tensor_copy(index[e.quarter][:, :], x_in[e.quarter][:, ROW1 - 1:ROW1]).then_inc(s["index_ready"], 1)
                    if (e - 2).real():
                        n = e - 2
                        pool.wait_ge(s["index_ready"], n.count(1, 1))
                        pool.wait_ge(s["down_copy"], n.count(1, 1))
                        pool.sem_inc(s["pool_turns"], 1)
                        pool.indirect_dma_start(out=out_rows, out_offset=bass.IndirectOffsetOnAxis(index[n.quarter][:, 0:1], 0),
                                                in_=y[n.parity][:, :], in_offset=None, bounds_check=N - 1,
                                                oob_is_err=False).then_inc(s_out[n.parity], 16)

                steps(pool, step, E1, 6, E1 - 1, E1 + 2, 4)
                for p in range(2):
                    pool.wait_ge(s_out[p], 16 * E1 // 2)

            @block.scalar
            def _(act):
                def step(e):
                    if e.real():
                        act.wait_ge(s["x_mm"], e.count(1, 1))
                        if (e - 2).real():
                            act.wait_ge(s["up"], (e - 2).count(2, 2))
                        nc.scalar.copy(xt[e.parity][:, :, :], bank[4 + e.parity][:, 0:2 * C1].rearrange("p (k t) -> p k t", k=2)).then_inc(s["x_copy"], 1)
                    if (e - 1).real():
                        n = e - 1
                        act.wait_ge(s["up"], n.count(2, 1))
                        if (n - 2).real():
                            act.wait_ge(s["down"], (n - 2).count(1, 1))
                        nc.scalar.activation(hid[n.parity][:, 0:KF // 2, :], bank[2 * n.parity][:, 0:4 * C1].rearrange("p (f t) -> p f t", f=KF // 2),
                                             ACT.Relu).then_inc(s["hid_a"], 1)

                steps(act, step, E1, 3, E1 - 2, E1 + 1, 4)

            @block.vector
            def _(dve):
                def step(e):
                    if (e - 2).real():
                        n = e - 2
                        dve.wait_ge(s["down"], n.count(1, 1))
                        if (n - 2).real():
                            dve.wait_ge(s_out[n.parity], (n - 2).turn(16, 16))
                        rows = x_in[n.quarter]
                        nc.vector.scalar_tensor_tensor(out=y[n.parity][:, :], in0=bank[6 + n.parity][0:C1, 0:D], scalar=rows[:, 2 * D:2 * D + 1],
                                                       in1=rows[:, D:2 * D], op0=ALU.mult, op1=ALU.add).then_inc(s["down_copy"], 1)
                    if (e - 1).real():
                        n = e - 1
                        dve.wait_ge(s["up"], n.count(2, 2))
                        if (n - 2).real():
                            dve.wait_ge(s["down"], (n - 2).count(1, 1))
                        nc.vector.tensor_scalar(hid[n.parity][:, KF // 2:KF, :], bank[2 * n.parity + 1][:, 0:4 * C1].rearrange("p (f t) -> p f t", f=KF // 2),
                                                0.0, None, ALU.max).then_inc(s["hid_v"], 1)

                steps(dve, step, E1, 4, E1 - 1, E1 + 2, 4)

            @block.tensor
            def _(pe):
                def transpose_in(e):
                    pe.wait_ge(s_in[e.parity], e.turn(16, 16))
                    if (e - 2).real():
                        pe.wait_ge(s["x_copy"], (e - 2).count(1, 1))
                    for h in range(2):
                        last = nc.tensor.transpose(bank[4 + e.parity][:, h * C1:(h + 1) * C1], x_in[e.quarter][:, h * P:(h + 1) * P], g.ident[0:C1, 0:C1])
                    last.then_inc(s["x_mm"], 1)

                transpose_in(Item(0, 0, E1, 4))

                def step(e):
                    if e.real():
                        pe.wait_ge(s["x_copy"], e.count(1, 1))
                        pe.wait_ge(g.s_ring1[e.quarter], e.turn(16, 16, 4))
                        if (e - 2).real():
                            pe.wait_ge(s["hid_a"], (e - 2).count(1, 1))
                            pe.wait_ge(s["hid_v"], (e - 2).count(1, 1))
                        for f in range(KF):
                            for k in range(2):
                                last = nc.tensor.matmul(bank[2 * e.parity + f // 4][:, f % 4 * C1:(f % 4 + 1) * C1],
                                                        g.ring1[e.quarter][:, k, f * P:(f + 1) * P], xt[e.parity][:, k, :], start=(k == 0), stop=(k == 1))
                            if f % 4 == 3:
                                last.then_inc(s["up"], 1)
                    if (e + 1).real():
                        transpose_in(e + 1)
                    if (e - 1).real():
                        n = e - 1
                        pe.wait_ge(g.s_ring2[n.quarter], n.turn(16, 16, 4))
                        pe.wait_ge(s["hid_a"], n.count(1, 1))
                        pe.wait_ge(s["hid_v"], n.count(1, 1))
                        if (n - 2).real():
                            pe.wait_ge(s["down_copy"], (n - 2).count(1, 1))
                        for f in range(KF):
                            last = nc.tensor.matmul(bank[6 + n.parity][0:C1, 0:D], hid[n.parity][:, f, :], g.ring2[n.quarter][:, f, :],
                                                    start=(f == 0), stop=(f == KF - 1))
                        last.then_inc(s["down"], 1)

                steps(pe, step, E1, 3, E1 - 2, E1 + 1, 4)


def kernel(**inputs):
    import numpy as np
    from concourse import bacc
    from concourse.bass_utils import run_bass_kernel_spmd

    nc = bacc.Bacc("TRN2", target_bir_lowering=False, num_devices=1)
    arrays, args = {}, {}
    for name, value in inputs.items():
        array = np.ascontiguousarray(value)
        arrays[f"in_{name}"] = array
        args[name] = nc.dram_tensor(f"in_{name}", array.shape, mybir.dt.from_np(array.dtype), kind="ExternalInput").ap()
    out = nc.dram_tensor("out", (B, T, D), F32, kind="ExternalOutput").ap()
    program(nc, args, out)
    return run_bass_kernel_spmd(nc, [arrays], core_ids=[0]).results[0]["out"]
```
